# Optimizing a Trainium2 kernel written in Bass

```python
import numpy as np
import jax
import jax.numpy as jnp

def _softmax(x, axis=-1):
    return jax.nn.softmax(x, axis=axis)
def _gelu(x):
    return jax.nn.gelu(x, approximate=True)
def _silu(x):
    return jax.nn.silu(x)
def _sigmoid(x):
    return jax.nn.sigmoid(x)
def _layernorm(x, axis=-1, eps=1e-5):
    m = jnp.mean(x, axis=axis, keepdims=True)
    v = jnp.var(x, axis=axis, keepdims=True)
    return (x - m) / jnp.sqrt(v + eps)
def _scatter_add(tgt, idx, src, axis=0):
    return tgt.at[idx].add(src)
def _segment_sum(src, seg, n):
    return jax.ops.segment_sum(src, seg, n)

kernel_name = 'mk_adj_ffn_d2_adj_256_98c791'

def setup_inputs(seed: int = 0):
    np.random.seed(seed)
    _w = jnp.asarray
    def _rec_inputs():
        import jax
        import jax.numpy as jnp
        _gk = jax.random.key(seed)
        x = -0.0002928 + 1 * jax.random.normal(jax.random.fold_in(_gk, 1), (64, 256, 256), jnp.float32)
        _a = jax.random.bernoulli(jax.random.fold_in(_gk, 2), 0.125, (64, 256, 256))
        _a = jnp.logical_or(_a, jnp.swapaxes(_a, -1, -2))
        _a = jnp.logical_or(_a, jnp.eye(256, dtype=bool))
        _af = _a.astype(jnp.float32)
        _af = _af * jax.random.uniform(jax.random.fold_in(_gk, 3), (64, 256, 256), jnp.float32, 0.05, 1)
        adj = _af
        _nm = jnp.ones((64, 256), dtype=bool)
        nodemask = jnp.where(_nm, 1.0, 0.0).astype(jnp.float32)
        return x, adj, nodemask
    x, adj, nodemask = _rec_inputs()
    def _L0_gnn_setup():
        import jax, jax.numpy as jnp
        import numpy as np
        B, N, F_IN, F_OUT = (8, 2048, 256, 256)
        key = jax.random.key(seed)
        k1, k2, k3, k4 = jax.random.split(key, 4)
        node_features = jax.random.normal(k1, (B, N, F_IN), dtype=jnp.float32)
        adj_matrix = jax.random.uniform(k2, (B, N, N), dtype=jnp.float32)
        lim = 1.0 / np.sqrt(F_IN)
        W = jax.random.uniform(k3, (F_OUT, F_IN), minval=-lim, maxval=lim, dtype=jnp.float32)
        b = jax.random.uniform(k4, (F_OUT,), minval=-lim, maxval=lim, dtype=jnp.float32)
        return {'node_features': node_features, 'adj_matrix': adj_matrix, 'W': W, 'b': b}
    _L0_gnn_all = _L0_gnn_setup()
    _L0_gnn_in = {k: v for k, v in _L0_gnn_all.items() if k in ('W', 'b', )}
    del _L0_gnn_all

    def _L0_ffn_setup():
        import jax, jax.numpy as jnp
        import numpy as np
        B, A = (4096, 8)
        IN, OUT = (256, 256)
        SH1, SH2 = (256, 128)
        EH1, EH2 = (128, 64)
        E, TOPK = (4, 2)

        def _shared_mlp(x, W1, b1, W2, b2, W3, b3):
            h = jax.nn.relu(x @ W1 + b1)
            h = jax.nn.relu(h @ W2 + b2)
            return h @ W3 + b3

        def _experts_mlp(x, eW1, eb1, eW2, eb2, eW3, eb3):
            h = jax.nn.relu(jnp.einsum('baf,efh->ebah', x, eW1) + eb1[:, None, None, :])
            h = jax.nn.relu(jnp.einsum('ebah,ehg->ebag', h, eW2) + eb2[:, None, None, :])
            o = jnp.einsum('ebag,ego->ebao', h, eW3) + eb3[:, None, None, :]
            return jnp.moveaxis(o, 0, -1)
        key = jax.random.key(seed)
        ks = jax.random.split(key, 16)
        s = 0.05
        return {'x': jax.random.normal(ks[0], (B, A, IN), jnp.float32), 'sW1': jax.random.normal(ks[1], (IN, SH1), jnp.float32) * s, 'sb1': jnp.zeros((SH1,), jnp.float32), 'sW2': jax.random.normal(ks[2], (SH1, SH2), jnp.float32) * s, 'sb2': jnp.zeros((SH2,), jnp.float32), 'sW3': jax.random.normal(ks[3], (SH2, OUT), jnp.float32) * s, 'sb3': jnp.zeros((OUT,), jnp.float32), 'eW1': jax.random.normal(ks[4], (E, IN, EH1), jnp.float32) * s, 'eb1': jnp.zeros((E, EH1), jnp.float32), 'eW2': jax.random.normal(ks[5], (E, EH1, EH2), jnp.float32) * s, 'eb2': jnp.zeros((E, EH2), jnp.float32), 'eW3': jax.random.normal(ks[6], (E, EH2, OUT), jnp.float32) * s, 'eb3': jnp.zeros((E, OUT), jnp.float32), 'gW': jax.random.normal(ks[7], (IN, E), jnp.float32) * s, 'gb': jnp.zeros((E,), jnp.float32)}
    _L0_ffn_all = _L0_ffn_setup()
    _L0_ffn_in = {k: v for k, v in _L0_ffn_all.items() if k in ('sW1', 'sb1', 'sW2', 'sb2', 'sW3', 'sb3', 'eW1', 'eb1', 'eW2', 'eb2', 'eW3', 'eb3', 'gW', 'gb', )}
    del _L0_ffn_all

    def _L1_gnn_setup():
        import jax, jax.numpy as jnp
        import numpy as np
        EPS = 1e-08
        key = jax.random.key(seed)
        kH, kA, kW = jax.random.split(key, 3)
        B, N, IN, OUT = (32, 512, 256, 256)
        H = jax.random.normal(kH, (B, N, IN), dtype=jnp.float32)
        A = jax.random.uniform(kA, (B, N, N), dtype=jnp.float32)
        mask = jnp.ones((B, N), dtype=jnp.float32)
        W = jax.random.normal(kW, (OUT, IN), dtype=jnp.float32) * (1.0 / np.sqrt(IN))
        b = jnp.zeros((OUT,), dtype=jnp.float32)
        return {'H': H, 'A': A, 'mask': mask, 'W': W, 'b': b}
    _L1_gnn_all = _L1_gnn_setup()
    _L1_gnn_in = {k: v for k, v in _L1_gnn_all.items() if k in ('W', 'b', )}
    del _L1_gnn_all

    def _L1_ffn_setup():
        import jax, jax.numpy as jnp
        import numpy as np
        NUM_EXPERTS = 8
        TOP_K = 2
        B, S, D = (8, 8192, 256)

        def _moe(tokens, router_w, w1, b1, w2, b2):
            N = tokens.shape[0]
            E = router_w.shape[0]
            logits = tokens.astype(jnp.float32) @ router_w.astype(jnp.float32).T
            probs = jax.nn.softmax(logits, axis=-1)
            rw, re = jax.lax.top_k(probs, TOP_K)
            if TOP_K > 1:
                rw = rw / jnp.maximum(rw.sum(-1, keepdims=True), 1e-12)
            rw = rw.astype(tokens.dtype)
            combine = jnp.zeros((N, E), tokens.dtype).at[jnp.arange(N)[:, None], re].set(rw)
            out = tokens
            for e in range(E):
                h = jax.nn.gelu(tokens @ w1[e] + b1[e], approximate=False)
                y = h @ w2[e] + b2[e]
                out = out + combine[:, e:e + 1] * y
            return out
        key = jax.random.key(seed)
        ks = jax.random.split(key, 4)
        scale = 1.0 / np.sqrt(D).astype(np.float32)
        return {'input_embeddings': jax.random.normal(ks[0], (B, S, D), jnp.float32), 'router_w': jax.random.normal(ks[1], (NUM_EXPERTS, D), jnp.float32) * scale, 'w1': jax.random.normal(ks[2], (NUM_EXPERTS, D, D), jnp.float32) * scale, 'b1': jnp.zeros((NUM_EXPERTS, D), jnp.float32), 'w2': jax.random.normal(ks[3], (NUM_EXPERTS, D, D), jnp.float32) * scale, 'b2': jnp.zeros((NUM_EXPERTS, D), jnp.float32)}
    _L1_ffn_all = _L1_ffn_setup()
    _L1_ffn_in = {k: v for k, v in _L1_ffn_all.items() if k in ('router_w', 'w1', 'b1', 'w2', 'b2', )}
    del _L1_ffn_all

    return {
        "x": x,
        "adj": adj,
        "nodemask": nodemask,
        "L0_gnn_W": _L0_gnn_in["W"],
        "L0_gnn_b": _L0_gnn_in["b"],
        "L0_ffn_sW1": _L0_ffn_in["sW1"],
        "L0_ffn_sb1": _L0_ffn_in["sb1"],
        "L0_ffn_sW2": _L0_ffn_in["sW2"],
        "L0_ffn_sb2": _L0_ffn_in["sb2"],
        "L0_ffn_sW3": _L0_ffn_in["sW3"],
        "L0_ffn_sb3": _L0_ffn_in["sb3"],
        "L0_ffn_eW1": _L0_ffn_in["eW1"],
        "L0_ffn_eb1": _L0_ffn_in["eb1"],
        "L0_ffn_eW2": _L0_ffn_in["eW2"],
        "L0_ffn_eb2": _L0_ffn_in["eb2"],
        "L0_ffn_eW3": _L0_ffn_in["eW3"],
        "L0_ffn_eb3": _L0_ffn_in["eb3"],
        "L0_ffn_gW": _L0_ffn_in["gW"],
        "L0_ffn_gb": _L0_ffn_in["gb"],
        "L1_gnn_W": _L1_gnn_in["W"],
        "L1_gnn_b": _L1_gnn_in["b"],
        "L1_ffn_router_w": _L1_ffn_in["router_w"],
        "L1_ffn_w1": _L1_ffn_in["w1"],
        "L1_ffn_b1": _L1_ffn_in["b1"],
        "L1_ffn_w2": _L1_ffn_in["w2"],
        "L1_ffn_b2": _L1_ffn_in["b2"],
    }

def reference(x, adj, nodemask, L0_gnn_W, L0_gnn_b, L0_ffn_sW1, L0_ffn_sb1, L0_ffn_sW2, L0_ffn_sb2, L0_ffn_sW3, L0_ffn_sb3, L0_ffn_eW1, L0_ffn_eb1, L0_ffn_eW2, L0_ffn_eb2, L0_ffn_eW3, L0_ffn_eb3, L0_ffn_gW, L0_ffn_gb, L1_gnn_W, L1_gnn_b, L1_ffn_router_w, L1_ffn_w1, L1_ffn_b1, L1_ffn_w2, L1_ffn_b2):
    import jax
    import jax.numpy as jnp
    def _L0_gnn_ref(node_features, adj_matrix, W, b):
        import jax, jax.numpy as jnp
        import numpy as np
        B, N, F_IN, F_OUT = (8, 2048, 256, 256)
        degree = jnp.sum(adj_matrix, axis=-1)
        d_inv_sqrt = jnp.power(degree, -0.5)
        d_inv_sqrt = jnp.where(jnp.isinf(d_inv_sqrt), 0.0, d_inv_sqrt)
        norm_adj = adj_matrix * d_inv_sqrt[:, :, None] * d_inv_sqrt[:, None, :]
        transformed = jnp.einsum('bnf,of->bno', node_features, W) + b
        output = jnp.einsum('bnm,bmo->bno', norm_adj, transformed)
        return jax.nn.relu(output)

    def _L0_ffn_ref(x, sW1, sb1, sW2, sb2, sW3, sb3, eW1, eb1, eW2, eb2, eW3, eb3, gW, gb):
        import jax, jax.numpy as jnp
        import numpy as np
        B, A = (4096, 8)
        IN, OUT = (256, 256)
        SH1, SH2 = (256, 128)
        EH1, EH2 = (128, 64)
        E, TOPK = (4, 2)

        def _shared_mlp(x, W1, b1, W2, b2, W3, b3):
            h = jax.nn.relu(x @ W1 + b1)
            h = jax.nn.relu(h @ W2 + b2)
            return h @ W3 + b3

        def _experts_mlp(x, eW1, eb1, eW2, eb2, eW3, eb3):
            h = jax.nn.relu(jnp.einsum('baf,efh->ebah', x, eW1) + eb1[:, None, None, :])
            h = jax.nn.relu(jnp.einsum('ebah,ehg->ebag', h, eW2) + eb2[:, None, None, :])
            o = jnp.einsum('ebag,ego->ebao', h, eW3) + eb3[:, None, None, :]
            return jnp.moveaxis(o, 0, -1)
        all_out = _experts_mlp(x, eW1, eb1, eW2, eb2, eW3, eb3)
        shared = _shared_mlp(x, sW1, sb1, sW2, sb2, sW3, sb3)
        gates = jax.nn.softmax(x @ gW + gb, axis=-1)
        topv, topi = jax.lax.top_k(gates, TOPK)
        topw = jax.nn.softmax(topv, axis=-1)
        sel = jnp.take_along_axis(all_out, topi[:, :, None, :], axis=-1)
        gated = jnp.sum(sel * topw[:, :, None, :], axis=-1)
        return shared + gated

    def _L1_gnn_ref(H, A, mask, W, b):
        import jax, jax.numpy as jnp
        import numpy as np
        EPS = 1e-08
        N = A.shape[-1]
        A_hat = A + jnp.eye(N, dtype=A.dtype)
        deg = A_hat.sum(axis=-1)
        dis = (deg + EPS) ** (-0.5)
        A_norm = dis[:, :, None] * A_hat * dis[:, None, :]
        H_lin = jnp.einsum('bni,oi->bno', H, W) + b
        out = jnp.einsum('bnm,bmo->bno', A_norm, H_lin)
        out = out * mask[:, :, None]
        return jax.nn.relu(out)

    def _L1_ffn_ref(input_embeddings, router_w, w1, b1, w2, b2):
        import jax, jax.numpy as jnp
        import numpy as np
        NUM_EXPERTS = 8
        TOP_K = 2
        B, S, D = (8, 8192, 256)

        def _moe(tokens, router_w, w1, b1, w2, b2):
            N = tokens.shape[0]
            E = router_w.shape[0]
            logits = tokens.astype(jnp.float32) @ router_w.astype(jnp.float32).T
            probs = jax.nn.softmax(logits, axis=-1)
            rw, re = jax.lax.top_k(probs, TOP_K)
            if TOP_K > 1:
                rw = rw / jnp.maximum(rw.sum(-1, keepdims=True), 1e-12)
            rw = rw.astype(tokens.dtype)
            combine = jnp.zeros((N, E), tokens.dtype).at[jnp.arange(N)[:, None], re].set(rw)
            out = tokens
            for e in range(E):
                h = jax.nn.gelu(tokens @ w1[e] + b1[e], approximate=False)
                y = h @ w2[e] + b2[e]
                out = out + combine[:, e:e + 1] * y
            return out
        b, s, d = input_embeddings.shape
        tokens = input_embeddings.reshape(b * s, d)
        return _moe(tokens, router_w, w1, b1, w2, b2).reshape(b, s, d)

    x = x + _L0_gnn_ref(_layernorm(x, axis=-1), adj, L0_gnn_W, L0_gnn_b)
    x = x + _L0_ffn_ref(_layernorm(x, axis=-1), L0_ffn_sW1, L0_ffn_sb1, L0_ffn_sW2, L0_ffn_sb2, L0_ffn_sW3, L0_ffn_sb3, L0_ffn_eW1, L0_ffn_eb1, L0_ffn_eW2, L0_ffn_eb2, L0_ffn_eW3, L0_ffn_eb3, L0_ffn_gW, L0_ffn_gb)
    x = x + _L1_gnn_ref(_layernorm(x, axis=-1), adj, nodemask, L1_gnn_W, L1_gnn_b)
    x = x + _L1_ffn_ref(_layernorm(x, axis=-1), L1_ffn_router_w, L1_ffn_w1, L1_ffn_b1, L1_ffn_w2, L1_ffn_b2)
    return x


_drawn_inputs = setup_inputs


def setup_inputs(seed=0):
    import zlib

    import numpy as np

    out = dict(_drawn_inputs(seed))
    spreads = {'L0_ffn_sb1': (0.0, 0.1),
     'L0_ffn_sb2': (0.0, 0.1),
     'L0_ffn_sb3': (0.0, 0.1),
     'L0_ffn_eb1': (0.0, 0.451),
     'L0_ffn_eb2': (0.0, 0.1),
     'L0_ffn_eb3': (0.0, 0.1),
     'L0_ffn_gb': (0.0, 0.1),
     'L1_gnn_b': (0.0, 0.1),
     'L1_ffn_b1': (0.0, 0.322),
     'L1_ffn_b2': (0.0, 0.1)}
    factors = {}
    for name, (base, spread) in spreads.items():
        noise = np.random.default_rng([zlib.crc32(name.encode()), seed]).standard_normal(out[name].shape)
        drawn = base * np.exp(spread * noise) if base else spread * noise
        out[name] = jnp.asarray(drawn.astype(out[name].dtype))
    for name, factor in factors.items():
        out[name] = (out[name] * factor).astype(out[name].dtype)
    return out
```

```python
from contextlib import ExitStack

import numpy as np

import concourse.bass as bass
from concourse import mybir

fp32 = mybir.dt.float32
f32r = mybir.dt.float32r
bf16 = mybir.dt.bfloat16
i32 = mybir.dt.int32
ALU = mybir.AluOpType
ACT = mybir.ActivationFunctionType
AX = mybir.AxisListType

P = 128
GRAPHS, N, D = 64, 256, 256
TOK = GRAPHS * N
T = 4
PT = T * P
PAIRS = GRAPHS // 2
KD = D // P
E0, E1 = 4, 8
EH1, EH2 = 128, 64
LN_EPS, DEG_EPS = 1e-5, 1e-8
KEY_FLOOR = -88.0
ROW = D + 2 * E1
CAP = TOK + P
TILES = 2 * TOK // P + E1
SKIP = 1 << 16
NJ = TILES

C_ID, C_TRI, C_SEL, C_MH, C_ML = 0, 128, 256, 512, 513
C_REV8, C_REV4, C_ECAP, C_TOK2, C_J, C_PAD = 514, 522, 526, 534, 538, 538 + NJ
C_ALL = C_PAD + ROW


def constants():
    c = np.zeros((P, C_ALL), np.float32)
    p = np.arange(P)
    c[:, C_ID:C_ID + P] = np.eye(P)
    c[:, C_TRI:C_TRI + P] = p[:, None] < p[None, :]
    for b in range(2):
        for m in range(P):
            e = 2 * b + m // EH2
            c[e, C_SEL + b * P + m] = 1.0
            c[8 + e, C_SEL + b * P + m] = 1.0
    c[[0, 1, 2, 3, 8, 9, 10, 11, 12], C_MH] = 1.0
    c[[4, 5, 6, 7, 13], C_ML] = 1.0
    c[:, C_REV8:C_REV8 + E1] = E1 - np.arange(E1)
    c[:, C_REV4:C_REV4 + E0] = E0 - np.arange(E0)
    c[:, C_ECAP:C_ECAP + E1] = CAP * np.arange(E1)
    c[:, C_TOK2:C_TOK2 + T] = 2 * (P * np.arange(T)[None, :] + p[:, None])
    c[:, C_J:C_J + NJ] = P * np.arange(NJ)
    c[:, C_PAD + D + E1:C_PAD + ROW] = SKIP
    return c


JOBS = [
    ("xT0k0", 0), ("xT0k1", 1), ("ATg0", 2), ("ATg1", 3), ("T0g0", 0), ("T0g1", 1), ("M0g0", 2), ("M0g1", 3),
    ("xT1k0", 0), ("xT1k1", 1), ("GL", 2), ("S1m0", 3), ("S1m1", 0), ("S2", 1), ("E1e0", 3), ("E1e1", 0),
    ("EP0", 1), ("E1e2", 3), ("E1e3", 0), ("EP1", 1), ("CBT", 2), ("G0", 2), ("G1", 2), ("O1g0", 3), ("O1g1", 0),
    ("xT2k0", 4), ("xT2k1", 5), ("T1g0", 6), ("T1g1", 7), ("M1g0", 4), ("M1g1", 5), ("xT3k0", 6), ("xT3k1", 7),
    ("RL", 4), ("POS", 5),
]
SPLIT = {j for j, _ in JOBS if j[:2] in ("xT", "AT", "T0", "T1", "S1", "S2", "E1") and not j.startswith("xT3")}
BANK, USE, HI_USE, USES, HI_USES = {}, {}, {}, [0] * 8, [0] * 8
for _j, _b in JOBS:
    USES[_b] += 1
    BANK[_j], USE[_j] = _b, USES[_b]
    if _j in SPLIT:
        HI_USES[_b] += 1
        HI_USE[_j] = HI_USES[_b]

W0 = {}
_at = 0
for _n, _c in [("g0", KD * D), ("g1", KD * D), ("sW1", KD * D), ("eW1", E0 * KD * EH1), ("sW2", KD * P), ("eW2", E0 * P),
               ("sW3", D), ("eW3", 2 * D), ("gW", KD * E0)]:
    W0[_n] = (_at, _c)
    _at += _c
W0_COLS = _at
B0 = {"g0": 0, "g1": D, "sb1": 2 * D, "eb1": 3 * D, "sb2": 3 * D + E0 * EH1}
B0_COLS = 3 * D + E0 * EH1 + P
LOW_ROW = 32


def build(nc, a, out):
    xres = nc.dram_tensor("xres", (TOK, D), fp32, kind="Internal").ap()
    routed = nc.dram_tensor("routed", (E1 * CAP + E1 * P, ROW), fp32, kind="Internal").ap()
    back = nc.dram_tensor("back", (2 * TOK, D), fp32, kind="Internal").ap()

    ctx = ExitStack()
    with ctx:
        def sem(name):
            return ctx.enter_context(nc.semaphore(name))

        def keep(name, shape, dt=fp32, stack=ctx):
            return stack.enter_context(nc.sbuf_tensor(name, shape, dt))

        cst = keep("cst", [P, C_ALL])
        ones_r = keep("ones_r", [P, PT], f32r)
        id_r = keep("id_r", [P, P], f32r)
        sel_r = keep("sel_r", [P, 2 * P], f32r)
        tri_b = keep("tri_b", [P, P], bf16)
        ones_b = keep("ones_b", [P, P], bf16)
        w0h = keep("w0h", [P, W0_COLS], f32r)
        w0l = keep("w0l", [P, W0_COLS], f32r)
        brow = keep("brow", [P, B0_COLS], f32r)
        o_bias = keep("o_bias", [P, D], f32r)
        eb2 = keep("eb2", [P, 2])
        rW = keep("rW", [P, KD, E1])
        gb = keep("gb", [P, E0])
        base = keep("base", [P, E1])
        tok2 = keep("tok2", [P, T])
        minus_half = keep("minus_half", [P, 16])
        mask_rows = keep("mask_rows", [P, P])
        mask_cols = keep("mask_cols", [P, P])
        tab_i = keep("tab_i", [P, 2 * NJ], i32)
        tab_f = keep("tab_f", [P, 3 * NJ])
        idx_credit = keep("idx_credit", [P, 4 + 8])
        cnt_i = keep("cnt_i", [P, 4 * E1], i32)
        cnt_f = keep("cnt_f", [P, 4 * E1])

        stage_stack = ExitStack()
        stage = keep("stage", [P, W0_COLS], fp32, stage_stack)
        bstage = keep("bstage", [P, B0_COLS], fp32, stage_stack)
        btmp = keep("btmp", [P, B0_COLS], f32r, stage_stack)
        ostage = keep("ostage", [16, D], fp32, stage_stack)
        ohi = keep("ohi", [16, D], f32r, stage_stack)
        olo = keep("olo", [16, D], f32r, stage_stack)
        otmp = keep("otmp", [16, D], fp32, stage_stack)
        stage_stack.close()
        A = ExitStack()

        def ka(name, shape, dt=fp32):
            return keep(name, shape, dt, A)

        xnY = ka("xnY", [P, T, D])
        xThY, xTlY = ka("xThY", [P, KD, PT], f32r), ka("xTlY", [P, KD, PT], f32r)
        ThY, TlY = ka("ThY", [P, T, D], f32r), ka("TlY", [P, T, D], f32r)
        rY = ka("rY", [P, T, D])
        xT3 = ka("xT3", [P, KD, PT])
        x3 = [ka(f"x3_{s}", [P, T, D]) for s in range(2)]
        pay = [ka(f"pay_{s}", [P, T, ROW]) for s in range(2)]
        x2 = [ka(f"x2_{s}", [P, T, D]) for s in range(2)]
        x = [ka(f"x_{s}", [P, T, D]) for s in range(2)]
        adj = [ka(f"adj_{s}", [P, T, N]) for s in range(2)]
        ATh = [ka(f"ATh_{s}", [P, 2, 2, N], f32r) for s in range(2)]
        ATl = [ka(f"ATl_{s}", [P, 2, 2, N], f32r) for s in range(2)]
        junk = ka("junk", [P, T, N], bf16)
        xn = ka("xn", [P, T, D])
        xTh, xTl = ka("xTh", [P, KD, PT], f32r), ka("xTl", [P, KD, PT], f32r)
        Th, Tl = ka("Th", [P, T, D], f32r), ka("Tl", [P, T, D], f32r)
        r = ka("r", [P, T, D])
        x1 = ka("x1", [P, T, D])
        hh, hl = ka("hh", [P, 4, PT], f32r), ka("hl", [P, 4, PT], f32r)
        s2h, s2l = ka("s2h", [P, PT], f32r), ka("s2l", [P, PT], f32r)
        ef = ka("ef", [P, 2, PT])
        gh, gl = ka("gh", [P, 2, PT], f32r), ka("gl", [P, 2, PT], f32r)
        cbT = ka("cbT", [P, PT], f32r)
        cb = ka("cb", [P, T, 16], f32r)
        st = {q: ka("st" + q, [P, T, 6]) for q in "0123"}
        mv = {q: ka("mv" + q, [P, T, 2]) for q in "0123"}
        vp = {q: ka("vp" + q, [P, 12]) for q in "0123"}
        rs = {q: ka("rs" + q, [P, 12]) for q in "0123"}
        deg, dz, nz = ka("deg", [P, T]), ka("dz", [P, T]), ka("nz", [P, T])
        dsc = [ka(f"dsc_{s}", [P, 3, T]) for s in range(2)]
        gt = {n: ka("gt_" + n, [P, T, E0]) for n in ("lg", "key", "ex", "pr", "r1", "oh1", "k2", "r2", "oh2", "w", "c")}
        gs = {n: ka("gs_" + n, [P, T]) for n in ("m", "s", "rs", "a", "b", "m2", "s2", "rs2")}
        rt = {n: ka("rt_" + n, [P, T, E1]) for n in ("lg", "key", "ex", "pr", "r1", "oh1", "k2", "r2", "oh2", "w", "pos", "q1", "q2")}
        rq = {n: ka("rq_" + n, [P, T]) for n in ("m", "s", "rs", "a", "b", "m2", "s2", "rs2")}
        mb = ka("mb", [P, T, E1], bf16)
        idx_f = ka("idx_f", [P, 2, T])
        idx = [ka(f"idx_{s}", [P, 2, T], i32) for s in range(2)]
        A.close()

        C = ExitStack()

        def kc(name, shape, dt=fp32):
            return keep(name, shape, dt, C)

        WC = 2 * KD * D
        w1h, w1l = kc("w1h", [P, E1 * WC], f32r), kc("w1l", [P, E1 * WC], f32r)
        b1r = kc("b1r", [P, 2 * E1 * D], f32r)
        SL = 4
        g = [kc(f"g_{s}", [P, ROW]) for s in range(SL)]
        gTh = [kc(f"gTh_{s}", [P, D], f32r) for s in range(SL)]
        gTl = [kc(f"gTl_{s}", [P, D], f32r) for s in range(SL)]
        hf = [kc(f"hf_{s}", [P, D]) for s in range(SL)]
        hTh = [kc(f"hTh_{s}", [P, D], f32r) for s in range(SL)]
        hTl = [kc(f"hTl_{s}", [P, D], f32r) for s in range(SL)]
        ysb = [kc(f"ysb_{s}", [P, D]) for s in range(SL)]
        wsel = [kc(f"wsel_{s}", [P, 2]) for s in range(SL)]
        isel = [kc(f"isel_{s}", [P, 2], i32) for s in range(SL)]
        mstage = kc("mstage", [P, E1 * WC // 4])
        mbst = kc("mbst", [P, 2 * E1 * D])
        mbtmp = kc("mbtmp", [P, 2 * E1 * D], f32r)
        C.close()
        Dk = ExitStack()
        dx = [keep(f"dx_{s}", [P, T, D], fp32, Dk) for s in range(2)]
        dy = [keep(f"dy_{s}", [P, T, 2 * D], fp32, Dk) for s in range(2)]
        dt_ = [keep(f"dt_{s}", [P, T, D], fp32, Dk) for s in range(2)]
        do = [keep(f"do_{s}", [P, T, D], fp32, Dk) for s in range(2)]
        Dk.close()

        ps = [ctx.enter_context(nc.psum_tensor(f"bank{b}", [P, 512], fp32)) for b in range(8)]

        bank_full = [sem(f"bank_full{b}") for b in range(8)]
        hi_done = [sem(f"hi_done{b}") for b in range(8)]
        bank_free = [sem(f"bank_free{b}") for b in range(8)]
        w_loaded, w_ready = sem("w_loaded"), sem("w_ready")
        bias_loaded, o_copied = sem("bias_loaded"), sem("o_copied")
        misc = sem("setup_steps")
        x_loaded, adj_loaded = [sem(f"x_loaded{s}") for s in range(2)], [sem(f"adj_loaded{s}") for s in range(2)]
        deg_ready = sem("deg_ready")
        var_ready = {q: sem("var_ready" + q) for q in "0123"}
        rstd_ready = {q: sem("rstd_ready" + q) for q in "0123"}
        xn_ready = {q: sem("xn_ready" + q) for q in "0123"}
        scale_ready = sem("scale_ready")
        r_ready, x1_ready, rY_ready, x3_ready = sem("r_ready"), sem("x1_ready"), sem("rY_ready"), sem("x3_ready")
        x3_summed = sem("x3_summed")
        g_shift, g_exp, g_diff, g_exp2, cb_ready = (sem(s) for s in ("g_shift", "g_exp", "g_diff", "g_exp2", "cb_ready"))
        hg_ready, gh_ready, gl_ready = sem("hg_ready"), sem("gh_ready"), sem("gl_ready")
        cbT_ready = sem("cbT_ready")
        r_shift, r_exp, mask_ready, idx_ready = (sem(s) for s in ("r_shift", "r_exp", "mask_ready", "idx_ready"))
        dve_x, dve_y = sem("dve_x_steps"), sem("dve_y_steps")
        scattered = [sem(f"scattered{s}") for s in range(2)]
        x3_stored = [sem(f"x3_stored{s}") for s in range(2)]

        counts_ready, padded, table_ready = sem("counts_ready"), sem("padded"), sem("table_ready")
        m_loaded, mw_loaded, mw_ready = sem("m_loaded"), sem("mw_loaded"), sem("mw_ready")
        slot_used = [sem(f"slot_used{s}") for s in range(SL)]
        g_loaded = [sem(f"g_loaded{s}") for s in range(SL)]
        returned = [sem(f"returned{s}") for s in range(SL)]
        gT_hi, gT_lo = [sem(f"gT_hi{s}") for s in range(SL)], [sem(f"gT_lo{s}") for s in range(SL)]
        hf_ready = [sem(f"hf_ready{s}") for s in range(SL)]
        hT_hi, hT_lo = [sem(f"hT_hi{s}") for s in range(SL)], [sem(f"hT_lo{s}") for s in range(SL)]
        y_ready = [sem(f"y_ready{s}") for s in range(SL)]
        pe_c = [sem(f"tile_products{s}") for s in range(SL)]
        sel_ready = [sem(f"sel_ready{s}") for s in range(SL)]
        c_done = sem("c_done")
        dx_loaded, dy_loaded = [sem(f"dx_loaded{s}") for s in range(2)], [sem(f"dy_loaded{s}") for s in range(2)]
        d_added, d_stored = [sem(f"d_added{s}") for s in range(2)], [sem(f"d_stored{s}") for s in range(2)]

        dve_setup, act_steps, a_done, m_clear, b_steps, mb_steps = (sem(n) for n in ("dve_setup", "act_steps", "a_done", "m_clear", "b_steps", "mb_steps"))
        mask_turned, mask_loaded, held = sem("mask_turned"), sem("mask_loaded"), sem("held")

        block = ctx.enter_context(nc.Block())

        def val(n, per, k):
            return n * per + k

        def w0(half, name, lo, cols):
            c0, _ = W0[name]
            return (w0h, w0l)[half][:, c0 + lo:c0 + lo + cols]

        def b3(ap, n):
            return ap.unsqueeze(2).to_broadcast([P, T, n])

        def hold(eng):
            eng.sem_inc(held, 1)

        class Steps:

            def __init__(self, eng, s, total):
                self.eng, self.sem, self.total, self.k = eng, s, total, 0

            def start(self, n):
                self.n, self.k = n, 0

            def __call__(self, ins):
                self.k += 1
                ins.then_inc(self.sem, 1)

            def settle(self):
                self.eng.wait_ge(self.sem, val(self.n, self.total, self.k))

            def end(self):
                assert self.k == self.total, (self.k, self.total)

        DVE_X, DVE_Y = 32, 32

        def over_pairs(eng, body):
            with eng.Fori(0, PAIRS // 2) as j:
                for s in range(2):
                    body(j, s)

        @block.sync
        def _(sp):
            sp.dma_start(cst[:, :], a["consts"]).then_inc(misc, 16)
            sp.dma_start(mask_rows[:, :], a["nodemask"]).then_inc(mask_loaded, 16)
            col = lambda name: stage[:, W0[name][0]:W0[name][0] + W0[name][1]]
            kp = lambda ap: ap.rearrange("(k p) n -> p k n", p=P)
            k2 = lambda ap, k: ap.rearrange("p (k n) -> p k n", k=k)
            sp.wait_ge(w_ready, 1)
            sp.dma_start(k2(col("g0"), KD), kp(a["g0W"])).then_inc(w_loaded, 16)
            sp.dma_start(k2(col("g1"), KD), kp(a["g1W"])).then_inc(w_loaded, 16)
            sp.dma_start(k2(col("sW1"), KD), kp(a["sW1"])).then_inc(w_loaded, 16)
            sp.dma_start(k2(col("sW2"), KD), kp(a["sW2"])).then_inc(w_loaded, 16)
            sp.dma_start(col("sW3"), a["sW3"]).then_inc(w_loaded, 16)
            sp.dma_start(k2(col("eW3"), 2), a["eW3"].rearrange("(b e) g o -> (e g) b o", b=2)).then_inc(w_loaded, 16)
            sp.dma_start(k2(col("gW"), KD), kp(a["gW"])).then_inc(w_loaded, 16)
            for e in range(E0):
                sp.dma_start(k2(col("eW1")[:, e * D:(e + 1) * D], KD), kp(a["eW1"][e])).then_inc(w_loaded, 16)
                c0 = e * P + (e % 2) * EH2
                sp.dma_start(col("eW2")[:, c0:c0 + EH2], a["eW2"][e]).then_inc(w_loaded, 16)
            sp.dma_start(rW[:, :, :], kp(a["rW"])).then_inc(w_loaded, 16)
            for row in (0, LOW_ROW):
                for name, src in (("g0", a["g0b"]), ("g1", a["g1b"]), ("sb1", a["sb1"]), ("eb1", a["eb1"]), ("sb2", a["sb2"])):
                    flat = src if len(src.shape) == 1 else src.rearrange("e n -> (e n)")
                    n = flat.shape[0]
                    sp.dma_start(bstage[row:row + 1, B0[name]:B0[name] + n], flat.rearrange("(a n) -> a n", a=1)).then_inc(bias_loaded, 16)
            for r0 in (0, 4, 8):
                sp.dma_start(ostage[r0:r0 + 4, :], a["eb3"]).then_inc(bias_loaded, 16)
            for r0 in (12, 13):
                sp.dma_start(ostage[r0:r0 + 1, :], a["sb3"].rearrange("(a n) -> a n", a=1)).then_inc(bias_loaded, 16)
            for b in range(2):
                sp.dma_start(eb2[:, b:b + 1], a["eb2"].rearrange("e (g a) -> (e g) a", a=1)[b * P:(b + 1) * P, :]).then_inc(bias_loaded, 16)
            sp.dma_start(gb[:, :], a["gb"].rearrange("(a n) -> a n", a=1).to_broadcast([P, E0])).then_inc(bias_loaded, 16)

            def load(j, s, base_pair):
                rows = bass.ds(j * (2 * PT) + (base_pair + s) * PT, PT)
                sp.dma_start(x[s][:, :, :], a["x"][rows, :].rearrange("(t p) f -> p t f", p=P)).then_inc(x_loaded[s], 16)
                sp.dma_start(adj[s][:, :, :], a["adj"][rows, :].rearrange("(t p) f -> p t f", p=P)).then_inc(adj_loaded[s], 16)

            for s in range(2):
                load(0, s, 0)

            def store_x3(j, s):
                n = j * 2 + s
                sp.wait_ge(x3_summed, val(n, 1, 1))
                hold(sp)
                rows = bass.ds(n * PT, PT)
                sp.dma_start(xres[rows, :].rearrange("(t p) f -> p t f", p=P), x3[s][:, :, :]).then_inc(x3_stored[s], 16)

            with sp.Fori(0, PAIRS // 2 - 1) as j:
                for s in range(2):
                    n = j * 2 + s
                    sp.wait_ge(x1_ready, val(n, 2, 2))
                    hold(sp)
                    sp.wait_ge(deg_ready, val(n, 1, 1))
                    hold(sp)
                    sp.wait_ge(bank_full[BANK["ATg1"]], val(n, USES[BANK["ATg1"]], USE["ATg1"]))
                    hold(sp)
                    load(j, s, 2)
                    store_x3(j, s)
            for s in range(2):
                store_x3(PAIRS // 2 - 1, s)

            for s in range(2):
                sp.wait_ge(scattered[s], (PAIRS // 2 + 1) * 2 * T * 16)
                sp.wait_ge(x3_stored[s], (PAIRS // 2 + 1) * 16)
            sp.sem_inc(a_done, 1)
            sp.wait_ge(counts_ready, 1)
            for e in range(E1):
                row = sp.value_load(cnt_i[0:1, e:e + 1], min_val=0, max_val=E1 * CAP)
                sp.dma_start(routed[bass.ds(row, P), :], cst[:, C_PAD:C_PAD + ROW]).then_inc(padded, 16)
            for e in range(E1):
                sp.dma_start(routed[E1 * CAP + e * P:E1 * CAP + (e + 1) * P, :], cst[:, C_PAD:C_PAD + ROW]).then_inc(padded, 16)
            sp.wait_ge(padded, 2 * E1 * 16)

            sp.wait_ge(table_ready, 1)
            with sp.Fori(0, TILES // SL) as j:
                for s in range(SL):
                    sp.wait_ge(slot_used[s], j + 1)
                    hold(sp)
                    row = sp.value_load(tab_i[0:1, bass.ds(j * SL + s, 1)], min_val=0, max_val=E1 * CAP + (E1 - 1) * P)
                    sp.dma_start(g[s][:, :], routed[bass.ds(row, P), :]).then_inc(g_loaded[s], 16)

            for s in range(SL):
                sp.wait_ge(returned[s], (TILES // SL + 1) * 16)

            def load_d(j, s, ahead):
                rows = bass.ds(j * (2 * PT) + (ahead + s) * PT, PT)
                sp.dma_start(dx[s][:, :, :], xres[rows, :].rearrange("(t p) f -> p t f", p=P)).then_inc(dx_loaded[s], 16)
                rows2 = bass.ds(j * (4 * PT) + (ahead + s) * 2 * PT, 2 * PT)
                sp.dma_start(dy[s][:, :, :].rearrange("p t (k f) -> p t k f", k=2),
                             back[rows2, :].rearrange("(t p k) f -> p t k f", p=P, k=2)).then_inc(dy_loaded[s], 16)

            for s in range(2):
                load_d(0, s, 0)
            with sp.Fori(0, PAIRS // 2 - 1) as j:
                for s in range(2):
                    sp.wait_ge(d_added[s], j * 2 + 2)
                    hold(sp)
                    load_d(j, s, 2)
            for s in range(2):
                sp.wait_ge(d_stored[s], (PAIRS // 2 + 1) * 16)

        @block.scalar
        def _(act):
            def freed(job, n, ins):
                ins.then_inc(bank_free[BANK[job]], 1)

            def full(job, n):
                act.wait_ge(bank_full[BANK[job]], val(n, USES[BANK[job]], USE[job]))

            def high(job, n, dst, func=ACT.Copy):
                full(job, n)
                nc.scalar.activation(dst, ps[BANK[job]][:, :], func).then_inc(hi_done[BANK[job]], 1)

            def high_scaled(job, n, dst, gph, d):
                full(job, n)
                for i in range(2):
                    t = 2 * gph + i
                    ins = nc.scalar.activation(dst[:, t, :], ps[BANK[job]][:, i * D:(i + 1) * D], ACT.Copy, scale=d[:, t:t + 1])
                ins.then_inc(hi_done[BANK[job]], 1)

            def conv_out(job, n, dst, gph, d, ready):
                full(job, n)
                for i in range(2):
                    t = 2 * gph + i
                    ins = nc.scalar.activation(dst[:, t, :], ps[BANK[job]][:, i * D:(i + 1) * D], ACT.Relu, scale=d[:, t:t + 1])
                ins.then_inc(bank_free[BANK[job]], 1)

            def layer0(j, s):
                n = j * 2 + s
                act.wait_ge(adj_loaded[s], val(j, 16, 16))
                for t in range(T):
                    ins = nc.scalar.activation(junk[:, t, :], adj[s][:, t, :], ACT.Copy, accum_out=deg[:, t:t + 1])
                ins.then_inc(deg_ready, 1)
                for k in range(KD):
                    high(f"xT0k{k}", n, xTh[:, k, :])
                for q in range(2):
                    high(f"ATg{q}", n, ATh[s][:, q, :, :].rearrange("p a b -> p (a b)"))
                act.wait_ge(scale_ready, val(n, 1, 1))
                for q in range(2):
                    high_scaled(f"T0g{q}", n, Th, q, dsc[s][:, 0, :])
                for q in range(2):
                    conv_out(f"M0g{q}", n, r, q, dsc[s][:, 0, :], r_ready)
                for k in range(KD):
                    high(f"xT1k{k}", n, xTh[:, k, :])
                for m in range(2):
                    high(f"S1m{m}", n, hh[:, m, :], ACT.Relu)
                act.wait_ge(g_shift, val(n, 1, 1))
                nc.scalar.activation(gt["ex"][:, :, :], gt["key"][:, :, :], ACT.Exp).then_inc(g_exp, 1)
                high("S2", n, s2h[:, :], ACT.Relu)
                for b in range(2):
                    for i in range(2):
                        high(f"E1e{2 * b + i}", n, hh[:, (2 * (b + 1) + i) % 4, :], ACT.Relu)
                    full(f"EP{b}", n)
                    nc.scalar.activation(ef[:, b, :], ps[BANK[f"EP{b}"]][:, :], ACT.Relu, bias=eb2[:, b:b + 1])\
                        .then_inc(bank_free[BANK[f"EP{b}"]], 1)
                    if b == 0:
                        act.wait_ge(g_diff, val(n, 1, 1))
                        nc.scalar.activation(gt["w"][:, :, :], gt["k2"][:, :, :], ACT.Exp).then_inc(g_exp2, 1)
                full("CBT", n)
                nc.scalar.activation(cbT[0:16, :], ps[BANK["CBT"]][0:16, :], ACT.Copy).then_inc(bank_free[BANK["CBT"]], 1)
                for b in range(2):
                    act.wait_ge(hg_ready, val(n, 2, b + 1))
                    nc.scalar.activation(gh[:, b, :], ef[:, b, :], ACT.Copy).then_inc(gh_ready, 1)

            def layer1(j, s):
                n = j * 2 + s
                for k in range(KD):
                    high(f"xT2k{k}", n, xThY[:, k, :])
                for q in range(2):
                    high_scaled(f"T1g{q}", n, ThY, q, dsc[s][:, 1, :])
                for q in range(2):
                    conv_out(f"M1g{q}", n, rY, q, dsc[s][:, 2, :], rY_ready)
                for k in range(KD):
                    job = f"xT3k{k}"
                    full(job, n)
                    nc.scalar.activation(xT3[:, k, :], ps[BANK[job]][:, :], ACT.Copy).then_inc(bank_free[BANK[job]], 1)
                act.wait_ge(r_shift, val(n, 1, 1))
                nc.scalar.activation(rt["ex"][:, :, :], rt["key"][:, :, :], ACT.Exp).then_inc(r_exp, 1)

            act.wait_ge(w_ready, 3)
            def body(j, s):
                layer0(j, s)
                layer1(j, s)
            over_pairs(act, body)

            act.wait_ge(a_done, 1)
            kp = lambda ap: ap.rearrange("(k p) n -> p k n", p=P)
            act.wait_ge(m_clear, 1)
            for row in (0, LOW_ROW):
                for w, name in enumerate(("b1", "b2")):
                    act.dma_start(mbst[row:row + 1, w * E1 * D:(w + 1) * E1 * D],
                                  a[name].rearrange("(a e) n -> a (e n)", a=1)).then_inc(m_loaded, 16)
            for h in range(4):
                if h:
                    act.wait_ge(mw_ready, 2 * h)
                for e in range(E1 // 4):
                    for w, name in enumerate(("w1", "w2")):
                        c0 = e * WC + w * KD * D
                        act.dma_start(mstage[:, c0:c0 + KD * D].rearrange("p (k n) -> p k n", k=KD),
                                      kp(a[name][h * E1 // 4 + e])).then_inc(mw_loaded, 16)
            for s in range(SL):
                act.sem_inc(y_ready[s], 1)

            with act.Fori(0, TILES // SL) as j:
                for s in range(SL):
                    act.wait_ge(pe_c[s], j * 4 + 1)
                    nc.scalar.activation(gTh[s][:, :], ps[2 * s][:, 0:D], ACT.Copy).then_inc(gT_hi[s], 1)
                for s in range(SL):
                    act.wait_ge(pe_c[s], j * 4 + 2)
                    nc.scalar.activation(hf[s][:, :], ps[2 * s + 1][:, 0:D], ACT.Gelu).then_inc(hf_ready[s], 1)
                for s in range(SL):
                    act.wait_ge(pe_c[s], j * 4 + 3)
                    nc.scalar.activation(hTh[s][:, :], ps[2 * s][:, 0:D], ACT.Copy).then_inc(hT_hi[s], 1)
                for s in range(SL):
                    act.wait_ge(pe_c[s], j * 4 + 4)
                    act.wait_ge(sel_ready[s], j + 1)
                    act.wait_ge(returned[s], j * 16 + 16)
                    nc.scalar.activation(ysb[s][:, :], ps[2 * s + 1][:, 0:D], ACT.Copy, scale=wsel[s][:, 0:1]).then_inc(y_ready[s], 1)

            with act.Fori(0, PAIRS // 2) as j:
                for s in range(2):
                    act.wait_ge(d_added[s], j * 2 + 2)
                    rows = bass.ds(j * (2 * PT) + s * PT, PT)
                    act.dma_start(out[rows, :].rearrange("(t p) f -> p t f", p=P), do[s][:, :, :]).then_inc(d_stored[s], 16)

        @block.vector
        def _(dve):
            X, Y = Steps(dve, dve_x, DVE_X), Steps(dve, dve_y, DVE_Y)
            V = nc.vector

            def low(job, n, dst, hi, op=None):
                dve.wait_ge(hi_done[BANK[job]], val(n, HI_USES[BANK[job]], HI_USE[job]))
                bank = ps[BANK[job]]
                if op is None:
                    ins = V.tensor_tensor(dst, bank[:, :], hi, ALU.subtract)
                else:
                    ins = V.scalar_tensor_tensor(out=dst, in0=bank[:, :], scalar=0.0, in1=hi, op0=op, op1=ALU.subtract)
                ins.then_inc(bank_free[BANK[job]], 1)

            def low_scaled(job, n, dst, hi, gph, d):
                dve.wait_ge(hi_done[BANK[job]], val(n, HI_USES[BANK[job]], HI_USE[job]))
                for i in range(2):
                    t = 2 * gph + i
                    ins = V.scalar_tensor_tensor(out=dst[:, t, :], in0=ps[BANK[job]][:, i * D:(i + 1) * D], scalar=d[:, t:t + 1],
                                                 in1=hi[:, t, :].bitcast(fp32), op0=ALU.mult, op1=ALU.subtract)
                ins.then_inc(bank_free[BANK[job]], 1)

            def stats(C, q, src):
                for t in range(T):
                    ins = V.bn_stats(st[q][:, t, :], src[:, t, :])
                C(ins)
                C.settle()
                hold(dve)
                for t in range(T):
                    ins = V.bn_aggr(mv[q][:, t, :], st[q][:, t, :])
                C(ins)
                C.settle()
                V.tensor_scalar(vp[q][:, 0:T], mv[q][:, :, 1], LN_EPS, None, ALU.add).then_inc(var_ready[q], 1)

            def norm(n, q, src, dst):
                dve.wait_ge(rstd_ready[q], val(n, 1, 1))
                for t in range(T):
                    ins = V.tensor_scalar(dst[:, t, 0:D], src[:, t, :], mv[q][:, t, 0:1], rs[q][:, t:t + 1], ALU.subtract, ALU.mult)
                ins.then_inc(xn_ready[q], 1)

            def top2(C, b, q, rev, n_e):
                C(V.scalar_tensor_tensor(out=b["r1"][:, :, :], in0=b["key"][:, :, :], scalar=0.0, in1=rev, op0=ALU.is_equal, op1=ALU.mult))
                C.settle()
                C(V.tensor_reduce(q["a"][:, :], b["r1"][:, :, :], axis=AX.X, op=ALU.max))
                C.settle()
                C(V.tensor_tensor(b["oh1"][:, :, :], b["r1"][:, :, :], b3(q["a"][:, :], n_e), ALU.is_equal))
                C.settle()
                C(V.scalar_tensor_tensor(out=b["r1"][:, :, :], in0=b["oh1"][:, :, :], scalar=-1000.0, in1=b["key"][:, :, :], op0=ALU.mult, op1=ALU.add))
                C.settle()
                C(V.tensor_reduce(q["m2"][:, :], b["r1"][:, :, :], axis=AX.X, op=ALU.max))
                C.settle()
                C(V.tensor_tensor(b["r2"][:, :, :], b["r1"][:, :, :], b3(q["m2"][:, :], n_e), ALU.is_equal))
                C.settle()
                C(V.tensor_tensor(b["r2"][:, :, :], b["r2"][:, :, :], rev, ALU.mult))
                C.settle()
                C(V.tensor_reduce(q["b"][:, :], b["r2"][:, :, :], axis=AX.X, op=ALU.max))
                C.settle()
                C(V.tensor_tensor(b["oh2"][:, :, :], b["r2"][:, :, :], b3(q["b"][:, :], n_e), ALU.is_equal))

            def shifted(C, b, q, n_e, ready):
                C(V.tensor_reduce(q["m"][:, :], b["lg"][:, :, :], axis=AX.X, op=ALU.max))
                C.settle()
                C(V.tensor_tensor(b["key"][:, :, :], b["lg"][:, :, :], b3(q["m"][:, :], n_e), ALU.subtract))
                C.settle()
                V.tensor_scalar(b["key"][:, :, :], b["key"][:, :, :], KEY_FLOOR, None, ALU.max).then_inc(ready, 1)

            def softmax(C, b, q, n_e):
                C(V.reduce_sum(q["s"][:, :], b["ex"][:, :, :], axis=AX.X))
                C.settle()
                C(V.reciprocal(q["rs"][:, :], q["s"][:, :]))
                C.settle()
                C(V.tensor_tensor(b["pr"][:, :, :], b["ex"][:, :, :], b3(q["rs"][:, :], n_e), ALU.mult))

            def rep(c0, n_e):
                return cst[:, c0:c0 + n_e].unsqueeze(1).to_broadcast([P, T, n_e])

            def layer0(j, s):
                n = j * 2 + s
                X.start(n)
                dve.wait_ge(x_loaded[s], val(j, 16, 16))
                stats(X, "0", x[s])
                dve.wait_ge(deg_ready, val(n, 1, 1))
                X(V.tensor_scalar(dz[:, :], deg[:, :], 0.0, None, ALU.is_equal))
                X.settle()
                X(V.tensor_tensor(vp["0"][:, 4:8], deg[:, :], dz[:, :], ALU.add))
                X(V.tensor_scalar(nz[:, :], dz[:, :], -1.0, 1.0, ALU.mult, ALU.add))
                V.tensor_scalar(vp["0"][:, 8:12], deg[:, :], 1.0, DEG_EPS, ALU.add, ALU.add).then_inc(var_ready["0"], 1)
                norm(n, "0", x[s], xn)
                X(V.tensor_tensor(dsc[s][:, 0, :], rs["0"][:, 4:8], nz[:, :], ALU.mult))
                X(V.tensor_copy(dsc[s][:, 1, :], rs["0"][:, 8:12]))
                V.tensor_tensor(dsc[s][:, 2, :], rs["0"][:, 8:12], mask_cols[:, bass.ds(j * (2 * T) + s * T, T)], ALU.mult).then_inc(scale_ready, 1)
                for k in range(KD):
                    low(f"xT0k{k}", n, xTl[:, k, :], xTh[:, k, :].bitcast(fp32))
                for q in range(2):
                    low(f"ATg{q}", n, ATl[s][:, q, :, :].rearrange("p a b -> p (a b)"), ATh[s][:, q, :, :].rearrange("p a b -> p (a b)").bitcast(fp32))
                dve.wait_ge(scale_ready, val(n, 1, 1))
                for q in range(2):
                    low_scaled(f"T0g{q}", n, Tl, Th, q, dsc[s][:, 0, :])
                dve.wait_ge(x1_ready, val(n, 2, 2))
                stats(X, "1", x1)
                norm(n, "1", x1, xn)
                for k in range(KD):
                    low(f"xT1k{k}", n, xTl[:, k, :], xTh[:, k, :].bitcast(fp32))
                dve.wait_ge(bank_full[BANK["GL"]], val(n, USES[BANK["GL"]], USE["GL"]))
                V.tensor_tensor(gt["lg"][:, :, :], ps[BANK["GL"]][:, 0:T * E0].rearrange("p (t e) -> p t e", t=T),
                                gb[:, :].unsqueeze(1).to_broadcast([P, T, E0]), ALU.add).then_inc(bank_free[BANK["GL"]], 1)
                dve.wait_ge(bank_free[BANK["GL"]], val(n, USES[BANK["GL"]], USE["GL"] + 1))
                shifted(X, gt, gs, E0, g_shift)
                for m in range(2):
                    low(f"S1m{m}", n, hl[:, m, :], hh[:, m, :].bitcast(fp32), ALU.max)
                dve.wait_ge(g_exp, val(n, 1, 1))
                softmax(X, gt, gs, E0)
                top2(X, gt, gs, rep(C_REV4, E0), E0)
                X(V.tensor_tensor(gt["k2"][:, :, :], gt["pr"][:, :, :], b3(gs["rs"][:, :], E0), ALU.subtract))
                X.settle()
                V.tensor_tensor(gt["oh1"][:, :, :], gt["oh1"][:, :, :], gt["oh2"][:, :, :], ALU.add).then_inc(g_diff, 1)
                low("S2", n, s2l[:, :], s2h[:, :].bitcast(fp32), ALU.max)
                for i in range(2):
                    low(f"E1e{i}", n, hl[:, 2 + i, :], hh[:, 2 + i, :].bitcast(fp32), ALU.max)
                dve.wait_ge(g_exp2, val(n, 1, 1))
                X(V.tensor_tensor(gt["w"][:, :, :], gt["w"][:, :, :], gt["oh1"][:, :, :], ALU.mult))
                X.settle()
                X(V.reduce_sum(gs["s2"][:, :], gt["w"][:, :, :], axis=AX.X))
                X.settle()
                X(V.reciprocal(gs["rs2"][:, :], gs["s2"][:, :]))
                X.settle()
                X(V.tensor_tensor(gt["c"][:, :, :], gt["w"][:, :, :], b3(gs["rs2"][:, :], E0), ALU.mult))
                X.settle()
                X(V.tensor_copy(cb[:, :, 0:4], gt["c"][:, :, :]))
                X.settle()
                X(V.tensor_copy(cb[:, :, 4:8], cb[:, :, 0:4].bitcast(fp32)))
                V.tensor_tensor(cb[:, :, 8:12], gt["c"][:, :, :], cb[:, :, 0:4].bitcast(fp32), ALU.subtract).then_inc(cb_ready, 1)
                for i in range(2):
                    low(f"E1e{2 + i}", n, hl[:, i, :], hh[:, i, :].bitcast(fp32), ALU.max)
                for b in range(2):
                    job = f"G{b}"
                    dve.wait_ge(bank_full[BANK[job]], val(n, USES[BANK[job]], USE[job]))
                    dve.wait_ge(bank_free[BANK[f"EP{b}"]], val(n, USES[BANK[f"EP{b}"]], USE[f"EP{b}"] + 1))
                    X(V.tensor_tensor(ef[:, b, :], ef[:, b, :], ps[BANK[job]][:, :], ALU.mult))
                    X.settle()
                    V.sem_inc(hg_ready, 1)
                    V.sem_inc(bank_free[BANK[job]], 1)
                for b in range(2):
                    dve.wait_ge(gh_ready, val(n, 2, b + 1))
                    V.tensor_tensor(gl[:, b, :], ef[:, b, :], gh[:, b, :].bitcast(fp32), ALU.subtract).then_inc(gl_ready, 1)
                for q in range(2):
                    job = f"O1g{q}"
                    dve.wait_ge(bank_full[BANK[job]], val(n, USES[BANK[job]], USE[job]))
                    V.tensor_tensor(x2[s][:, 2 * q:2 * q + 2, :].rearrange("p a b -> p (a b)"), x1[:, 2 * q:2 * q + 2, :].rearrange("p a b -> p (a b)"),
                                    ps[BANK[job]][:, :], ALU.add).then_inc(bank_free[BANK[job]], 1)
                X.end()

            def layer1(j, s):
                n = j * 2 + s
                Y.start(n)
                for q in range(2):
                    dve.wait_ge(bank_free[BANK[f"O1g{q}"]], val(n, USES[BANK[f"O1g{q}"]], USE[f"O1g{q}"] + 1))
                stats(Y, "2", x2[s])
                norm(n, "2", x2[s], xnY)
                for k in range(KD):
                    low(f"xT2k{k}", n, xTlY[:, k, :], xThY[:, k, :].bitcast(fp32))
                for q in range(2):
                    low_scaled(f"T1g{q}", n, TlY, ThY, q, dsc[s][:, 1, :])
                dve.wait_ge(x3_ready, val(n, 2, 2))
                stats(Y, "3", x3[s])
                dve.wait_ge(scattered[s], val(j, 2 * T * 16, 2 * T * 16))
                norm(n, "3", x3[s], pay[s])
                job = "RL"
                dve.wait_ge(bank_full[BANK[job]], val(n, USES[BANK[job]], USE[job]))
                Y(V.tensor_copy(rt["lg"][:, :, :], ps[BANK[job]][:, 0:T * E1].rearrange("p (t e) -> p t e", t=T)))
                Y.settle()
                V.sem_inc(bank_free[BANK[job]], 1)
                shifted(Y, rt, rq, E1, r_shift)
                dve.wait_ge(r_shift, val(n, 1, 1))
                top2(Y, rt, rq, rep(C_REV8, E1), E1)
                Y.settle()
                V.tensor_tensor(mb[:, :, :], rt["oh1"][:, :, :], rt["oh2"][:, :, :], ALU.add).then_inc(mask_ready, 1)
                dve.wait_ge(r_exp, val(n, 1, 1))
                softmax(Y, rt, rq, E1)
                Y.settle()
                dve.wait_ge(mask_ready, val(n, 1, 1))
                Y(V.tensor_tensor(rt["w"][:, :, :], rt["pr"][:, :, :], mb[:, :, :], ALU.mult))
                Y.settle()
                Y(V.reduce_sum(rq["s2"][:, :], rt["w"][:, :, :], axis=AX.X))
                Y.settle()
                Y(V.tensor_scalar(rq["s2"][:, :], rq["s2"][:, :], 1e-12, None, ALU.max))
                Y.settle()
                Y(V.reciprocal(rq["rs2"][:, :], rq["s2"][:, :]))
                Y.settle()
                Y(V.tensor_tensor(pay[s][:, :, D:D + E1], rt["w"][:, :, :], b3(rq["rs2"][:, :], E1), ALU.mult))
                Y(V.tensor_tensor(pay[s][:, :, D + E1:ROW], rt["oh2"][:, :, :], b3(tok2[:, :], E1), ALU.add))
                job = "POS"
                dve.wait_ge(bank_full[BANK[job]], val(n, USES[BANK[job]], USE[job]))
                Y(V.tensor_tensor(rt["pos"][:, :, :], ps[BANK[job]][:, 0:T * E1].rearrange("p (t e) -> p t e", t=T),
                                  base[:, :].unsqueeze(1).to_broadcast([P, T, E1]), ALU.add))
                Y.settle()
                Y(V.tensor_tensor(base[:, :], ps[BANK[job]][:, T * E1:(T + 1) * E1], base[:, :], ALU.add))
                Y(V.tensor_scalar(tok2[:, :], tok2[:, :], float(2 * PT), None, ALU.add))
                Y(V.tensor_tensor(rt["q1"][:, :, :], rt["pos"][:, :, :], rt["oh1"][:, :, :], ALU.mult))
                Y(V.tensor_tensor(rt["q2"][:, :, :], rt["pos"][:, :, :], rt["oh2"][:, :, :], ALU.mult))
                Y.settle()
                V.sem_inc(bank_free[BANK[job]], 1)
                Y(V.reduce_sum(idx_f[:, 0, :], rt["q1"][:, :, :], axis=AX.X))
                Y(V.reduce_sum(idx_f[:, 1, :], rt["q2"][:, :, :], axis=AX.X))
                Y.settle()
                V.tensor_copy(idx[s][:, :, :], idx_f[:, :, :]).then_inc(idx_ready, 1)
                Y.end()

            V.memset(stage[:, :], 0.0)
            V.memset(bstage[:, :], 0.0)
            V.memset(ostage[:, :], 0.0).then_inc(w_ready, 1)
            V.memset(minus_half[:, :], -0.5)
            V.memset(cbT[:, :].bitcast(fp32), 0.0)
            V.memset(ones_b[:, :], 1.0)
            V.memset(cb[:, :, :].bitcast(fp32), 0.0)
            V.memset(btmp[:, :].bitcast(fp32), 0.0)
            V.memset(otmp[:, :], 1.0).then_inc(dve_setup, 1)
            dve.wait_ge(dve_setup, 1)
            V.memset(cb[:, :, 12:14].bitcast(fp32), 1.0)
            V.memset(ones_r[:, :].bitcast(fp32), 1.0).then_inc(dve_setup, 1)
            dve.wait_ge(dve_setup, 2)
            dve.wait_ge(misc, 16)
            V.tensor_copy(id_r[:, :], cst[:, C_ID:C_ID + P])
            V.tensor_copy(sel_r[:, :], cst[:, C_SEL:C_SEL + 2 * P])
            V.tensor_copy(tri_b[:, :], cst[:, C_TRI:C_TRI + P])
            V.tensor_copy(base[:, :], cst[:, C_ECAP:C_ECAP + E1])
            V.tensor_copy(tok2[:, :], cst[:, C_TOK2:C_TOK2 + T])
            dve.wait_ge(mask_turned, 1)
            V.tensor_copy(mask_cols[:, :], ps[0][:, 0:P]).then_inc(dve_setup, 1)
            dve.wait_ge(dve_setup, 3)
            for b in range(8):
                V.sem_inc(bank_free[b], 1)
            dve.wait_ge(bias_loaded, 16 * 18)
            V.tensor_copy(brow[:, :], bstage[:, :]).then_inc(dve_setup, 1)
            V.tensor_copy(ohi[:, :], ostage[:, :]).then_inc(dve_setup, 1)
            dve.wait_ge(dve_setup, 5)
            V.tensor_copy(btmp[LOW_ROW:LOW_ROW + 1, :], brow[LOW_ROW:LOW_ROW + 1, :].bitcast(fp32)).then_inc(dve_setup, 1)
            V.tensor_tensor(olo[:, :], ostage[:, :], ohi[:, :].bitcast(fp32), ALU.subtract).then_inc(dve_setup, 1)
            dve.wait_ge(dve_setup, 7)
            V.tensor_tensor(brow[LOW_ROW:LOW_ROW + 1, :], bstage[LOW_ROW:LOW_ROW + 1, :], btmp[LOW_ROW:LOW_ROW + 1, :].bitcast(fp32), ALU.subtract)
            V.tensor_scalar(otmp[:, :], ohi[:, :].bitcast(fp32), cst[0:16, C_MH:C_MH + 1], None, ALU.mult)
            V.memset(o_bias[:, :].bitcast(fp32), 0.0).then_inc(dve_setup, 1)
            dve.wait_ge(dve_setup, 8)
            V.scalar_tensor_tensor(out=o_bias[0:16, :], in0=olo[:, :].bitcast(fp32), scalar=cst[0:16, C_ML:C_ML + 1], in1=otmp[:, :],
                                   op0=ALU.mult, op1=ALU.add)
            dve.wait_ge(w_loaded, 16 * 16)
            V.tensor_copy(w0h[:, :], stage[:, :]).then_inc(w_ready, 1)
            dve.wait_ge(w_ready, 2)
            V.tensor_tensor(w0l[:, :], stage[:, :], w0h[:, :].bitcast(fp32), ALU.subtract).then_inc(w_ready, 1)
            dve.wait_ge(w_ready, 3)

            def body(j, s):
                layer0(j, s)
                layer1(j, s)
            over_pairs(dve, body)

            dve.wait_ge(idx_ready, PAIRS)
            k = [0]

            def b_step(ins):
                k[0] += 1
                ins.then_inc(b_steps, 1)
                dve.wait_ge(b_steps, k[0])

            V.tensor_copy(cnt_i[:, 0:E1], base[:, :]).then_inc(counts_ready, 1)
            dve.wait_ge(counts_ready, 1)
            b_step(V.tensor_tensor(cnt_f[:, 0:E1], base[:, :], cst[:, C_ECAP:C_ECAP + E1], ALU.subtract))
            b_step(V.tensor_scalar(cnt_f[:, 0:E1], cnt_f[:, 0:E1], float(P - 1), None, ALU.add))
            b_step(V.tensor_copy(cnt_i[:, E1:2 * E1], cnt_f[:, 0:E1]))
            b_step(V.tensor_scalar(cnt_i[:, 2 * E1:3 * E1], cnt_i[:, E1:2 * E1], 7, None, ALU.logical_shift_right))
            b_step(V.tensor_copy(cnt_f[:, E1:2 * E1], cnt_i[:, 2 * E1:3 * E1]))
            b_step(V.tensor_scalar(cnt_f[:, E1:2 * E1], cnt_f[:, E1:2 * E1], float(P), None, ALU.mult))
            b_step(V.tensor_copy(cnt_f[:, 2 * E1:3 * E1], cnt_f[:, E1:2 * E1]))
            for e in range(1, E1):
                b_step(V.tensor_tensor(cnt_f[:, 2 * E1 + e:2 * E1 + e + 1], cnt_f[:, 2 * E1 + e:2 * E1 + e + 1],
                                       cnt_f[:, 2 * E1 + e - 1:2 * E1 + e], ALU.add))
            b_step(V.tensor_scalar(cnt_f[:, 3 * E1:4 * E1], cnt_f[:, E1:2 * E1], -1.0, float(CAP), ALU.mult, ALU.add))
            b_step(V.tensor_copy(tab_f[:, 0:NJ], cst[:, C_J:C_J + NJ]))
            for e in range(E1):
                b_step(V.tensor_scalar(tab_f[:, NJ:2 * NJ], cst[:, C_J:C_J + NJ], cnt_f[:, 2 * E1 + e:2 * E1 + e + 1],
                                       cnt_f[:, 3 * E1 + e:3 * E1 + e + 1], ALU.is_ge, ALU.mult))
                b_step(V.tensor_tensor(tab_f[:, 0:NJ], tab_f[:, 0:NJ], tab_f[:, NJ:2 * NJ], ALU.add))
            b_step(V.memset(tab_f[:, 2 * NJ:3 * NJ], 0.0))
            for e in range(E1 - 1):
                b_step(V.tensor_scalar(tab_f[:, NJ:2 * NJ], cst[:, C_J:C_J + NJ], cnt_f[:, 2 * E1 + e:2 * E1 + e + 1], None, ALU.is_ge))
                b_step(V.tensor_tensor(tab_f[:, 2 * NJ:3 * NJ], tab_f[:, 2 * NJ:3 * NJ], tab_f[:, NJ:2 * NJ], ALU.add))
            V.tensor_copy(tab_i[:, 0:NJ], tab_f[:, 0:NJ])
            V.tensor_copy(tab_i[:, NJ:2 * NJ], tab_f[:, 2 * NJ:3 * NJ]).then_inc(table_ready, 1)

            dve.wait_ge(a_done, 1)
            V.memset(mbst[:, :], 0.0).then_inc(m_clear, 1)
            dve.wait_ge(m_loaded, 16 * 4)
            quarter = E1 * WC // 4
            V.tensor_copy(b1r[:, :], mbst[:, :]).then_inc(mb_steps, 1)
            dve.wait_ge(mb_steps, 1)
            V.tensor_copy(mbtmp[LOW_ROW:LOW_ROW + 1, :], b1r[LOW_ROW:LOW_ROW + 1, :].bitcast(fp32)).then_inc(mb_steps, 1)
            dve.wait_ge(mb_steps, 2)
            V.tensor_tensor(b1r[LOW_ROW:LOW_ROW + 1, :], mbst[LOW_ROW:LOW_ROW + 1, :], mbtmp[LOW_ROW:LOW_ROW + 1, :].bitcast(fp32), ALU.subtract)
            for h in range(4):
                dve.wait_ge(mw_loaded, 16 * (h + 1) * E1 // 2)
                cols = slice(h * quarter, (h + 1) * quarter)
                V.tensor_copy(w1h[:, cols], mstage[:, :]).then_inc(mw_ready, 1)
                dve.wait_ge(mw_ready, 2 * h + 1)
                V.tensor_tensor(w1l[:, cols], mstage[:, :], w1h[:, cols].bitcast(fp32), ALU.subtract).then_inc(mw_ready, 1)

            for s in range(SL):
                V.sem_inc(slot_used[s], 1)
            with dve.Fori(0, TILES // SL) as j:
                for s in range(SL):
                    dve.wait_ge(gT_hi[s], j + 1)
                    V.tensor_tensor(gTl[s][:, :], ps[2 * s][:, 0:D], gTh[s][:, :].bitcast(fp32), ALU.subtract).then_inc(gT_lo[s], 1)
                for s in range(SL):
                    dve.wait_ge(g_loaded[s], j * 16 + 16)
                    e = dve.value_load(tab_i[0:1, bass.ds(j * SL + (NJ + s), 1)], min_val=0, max_val=E1 - 1)
                    dve.wait_ge(returned[s], j * 16 + 16)
                    dve.wait_ge(y_ready[s], j + 1)
                    V.tensor_copy(isel[s][:, 0:1], g[s][:, bass.ds(e + (D + E1), 1)])
                    V.tensor_copy(wsel[s][:, 0:1], g[s][:, bass.ds(e + D, 1)]).then_inc(sel_ready[s], 1)
                    dve.wait_ge(sel_ready[s], j + 1)
                    V.sem_inc(slot_used[s], 1)
                for s in range(SL):
                    dve.wait_ge(hT_hi[s], j + 1)
                    V.tensor_tensor(hTl[s][:, :], ps[2 * s][:, 0:D], hTh[s][:, :].bitcast(fp32), ALU.subtract).then_inc(hT_lo[s], 1)

            for s in range(2):
                V.sem_inc(d_stored[s], 16)
            with dve.Fori(0, PAIRS // 2) as j:
                for s in range(2):
                    dve.wait_ge(dy_loaded[s], j * 16 + 16)
                    dve.wait_ge(dx_loaded[s], j * 16 + 16)
                    V.tensor_tensor(dt_[s][:, :, :], dx[s][:, :, :], dy[s][:, :, 0:D], ALU.add).then_inc(d_added[s], 1)
                    dve.wait_ge(d_added[s], j * 2 + 1)
                    dve.wait_ge(d_stored[s], j * 16 + 16)
                    V.tensor_tensor(do[s][:, :, :], dt_[s][:, :, :], dy[s][:, :, D:2 * D], ALU.add).then_inc(d_added[s], 1)

        @block.gpsimd
        def _(pool):
            G = nc.gpsimd
            for s in range(2):
                pool.dma_start(idx_credit[:, 2 * s:2 * s + 2], a["consts"][:, 0:2]).then_inc(scattered[s], 2 * T * 16)
            for s in range(SL):
                pool.dma_start(idx_credit[:, 4 + 2 * s:6 + 2 * s], a["consts"][:, 0:2]).then_inc(returned[s], 16)
            pool.wait_ge(dve_setup, 3)
            for s in range(2):
                G.sem_inc(x3_stored[s], 16)

            def power(n, q, cols):
                per = 2 if q == "0" else 1
                pool.wait_ge(var_ready[q], val(n, per, per))
                G.tensor_tensor(rs[q][:, 0:cols], vp[q][:, 0:cols], minus_half[:, 0:cols], ALU.pow).then_inc(rstd_ready[q], 1)

            def residual(n, name, src, add, dst, ready):
                for q in range(2):
                    job = f"{name}g{q}"
                    pool.wait_ge(bank_free[BANK[job]], val(n, USES[BANK[job]], USE[job] + 1))
                    half = lambda b: b[:, 2 * q:2 * q + 2, :].rearrange("p a b -> p (a b)")
                    G.tensor_tensor(half(dst), half(src), half(add), ALU.add).then_inc(ready, 1)

            def body(j, s):
                n = j * 2 + s
                power(n, "0", 12)
                residual(n, "M0", x[s], r, x1, x1_ready)
                power(n, "1", T)
                power(n, "2", T)
                pool.wait_ge(x3_stored[s], val(j, 16, 16))
                residual(n, "M1", x2[s], rY, x3[s], x3_ready)
                power(n, "3", T)
                pool.wait_ge(xn_ready["3"], val(n, 1, 1))
                G.tensor_tensor(x3[s][:, :, :], x3[s][:, :, :], pay[s][:, :, 0:D], ALU.add).then_inc(x3_summed, 1)
                pool.wait_ge(idx_ready, val(n, 1, 1))
                hold(pool)
                for t in range(T):
                    for k in range(2):
                        G.indirect_dma_start(out=routed, out_offset=bass.IndirectOffsetOnAxis(ap=idx[s][:, k, t:t + 1], axis=0),
                                             in_=pay[s][:, t, :], in_offset=None).then_inc(scattered[s], 16)

            over_pairs(pool, body)

            with pool.Fori(0, TILES // SL) as j:
                for s in range(SL):
                    pool.wait_ge(y_ready[s], j + 2)
                    pool.wait_ge(sel_ready[s], j + 1)
                    hold(pool)
                    G.indirect_dma_start(out=back, out_offset=bass.IndirectOffsetOnAxis(ap=isel[s][:, 0:1], axis=0),
                                         in_=ysb[s][:, :], in_offset=None, bounds_check=2 * TOK - 1, oob_is_err=False)\
                        .then_inc(returned[s], 16)

        @block.tensor
        def _(pe):
            mm, turn = nc.tensor.matmul, nc.tensor.transpose
            ident = cst[:, C_ID:C_ID + P]

            def free(job, n):
                pe.wait_ge(bank_free[BANK[job]], val(n, USES[BANK[job]], USE[job]))

            def read_out(job, n):
                pe.wait_ge(bank_free[BANK[job]], val(n, USES[BANK[job]], USE[job] + 1))

            def filled(job, ins):
                ins.then_inc(bank_full[BANK[job]], 1)

            def mm3(o, left, right, start, stop):
                mm(o, left[0], right[0], start=start, stop=False)
                mm(o, left[0], right[1], start=False, stop=False)
                return mm(o, left[1], right[0], start=False, stop=stop)

            def W(name, lo, cols):
                return w0(0, name, lo, cols), w0(1, name, lo, cols)

            def transposes(n, name, src, feature):
                for k in range(KD):
                    job = f"{name}k{k}"
                    free(job, n)
                    for t in range(T):
                        ins = turn(ps[BANK[job]][:, t * P:(t + 1) * P], src[:, t, k * P:(k + 1) * P], ident)
                    filled(job, ins)

            def linear(n, name, xt, h, l, w, bias):
                for k in range(KD):
                    read_out(f"{xt}k{k}", n)
                for q in range(2):
                    job = f"{name}g{q}"
                    free(job, n)
                    for i in range(2):
                        t = 2 * q + i
                        o = ps[BANK[job]][:, i * D:(i + 1) * D]
                        mm(o, ones_r[:, 0:P], brow[:, B0[bias]:B0[bias] + D], start=True, stop=False)
                        for k in range(KD):
                            cols = slice(t * P, (t + 1) * P)
                            ins = mm3(o, (h[:, k, cols], l[:, k, cols]), W(w, k * D, D), False, k == KD - 1)
                    filled(job, ins)

            def conv(n, s, name, tname, h, l, loops):
                for q in range(2):
                    job = f"{name}g{q}"
                    read_out(f"{tname}g{q}", n)
                    if not loops:
                        read_out(f"ATg{q}", n)
                    free(job, n)
                    for i in range(2):
                        o = ps[BANK[job]][:, i * D:(i + 1) * D]
                        for jb in range(2):
                            cols = slice(i * P, (i + 1) * P)
                            ins = mm3(o, (ATh[s][:, q, jb, cols], ATl[s][:, q, jb, cols]), (h[:, 2 * q + jb, :], l[:, 2 * q + jb, :]),
                                      jb == 0, jb == 1 and not loops)
                        if loops:
                            mm(o, id_r[:, :], h[:, 2 * q + i, :], start=False, stop=False)
                            ins = mm(o, id_r[:, :], l[:, 2 * q + i, :], start=False, stop=True)
                    filled(job, ins)

            def dense(n, job, weights, rights, bias):
                free(job, n)
                o = ps[BANK[job]][:, :]
                if bias is not None:
                    mm(o, brow[:, bias:bias + P], ones_r[:, :], start=True, stop=False)
                for k, (w, x_) in enumerate(zip(weights, rights)):
                    ins = mm3(o, w, x_, bias is None and k == 0, k == len(weights) - 1)
                filled(job, ins)

            def layer0(j, s):
                n = j * 2 + s
                pe.wait_ge(xn_ready["0"], val(n, 1, 1))
                transposes(n, "xT0", xn, None)
                pe.wait_ge(adj_loaded[s], val(j, 16, 16))
                for q in range(2):
                    job = f"ATg{q}"
                    free(job, n)
                    for jb in range(2):
                        for i in range(2):
                            ins = turn(ps[BANK[job]][:, jb * N + i * P:jb * N + (i + 1) * P], adj[s][:, 2 * q + i, jb * P:(jb + 1) * P], ident)
                    filled(job, ins)
                linear(n, "T0", "xT0", xTh, xTl, "g0", "g0")
                conv(n, s, "M0", "T0", Th, Tl, False)
                pe.wait_ge(xn_ready["1"], val(n, 1, 1))
                transposes(n, "xT1", xn, None)
                xT = [(xTh[:, k, :], xTl[:, k, :]) for k in range(KD)]
                for k in range(KD):
                    read_out(f"xT1k{k}", n)
                job = "GL"
                free(job, n)
                for t in range(T):
                    for k in range(KD):
                        cols = slice(t * P, (t + 1) * P)
                        ins = mm3(ps[BANK[job]][:, t * E0:(t + 1) * E0], (xTh[:, k, cols], xTl[:, k, cols]), W("gW", k * E0, E0), k == 0, k == KD - 1)
                filled(job, ins)
                for m in range(2):
                    dense(n, f"S1m{m}", [W("sW1", k * D + m * P, P) for k in range(KD)], xT, B0["sb1"] + m * P)
                for m in range(2):
                    read_out(f"S1m{m}", n)
                H = [(hh[:, m, :], hl[:, m, :]) for m in range(4)]
                dense(n, "S2", [W("sW2", k * P, P) for k in range(KD)], H[0:2], B0["sb2"])
                for b in range(2):
                    for i in range(2):
                        e = 2 * b + i
                        dense(n, f"E1e{e}", [W("eW1", e * D + k * EH1, EH1) for k in range(KD)], xT, B0["eb1"] + e * EH1)
                    for i in range(2):
                        read_out(f"E1e{2 * b + i}", n)
                    dense(n, f"EP{b}", [W("eW2", (2 * b + i) * P, P) for i in range(2)], [H[(2 * (b + 1) + i) % 4] for i in range(2)], None)
                job = "CBT"
                pe.wait_ge(cb_ready, val(n, 1, 1))
                free(job, n)
                for t in range(T):
                    ins = turn(ps[BANK[job]][0:16, t * P:(t + 1) * P], cb[:, t, :].bitcast(fp32), ident)
                filled(job, ins)
                read_out("CBT", n)
                for b in range(2):
                    job = f"G{b}"
                    free(job, n)
                    filled(job, mm(ps[BANK[job]][:, :], sel_r[:, b * P:(b + 1) * P], cbT[:, :], start=True, stop=True))
                read_out("S2", n)
                pe.wait_ge(gl_ready, val(n, 2, 2))
                for q in range(2):
                    job = f"O1g{q}"
                    free(job, n)
                    for i in range(2):
                        cols = slice((2 * q + i) * P, (2 * q + i + 1) * P)
                        o = ps[BANK[job]][:, i * D:(i + 1) * D]
                        mm(o, cbT[:, cols], o_bias[:, :], start=True, stop=False)
                        mm3(o, (s2h[:, cols], s2l[:, cols]), W("sW3", 0, D), False, False)
                        for b in range(2):
                            ins = mm3(o, (gh[:, b, cols], gl[:, b, cols]), W("eW3", b * D, D), False, b == 1)
                    filled(job, ins)

            def layer1(j, s):
                n = j * 2 + s
                pe.wait_ge(xn_ready["2"], val(n, 1, 1))
                transposes(n, "xT2", xnY, None)
                linear(n, "T1", "xT2", xThY, xTlY, "g1", "g1")
                conv(n, s, "M1", "T1", ThY, TlY, True)
                pe.wait_ge(xn_ready["3"], val(n, 1, 1))
                transposes(n, "xT3", pay[s], None)
                for k in range(KD):
                    read_out(f"xT3k{k}", n)
                job = "RL"
                free(job, n)
                for t in range(T):
                    for k in range(KD):
                        ins = mm(ps[BANK[job]][:, t * E1:(t + 1) * E1], xT3[:, k, t * P:(t + 1) * P], rW[:, k, :], start=(k == 0), stop=(k == KD - 1))
                filled(job, ins)
                job = "POS"
                pe.wait_ge(mask_ready, val(n, 1, 1))
                free(job, n)
                for t in range(T):
                    o = ps[BANK[job]][:, t * E1:(t + 1) * E1]
                    for u in range(t):
                        mm(o, ones_b[:, :], mb[:, u, :], start=(u == 0), stop=False)
                    mm(o, tri_b[:, :], mb[:, t, :], start=(t == 0), stop=True)
                for t in range(T):
                    ins = mm(ps[BANK[job]][:, T * E1:(T + 1) * E1], ones_b[:, :], mb[:, t, :], start=(t == 0), stop=(t == T - 1))
                filled(job, ins)

            pe.wait_ge(misc, 16)
            pe.wait_ge(mask_loaded, 16)
            turn(ps[0][:, 0:P], mask_rows[:, :], ident).then_inc(mask_turned, 1)
            pe.wait_ge(w_ready, 3)

            def body(j, s):
                layer0(j, s)
                layer1(j, s)
            over_pairs(pe, body)

            pe.wait_ge(table_ready, 1)
            pe.wait_ge(mw_ready, 8)
            with pe.Fori(0, TILES // SL) as j:
                experts = []
                for s in range(SL):
                    pe.wait_ge(g_loaded[s], j * 16 + 16)
                    for k in range(KD):
                        ins = turn(ps[2 * s][:, k * P:(k + 1) * P], g[s][:, k * P:(k + 1) * P], ident)
                    ins.then_inc(pe_c[s], 1)
                for s in range(SL):
                    experts.append(pe.value_load(tab_i[0:1, bass.ds(j * SL + (NJ + s), 1)], min_val=0, max_val=E1 - 1))

                def product(s, w, h, l):
                    e = experts[s]
                    o = ps[2 * s + 1][:, 0:D]
                    mm(o, ones_r[:, 0:P], b1r[:, bass.ds(e * D + w * E1 * D, D)], start=True, stop=False)
                    for k in range(KD):
                        cols = slice(k * P, (k + 1) * P)
                        c = bass.ds(e * WC + (w * KD + k) * D, D)
                        ins = mm3(o, (h[s][:, cols], l[s][:, cols]), (w1h[:, c], w1l[:, c]), False, k == KD - 1)
                    ins.then_inc(pe_c[s], 1)

                for s in range(SL):
                    pe.wait_ge(gT_lo[s], j + 1)
                    pe.wait_ge(y_ready[s], j + 1)
                    product(s, 0, gTh, gTl)
                for s in range(SL):
                    pe.wait_ge(hf_ready[s], j + 1)
                    for k in range(KD):
                        ins = turn(ps[2 * s][:, k * P:(k + 1) * P], hf[s][:, k * P:(k + 1) * P], ident)
                    ins.then_inc(pe_c[s], 1)
                for s in range(SL):
                    pe.wait_ge(hT_lo[s], j + 1)
                    product(s, 1, hTh, hTl)


def kernel(x, adj, nodemask, L0_gnn_W, L0_gnn_b, L0_ffn_sW1, L0_ffn_sb1, L0_ffn_sW2, L0_ffn_sb2, L0_ffn_sW3, L0_ffn_sb3,
           L0_ffn_eW1, L0_ffn_eb1, L0_ffn_eW2, L0_ffn_eb2, L0_ffn_eW3, L0_ffn_eb3, L0_ffn_gW, L0_ffn_gb, L1_gnn_W, L1_gnn_b,
           L1_ffn_router_w, L1_ffn_w1, L1_ffn_b1, L1_ffn_w2, L1_ffn_b2):
    import concourse.bacc as bacc
    from concourse.bass_utils import run_bass_kernel_spmd

    lay = lambda v: np.ascontiguousarray(np.asarray(v))
    arrays = {
        "x": lay(x).reshape(TOK, D), "adj": lay(adj).reshape(TOK, N), "nodemask": lay(nodemask).reshape(P, P),
        "g0W": lay(np.asarray(L0_gnn_W).T), "g0b": lay(L0_gnn_b), "g1W": lay(np.asarray(L1_gnn_W).T), "g1b": lay(L1_gnn_b),
        "sW1": lay(L0_ffn_sW1), "sb1": lay(L0_ffn_sb1), "sW2": lay(L0_ffn_sW2), "sb2": lay(L0_ffn_sb2),
        "sW3": lay(L0_ffn_sW3), "sb3": lay(L0_ffn_sb3), "eW1": lay(L0_ffn_eW1), "eb1": lay(L0_ffn_eb1),
        "eW2": lay(L0_ffn_eW2), "eb2": lay(L0_ffn_eb2), "eW3": lay(L0_ffn_eW3), "eb3": lay(L0_ffn_eb3),
        "gW": lay(L0_ffn_gW), "gb": lay(L0_ffn_gb), "rW": lay(np.asarray(L1_ffn_router_w).T),
        "w1": lay(L1_ffn_w1), "b1": lay(L1_ffn_b1), "w2": lay(L1_ffn_w2), "b2": lay(L1_ffn_b2),
        "consts": constants(),
    }
    nc = bacc.Bacc("TRN2", target_bir_lowering=False, num_devices=1)
    a = {n: nc.dram_tensor("in_" + n, v.shape, mybir.dt.from_np(v.dtype), kind="ExternalInput").ap() for n, v in arrays.items()}
    out = nc.dram_tensor("out", (TOK, D), fp32, kind="ExternalOutput").ap()
    build(nc, a, out)
    res = run_bass_kernel_spmd(nc, [{"in_" + n: v for n, v in arrays.items()}], core_ids=[0])
    return res.results[0]["out"].reshape(GRAPHS, N, D)
```

```python
from contextlib import ExitStack

import numpy as np

import concourse.bass as bass
from concourse import mybir

fp32 = mybir.dt.float32
f32r = mybir.dt.float32r
bf16 = mybir.dt.bfloat16
i32 = mybir.dt.int32
ALU = mybir.AluOpType
ACT = mybir.ActivationFunctionType
AX = mybir.AxisListType

P = 128
GRAPHS, N, D = 64, 256, 256
TOK = GRAPHS * N
T = 4
PT = T * P
PAIRS = GRAPHS // 2
RING = 4
KD = D // P
E0, E1 = 4, 8
EH1, EH2 = 128, 64
LN_EPS, DEG_EPS = 1e-5, 1e-8
KEY_FLOOR = -88.0
ROW = D + 2 * E1
CAP = TOK + P
TILES = 2 * TOK // P + E1
SKIP = 1 << 16
NJ = TILES

C_ID, C_TRI, C_SEL, C_MH, C_ML = 0, 128, 256, 512, 513
C_REV8, C_REV4, C_ECAP, C_TOK2, C_J, C_PAD = 514, 522, 526, 534, 538, 538 + NJ
C_ALL = C_PAD + ROW


def constants():
    c = np.zeros((P, C_ALL), np.float32)
    p = np.arange(P)
    c[:, C_ID:C_ID + P] = np.eye(P)
    c[:, C_TRI:C_TRI + P] = p[:, None] < p[None, :]
    for b in range(2):
        for m in range(P):
            e = 2 * b + m // EH2
            c[e, C_SEL + b * P + m] = 1.0
            c[8 + e, C_SEL + b * P + m] = 1.0
    c[[0, 1, 2, 3, 8, 9, 10, 11, 12], C_MH] = 1.0
    c[[4, 5, 6, 7, 13], C_ML] = 1.0
    c[:, C_REV8:C_REV8 + E1] = E1 - np.arange(E1)
    c[:, C_REV4:C_REV4 + E0] = E0 - np.arange(E0)
    c[:, C_ECAP:C_ECAP + E1] = CAP * np.arange(E1)
    c[:, C_TOK2:C_TOK2 + T] = 2 * (P * np.arange(T)[None, :] + p[:, None])
    c[:, C_J:C_J + NJ] = P * np.arange(NJ)
    c[:, C_PAD + D + E1:C_PAD + ROW] = SKIP
    return c


JOBS = [
    ("xT0k0", 0), ("xT0k1", 1), ("ATg0", 0), ("ATg1", 1), ("T0g0", 0), ("T0g1", 1), ("M0g0", 0), ("M0g1", 1),
    ("xT1k0", 2), ("xT1k1", 3), ("GL", 7), ("S1m0", 2), ("S1m1", 3), ("S2", 7), ("E1e0", 2), ("E1e1", 3),
    ("EP0", 7), ("E1e2", 2), ("E1e3", 3), ("EP1", 7), ("CBT", 7), ("G0", 2), ("G1", 3), ("O1g0", 7), ("O1g1", 2),
    ("xT2k0", 4), ("xT2k1", 5), ("T1g0", 4), ("T1g1", 5), ("M1g0", 4), ("M1g1", 5),
    ("xT3k0", 6), ("xT3k1", 6), ("RL", 6), ("POS", 6),
]
SPLIT = {j for j, _ in JOBS if j[:2] in ("xT", "AT", "T0", "T1", "S1", "S2", "E1") and not j.startswith("xT3")}
BANK, USE, HI_USE, USES, HI_USES = {}, {}, {}, [0] * 8, [0] * 8
for _j, _b in JOBS:
    USES[_b] += 1
    BANK[_j], USE[_j] = _b, USES[_b]
    if _j in SPLIT:
        HI_USES[_b] += 1
        HI_USE[_j] = HI_USES[_b]

W0 = {}
_at = 0
for _n, _c in [("g0", KD * D), ("g1", KD * D), ("sW1", KD * D), ("eW1", E0 * KD * EH1), ("sW2", KD * P), ("eW2", E0 * P),
               ("sW3", D), ("eW3", 2 * D), ("gW", KD * E0)]:
    W0[_n] = (_at, _c)
    _at += _c
W0_COLS = _at
B0 = {"g0": 0, "g1": D, "sb1": 2 * D, "eb1": 3 * D, "sb2": 3 * D + E0 * EH1}
B0_COLS = 3 * D + E0 * EH1 + P
LOW_ROW = 32


def build(nc, a, out):
    xres = nc.dram_tensor("xres", (TOK, D), fp32, kind="Internal").ap()
    routed = nc.dram_tensor("routed", (E1 * CAP + E1 * P, ROW), fp32, kind="Internal").ap()
    back = nc.dram_tensor("back", (2 * TOK, D), fp32, kind="Internal").ap()

    ctx = ExitStack()
    with ctx:
        def sem(name):
            return ctx.enter_context(nc.semaphore(name))

        def keep(name, shape, dt=fp32, stack=ctx):
            return stack.enter_context(nc.sbuf_tensor(name, shape, dt))

        cst = keep("cst", [P, C_ALL])
        ones_r = keep("ones_r", [P, PT], f32r)
        id_r = keep("id_r", [P, P], f32r)
        sel_r = keep("sel_r", [P, 2 * P], f32r)
        tri_b = keep("tri_b", [P, P], bf16)
        ones_b = keep("ones_b", [P, P], bf16)
        w0h = keep("w0h", [P, W0_COLS], f32r)
        w0l = keep("w0l", [P, W0_COLS], f32r)
        brow = keep("brow", [P, B0_COLS], f32r)
        o_bias = keep("o_bias", [P, D], f32r)
        eb2 = keep("eb2", [P, 2])
        rW = keep("rW", [P, KD, E1])
        gb = keep("gb", [P, E0])
        base = keep("base", [P, E1])
        tok2 = keep("tok2", [P, T])
        minus_half = keep("minus_half", [P, 16])
        mask_rows = keep("mask_rows", [P, P])
        mask_cols = keep("mask_cols", [P, P])
        idx_credit = keep("idx_credit", [P, 4 + 8])
        cnt_i = keep("cnt_i", [P, 4 * E1], i32)
        cnt_f = keep("cnt_f", [P, 4 * E1])

        stage_stack = ExitStack()
        stage = keep("stage", [P, W0_COLS], fp32, stage_stack)
        bstage = keep("bstage", [P, B0_COLS], fp32, stage_stack)
        btmp = keep("btmp", [P, B0_COLS], f32r, stage_stack)
        ostage = keep("ostage", [16, D], fp32, stage_stack)
        ohi = keep("ohi", [16, D], f32r, stage_stack)
        olo = keep("olo", [16, D], f32r, stage_stack)
        otmp = keep("otmp", [16, D], fp32, stage_stack)
        stage_stack.close()
        A = ExitStack()

        def ka(name, shape, dt=fp32):
            return keep(name, shape, dt, A)

        xnY = ka("xnY", [P, T, D])
        xThY, xTlY = ka("xThY", [P, KD, PT], f32r), ka("xTlY", [P, KD, PT], f32r)
        ThY, TlY = ka("ThY", [P, T, D], f32r), ka("TlY", [P, T, D], f32r)
        xT3 = ka("xT3", [P, KD, PT])
        xo = ka("xo", [P, T, D])
        pay = [ka(f"pay_{s}", [P, T, ROW]) for s in range(2)]
        x = [ka(f"x_{s}", [P, T, D]) for s in range(RING)]
        adj = [ka(f"adj_{s}", [P, T, N]) for s in range(2)]
        ATh = [ka(f"ATh_{s}", [P, 2, 2, N], f32r) for s in range(RING)]
        ATl = [ka(f"ATl_{s}", [P, 2, 2, N], f32r) for s in range(RING)]
        junk = ka("junk", [P, T, N], bf16)
        xnA = ka("xnA", [P, T, D])
        xThA, xTlA = ka("xThA", [P, KD, PT], f32r), ka("xTlA", [P, KD, PT], f32r)
        ThA, TlA = ka("ThA", [P, T, D], f32r), ka("TlA", [P, T, D], f32r)
        xnB = ka("xnB", [P, T, D])
        xThB, xTlB = ka("xThB", [P, KD, PT], f32r), ka("xTlB", [P, KD, PT], f32r)
        hh, hl = ka("hh", [P, 4, PT], f32r), ka("hl", [P, 4, PT], f32r)
        gh, gl = hh[:, 2:4, :], hl[:, 2:4, :]
        s2h, s2l = ka("s2h", [P, PT], f32r), ka("s2l", [P, PT], f32r)
        ef = ka("ef", [P, 2, PT])
        cbT = ka("cbT", [P, PT], f32r)
        cb = ka("cb", [P, T, 16], f32r)
        st = {q: ka("st" + q, [P, T, 6]) for q in "0123"}
        mv = {q: ka("mv" + q, [P, T, 2]) for q in "0123"}
        vp = {q: ka("vp" + q, [P, 16]) for q in "0123"}
        rs = {q: ka("rs" + q, [P, 16]) for q in "0123"}
        deg, dz, nz = ka("deg", [P, T]), ka("dz", [P, T]), ka("nz", [P, T])
        dsc = [ka(f"dsc_{s}", [P, 3, T]) for s in range(RING)]
        ch = {n: ka("ch_" + n, [P, 2 * T, E1]) for n in ("lg", "key", "ex", "pr", "r1", "oh1", "r2", "oh2", "msk", "w", "c")}
        cs = {n: ka("cs_" + n, [P, 2 * T]) for n in ("m", "s", "rs", "a", "b", "m2", "s2", "rs2")}
        rt = {n: ka("rt_" + n, [P, T, E1]) for n in ("pos", "q1", "q2")}
        mb = ka("mb", [P, T, E1], bf16)
        idx_f = ka("idx_f", [P, 2, T])
        idx = [ka(f"idx_{s}", [P, 2, T], i32) for s in range(2)]
        A.close()

        C = ExitStack()
        tab_i = keep("tab_i", [P, 2 * NJ], i32, C)
        tab_f = keep("tab_f", [P, 3 * NJ], fp32, C)

        def kc(name, shape, dt=fp32):
            return keep(name, shape, dt, C)

        WC = 2 * KD * D
        w1h, w1l = kc("w1h", [P, E1 * WC], f32r), kc("w1l", [P, E1 * WC], f32r)
        b1r = kc("b1r", [P, 2 * E1 * D], f32r)
        SL = 4
        g = [kc(f"g_{s}", [P, ROW]) for s in range(SL)]
        gTh = [kc(f"gTh_{s}", [P, D], f32r) for s in range(SL)]
        gTl = [kc(f"gTl_{s}", [P, D], f32r) for s in range(SL)]
        hf = [kc(f"hf_{s}", [P, D]) for s in range(SL)]
        hTh = [kc(f"hTh_{s}", [P, D], f32r) for s in range(SL)]
        hTl = [kc(f"hTl_{s}", [P, D], f32r) for s in range(SL)]
        ysb = [kc(f"ysb_{s}", [P, D]) for s in range(SL)]
        wsel = [kc(f"wsel_{s}", [P, 2]) for s in range(SL)]
        isel = [kc(f"isel_{s}", [P, 2], i32) for s in range(SL)]
        mstage = kc("mstage", [P, E1 * WC // 4])
        mbst = kc("mbst", [P, 2 * E1 * D])
        mbtmp = kc("mbtmp", [P, 2 * E1 * D], f32r)
        C.close()
        Dk = ExitStack()
        dx = [keep(f"dx_{s}", [P, T, D], fp32, Dk) for s in range(2)]
        dy = [keep(f"dy_{s}", [P, T, 2 * D], fp32, Dk) for s in range(2)]
        dt_ = [keep(f"dt_{s}", [P, T, D], fp32, Dk) for s in range(2)]
        do = [keep(f"do_{s}", [P, T, D], fp32, Dk) for s in range(2)]
        Dk.close()

        ps = [ctx.enter_context(nc.psum_tensor(f"bank{b}", [P, 512], fp32)) for b in range(8)]

        bank_full = [sem(f"bank_full{b}") for b in range(8)]
        hi_done = [sem(f"hi_done{b}") for b in range(8)]
        bank_free = [sem(f"bank_free{b}") for b in range(8)]
        w_loaded, w_ready = sem("w_loaded"), sem("w_ready")
        bias_loaded, o_copied = sem("bias_loaded"), sem("o_copied")
        misc = sem("setup_steps")
        x_loaded, adj_loaded = [sem(f"x_loaded{s}") for s in range(RING)], [sem(f"adj_loaded{s}") for s in range(2)]
        deg_ready = sem("deg_ready")
        var_ready = {q: sem("var_ready" + q) for q in "0123"}
        rstd_ready = {q: sem("rstd_ready" + q) for q in "0123"}
        xn_ready = {q: sem("xn_ready" + q) for q in "0123"}
        nb_steps = sem("power_steps")
        scale_ready = sem("scale_ready")
        x1_ready, x3_ready, x3_summed = sem("x1_ready"), sem("x3_ready"), sem("x3_summed")
        shift_ready, exp_ready, diff_ready, exp2_ready, cb_ready = (sem(s) for s in ("shift_ready", "exp_ready", "diff_ready", "exp2_ready", "cb_ready"))
        gh_ready, gl_ready = sem("gh_ready"), sem("gl_ready")
        mask_ready, idx_ready = sem("mask_ready"), sem("idx_ready")
        choice_steps, dz_ready = sem("choice_steps"), sem("dz_ready")
        pow_ready = {q: sem("pow_ready" + q) for q in "0123"}
        st_ready, mv_ready = {q: sem("st_ready" + q) for q in "0123"}, {q: sem("mv_ready" + q) for q in "0123"}
        scattered = [sem(f"scattered{s}") for s in range(2)]
        x3_stored = sem("x3_stored")

        counts_ready, padded, table_ready = sem("counts_ready"), sem("padded"), sem("table_ready")
        m_loaded, mw_loaded, mw_ready = sem("m_loaded"), sem("mw_loaded"), sem("mw_ready")
        slot_used = [sem(f"slot_used{s}") for s in range(SL)]
        g_loaded = [sem(f"g_loaded{s}") for s in range(SL)]
        returned = [sem(f"returned{s}") for s in range(SL)]
        gT_hi, gT_lo = [sem(f"gT_hi{s}") for s in range(SL)], [sem(f"gT_lo{s}") for s in range(SL)]
        hf_ready = [sem(f"hf_ready{s}") for s in range(SL)]
        hT_hi, hT_lo = [sem(f"hT_hi{s}") for s in range(SL)], [sem(f"hT_lo{s}") for s in range(SL)]
        y_ready = [sem(f"y_ready{s}") for s in range(SL)]
        pe_c = [sem(f"tile_products{s}") for s in range(SL)]
        sel_ready = [sem(f"sel_ready{s}") for s in range(SL)]
        c_done = sem("c_done")
        dx_loaded, dy_loaded = [sem(f"dx_loaded{s}") for s in range(2)], [sem(f"dy_loaded{s}") for s in range(2)]
        d_added, d_stored = [sem(f"d_added{s}") for s in range(2)], [sem(f"d_stored{s}") for s in range(2)]

        dve_setup, act_steps, a_done, m_clear, b_steps, mb_steps = (sem(n) for n in ("dve_setup", "act_steps", "a_done", "m_clear", "b_steps", "mb_steps"))
        mask_turned, mask_loaded, held = sem("mask_turned"), sem("mask_loaded"), sem("held")

        block = ctx.enter_context(nc.Block())

        def val(n, per, k):
            turn, a_turn, first = n
            return first * per + k if a_turn == 0 else turn * (a_turn * per) + (first * per + k)

        def ago(n, d):
            return n[0], n[1], n[2] - d

        def slot(n, ring=RING):
            return n[2] % ring

        def rows_of(n, per, count):
            return bass.ds(val(n, per, 0), count)

        def w0(half, name, lo, cols):
            c0, _ = W0[name]
            return (w0h, w0l)[half][:, c0 + lo:c0 + lo + cols]

        def b3(ap, n):
            return ap.unsqueeze(2).to_broadcast([P, T, n])

        def hold(eng):
            eng.sem_inc(held, 1)

        STEPS = PAIRS + RING - 1
        FIRST = RING
        TURNS = (PAIRS - 1 - FIRST) // RING

        def over_steps(eng, step):
            for k in range(FIRST):
                step((None, 0, k))
            with eng.Fori(0, TURNS) as j:
                for u in range(RING):
                    step((j, RING, FIRST + u))
            for k in range(FIRST + TURNS * RING, STEPS):
                step((None, 0, k))

        def adj_value(n):
            return 16 * (n[2] // 2) + 16 if n[1] == 0 else n[0] * (16 * n[1] // 2) + 16 * (n[2] // 2) + 16

        def x_value(n):
            return 16 * (n[2] // RING) + 16 if n[1] == 0 else n[0] * 16 + 16 * (n[2] // RING) + 16

        def scatter_value(n):
            each = 2 * T * 16
            return each * (n[2] // 2) + each if n[1] == 0 else n[0] * (each * n[1] // 2) + each * (n[2] // 2) + each

        def active(n):
            return n[1] != 0 or 0 <= n[2] < PAIRS

        def starts(n):
            return n[2] + 1 < PAIRS if n[1] == 0 else True

        @block.sync
        def _(sp):
            sp.dma_start(cst[:, :], a["consts"]).then_inc(misc, 16)
            sp.dma_start(mask_rows[:, :], a["nodemask"]).then_inc(mask_loaded, 16)
            col = lambda name: stage[:, W0[name][0]:W0[name][0] + W0[name][1]]
            kp = lambda ap: ap.rearrange("(k p) n -> p k n", p=P)
            k2 = lambda ap, k: ap.rearrange("p (k n) -> p k n", k=k)
            sp.wait_ge(w_ready, 1)
            sp.dma_start(k2(col("g0"), KD), kp(a["g0W"])).then_inc(w_loaded, 16)
            sp.dma_start(k2(col("g1"), KD), kp(a["g1W"])).then_inc(w_loaded, 16)
            sp.dma_start(k2(col("sW1"), KD), kp(a["sW1"])).then_inc(w_loaded, 16)
            sp.dma_start(k2(col("sW2"), KD), kp(a["sW2"])).then_inc(w_loaded, 16)
            sp.dma_start(col("sW3"), a["sW3"]).then_inc(w_loaded, 16)
            sp.dma_start(k2(col("eW3"), 2), a["eW3"].rearrange("(b e) g o -> (e g) b o", b=2)).then_inc(w_loaded, 16)
            sp.dma_start(k2(col("gW"), KD), kp(a["gW"])).then_inc(w_loaded, 16)
            for e in range(E0):
                sp.dma_start(k2(col("eW1")[:, e * D:(e + 1) * D], KD), kp(a["eW1"][e])).then_inc(w_loaded, 16)
                c0 = e * P + (e % 2) * EH2
                sp.dma_start(col("eW2")[:, c0:c0 + EH2], a["eW2"][e]).then_inc(w_loaded, 16)
            sp.dma_start(rW[:, :, :], kp(a["rW"])).then_inc(w_loaded, 16)
            for row in (0, LOW_ROW):
                for name, src in (("g0", a["g0b"]), ("g1", a["g1b"]), ("sb1", a["sb1"]), ("eb1", a["eb1"]), ("sb2", a["sb2"])):
                    flat = src if len(src.shape) == 1 else src.rearrange("e n -> (e n)")
                    n = flat.shape[0]
                    sp.dma_start(bstage[row:row + 1, B0[name]:B0[name] + n], flat.rearrange("(a n) -> a n", a=1)).then_inc(bias_loaded, 16)
            for r0 in (0, 4, 8):
                sp.dma_start(ostage[r0:r0 + 4, :], a["eb3"]).then_inc(bias_loaded, 16)
            for r0 in (12, 13):
                sp.dma_start(ostage[r0:r0 + 1, :], a["sb3"].rearrange("(a n) -> a n", a=1)).then_inc(bias_loaded, 16)
            for b in range(2):
                sp.dma_start(eb2[:, b:b + 1], a["eb2"].rearrange("e (g a) -> (e g) a", a=1)[b * P:(b + 1) * P, :]).then_inc(bias_loaded, 16)
            sp.dma_start(gb[:, :], a["gb"].rearrange("(a n) -> a n", a=1).to_broadcast([P, E0])).then_inc(bias_loaded, 16)

            def load(n):
                rows = rows_of(n, PT, PT)
                sp.dma_start(x[slot(n)][:, :, :], a["x"][rows, :].rearrange("(t p) f -> p t f", p=P)).then_inc(x_loaded[slot(n)], 16)

            def load_adj(n):
                rows = rows_of(n, PT, PT)
                sp.dma_start(adj[slot(n, 2)][:, :, :], a["adj"][rows, :].rearrange("(t p) f -> p t f", p=P)).then_inc(adj_loaded[slot(n, 2)], 16)

            load((None, 0, 0))
            load_adj((None, 0, 0))

            def step(k):
                d, nxt = ago(k, 3), ago(k, -1)
                if starts(k):
                    if k[1] != 0 or k[2] >= 1:
                        sp.wait_ge(bank_full[BANK["ATg1"]], val(ago(k, 1), USES[BANK["ATg1"]], USE["ATg1"]))
                        hold(sp)
                        sp.wait_ge(deg_ready, val(ago(k, 1), 1, 1))
                        hold(sp)
                    load_adj(nxt)
                if active(d):
                    sp.wait_ge(x3_summed, val(d, 1, 1))
                    hold(sp)
                    sp.dma_start(xres[rows_of(d, PT, PT), :].rearrange("(t p) f -> p t f", p=P), xo[:, :, :]).then_inc(x3_stored, 16)
                if starts(k):
                    load(nxt)

            over_steps(sp, step)

            for s in range(2):
                sp.wait_ge(scattered[s], (PAIRS // 2 + 1) * 2 * T * 16)
            sp.wait_ge(x3_stored, (PAIRS + 1) * 16)
            sp.sem_inc(a_done, 1)
            sp.wait_ge(counts_ready, 1)
            for e in range(E1):
                row = sp.value_load(cnt_i[0:1, e:e + 1], min_val=0, max_val=E1 * CAP)
                sp.dma_start(routed[bass.ds(row, P), :], cst[:, C_PAD:C_PAD + ROW]).then_inc(padded, 16)
            for e in range(E1):
                sp.dma_start(routed[E1 * CAP + e * P:E1 * CAP + (e + 1) * P, :], cst[:, C_PAD:C_PAD + ROW]).then_inc(padded, 16)
            sp.wait_ge(padded, 2 * E1 * 16)

            sp.wait_ge(table_ready, 1)
            with sp.Fori(0, TILES // SL) as j:
                for s in range(SL):
                    sp.wait_ge(slot_used[s], j + 1)
                    hold(sp)
                    row = sp.value_load(tab_i[0:1, bass.ds(j * SL + s, 1)], min_val=0, max_val=E1 * CAP + (E1 - 1) * P)
                    sp.dma_start(g[s][:, :], routed[bass.ds(row, P), :]).then_inc(g_loaded[s], 16)

            for s in range(SL):
                sp.wait_ge(returned[s], (TILES // SL + 1) * 16)

            def load_d(j, s, ahead):
                rows = bass.ds(j * (2 * PT) + (ahead + s) * PT, PT)
                sp.dma_start(dx[s][:, :, :], xres[rows, :].rearrange("(t p) f -> p t f", p=P)).then_inc(dx_loaded[s], 16)
                rows2 = bass.ds(j * (4 * PT) + (ahead + s) * 2 * PT, 2 * PT)
                sp.dma_start(dy[s][:, :, :].rearrange("p t (k f) -> p t k f", k=2),
                             back[rows2, :].rearrange("(t p k) f -> p t k f", p=P, k=2)).then_inc(dy_loaded[s], 16)

            for s in range(2):
                load_d(0, s, 0)
            with sp.Fori(0, PAIRS // 2 - 1) as j:
                for s in range(2):
                    sp.wait_ge(d_added[s], j * 2 + 2)
                    hold(sp)
                    load_d(j, s, 2)
            for s in range(2):
                sp.wait_ge(d_stored[s], (PAIRS // 2 + 1) * 16)

        @block.scalar
        def _(act):
            def freed(job, n, ins):
                ins.then_inc(bank_free[BANK[job]], 1)

            def full(job, n):
                act.wait_ge(bank_full[BANK[job]], val(n, USES[BANK[job]], USE[job]))

            def high(job, n, dst, func=ACT.Copy):
                full(job, n)
                nc.scalar.activation(dst, ps[BANK[job]][:, :], func).then_inc(hi_done[BANK[job]], 1)

            def high_scaled(job, n, dst, gph, d):
                full(job, n)
                for i in range(2):
                    t = 2 * gph + i
                    ins = nc.scalar.activation(dst[:, t, :], ps[BANK[job]][:, i * D:(i + 1) * D], ACT.Copy, scale=d[:, t:t + 1])
                ins.then_inc(hi_done[BANK[job]], 1)

            def expert_out(i, n):
                job = f"EP{i}"
                full(job, n)
                nc.scalar.activation(ef[:, i, :], ps[BANK[job]][:, :], ACT.Relu, bias=eb2[:, i:i + 1]).then_inc(bank_free[BANK[job]], 1)

            def conv_out(job, n, dst, gph, d):
                full(job, n)
                for i in range(2):
                    t = 2 * gph + i
                    ins = nc.scalar.activation(dst[:, t, :], ps[BANK[job]][:, i * D:(i + 1) * D], ACT.Relu, scale=d[:, t:t + 1])
                ins.then_inc(bank_free[BANK[job]], 1)

            def norm(n, q, src, dst):
                act.wait_ge(rstd_ready[q], val(n, 1, 1))
                for t in range(T):
                    ins = nc.scalar.activation(dst[:, t, 0:D], src[:, t, :], ACT.Identity, scale=rs[q][:, t:t + 1], bias=rs[q][:, 12 + t:13 + t])
                ins.then_inc(xn_ready[q], 1)

            def degrees(n):
                act.wait_ge(adj_loaded[slot(n, 2)], adj_value(n))
                for t in range(T):
                    ins = nc.scalar.activation(junk[:, t, :], adj[slot(n, 2)][:, t, :], ACT.Copy, accum_out=deg[:, t:t + 1])
                ins.then_inc(deg_ready, 1)

            def lead(n):
                for i in range(KD):
                    high(f"xT0k{i}", n, xThA[:, i, :])
                for q in range(2):
                    high(f"ATg{q}", n, ATh[slot(n)][:, q, :, :].rearrange("p a b -> p (a b)"))

            def router_in(n, i):
                job = f"xT3k{i}"
                full(job, n)
                nc.scalar.activation(xT3[:, i, :], ps[BANK[job]][:, :], ACT.Copy).then_inc(bank_free[BANK[job]], 1)

            def step(k):
                a, b, c, d, nxt = k, ago(k, 1), ago(k, 2), ago(k, 3), ago(k, -1)
                A, B, C_, D_ = active(a), active(b), active(c), active(d)
                if k[1] == 0 and k[2] == 0:
                    degrees(a)
                    act.wait_ge(x_loaded[0], 16)
                    norm(a, "0", x[0], xnA)
                    lead(a)
                if B:
                    for i in range(KD):
                        high(f"xT1k{i}", b, xThB[:, i, :])
                if D_:
                    router_in(d, 0)
                if A:
                    act.wait_ge(scale_ready, val(a, 1, 1))
                    for q in range(2):
                        high_scaled(f"T0g{q}", a, ThA, q, dsc[slot(a)][:, 0, :])
                if D_:
                    router_in(d, 1)
                if C_:
                    norm(c, "2", x[slot(c)], xnY)
                if B:
                    for m in range(2):
                        high(f"S1m{m}", b, hh[:, m, :], ACT.Relu)
                if B or D_:
                    act.wait_ge(shift_ready, val(b, 1, 1))
                    nc.scalar.activation(ch["ex"][:, :, :], ch["key"][:, :, :], ACT.Exp).then_inc(exp_ready, 1)
                if A:
                    for q in range(2):
                        conv_out(f"M0g{q}", a, xnA, q, dsc[slot(a)][:, 0, :])
                if C_:
                    for i in range(KD):
                        high(f"xT2k{i}", c, xThY[:, i, :])
                if B:
                    for i in range(2):
                        high(f"E1e{i}", b, hh[:, 2 + i, :], ACT.Relu)
                    high("S2", b, s2h[:, :], ACT.Relu)
                if B or D_:
                    act.wait_ge(diff_ready, val(b, 1, 1))
                    nc.scalar.activation(ch["pr"][:, 0:T, :], ch["w"][:, 0:T, :], ACT.Exp).then_inc(exp2_ready, 1)
                if C_:
                    for q in range(2):
                        high_scaled(f"T1g{q}", c, ThY, q, dsc[slot(c)][:, 1, :])
                if B:
                    for i in range(2):
                        high(f"E1e{2 + i}", b, hh[:, i, :], ACT.Relu)
                if starts(k):
                    degrees(nxt)
                if B:
                    expert_out(0, b)
                if A:
                    norm(a, "1", x[slot(a)], xnB)
                if B:
                    expert_out(1, b)
                    full("CBT", b)
                    nc.scalar.activation(cbT[0:16, :], ps[BANK["CBT"]][0:16, :], ACT.Copy).then_inc(bank_free[BANK["CBT"]], 1)
                if starts(k):
                    norm(nxt, "0", x[slot(nxt)], xnA)
                if C_:
                    for q in range(2):
                        conv_out(f"M1g{q}", c, xnY, q, dsc[slot(c)][:, 2, :])
                if B:
                    for i in range(2):
                        act.wait_ge(bank_free[BANK[f"G{i}"]], val(b, USES[BANK[f"G{i}"]], USE[f"G{i}"] + 1))
                        nc.scalar.activation(gh[:, i, :], ef[:, i, :], ACT.Copy).then_inc(gh_ready, 1)
                if starts(k):
                    lead(nxt)
                if C_:
                    act.wait_ge(scattered[slot(c, 2)], scatter_value(c))
                    norm(c, "3", x[slot(c)], pay[slot(c, 2)])

            act.wait_ge(w_ready, 3)
            over_steps(act, step)

            act.wait_ge(a_done, 1)
            kp = lambda ap: ap.rearrange("(k p) n -> p k n", p=P)
            act.wait_ge(m_clear, 1)
            for row in (0, LOW_ROW):
                for w, name in enumerate(("b1", "b2")):
                    act.dma_start(mbst[row:row + 1, w * E1 * D:(w + 1) * E1 * D],
                                  a[name].rearrange("(a e) n -> a (e n)", a=1)).then_inc(m_loaded, 16)
            for h in range(4):
                if h:
                    act.wait_ge(mw_ready, 2 * h)
                for e in range(E1 // 4):
                    for w, name in enumerate(("w1", "w2")):
                        c0 = e * WC + w * KD * D
                        act.dma_start(mstage[:, c0:c0 + KD * D].rearrange("p (k n) -> p k n", k=KD),
                                      kp(a[name][h * E1 // 4 + e])).then_inc(mw_loaded, 16)
            for s in range(SL):
                act.sem_inc(y_ready[s], 1)

            with act.Fori(0, TILES // SL) as j:
                for s in range(SL):
                    act.wait_ge(pe_c[s], j * 4 + 1)
                    nc.scalar.activation(gTh[s][:, :], ps[2 * s][:, 0:D], ACT.Copy).then_inc(gT_hi[s], 1)
                for s in range(SL):
                    act.wait_ge(pe_c[s], j * 4 + 2)
                    nc.scalar.activation(hf[s][:, :], ps[2 * s + 1][:, 0:D], ACT.Gelu).then_inc(hf_ready[s], 1)
                for s in range(SL):
                    act.wait_ge(pe_c[s], j * 4 + 3)
                    nc.scalar.activation(hTh[s][:, :], ps[2 * s][:, 0:D], ACT.Copy).then_inc(hT_hi[s], 1)
                for s in range(SL):
                    act.wait_ge(pe_c[s], j * 4 + 4)
                    act.wait_ge(sel_ready[s], j + 1)
                    act.wait_ge(returned[s], j * 16 + 16)
                    nc.scalar.activation(ysb[s][:, :], ps[2 * s + 1][:, 0:D], ACT.Copy, scale=wsel[s][:, 0:1]).then_inc(y_ready[s], 1)

            with act.Fori(0, PAIRS // 2) as j:
                for s in range(2):
                    act.wait_ge(d_added[s], j * 2 + 2)
                    rows = bass.ds(j * (2 * PT) + s * PT, PT)
                    act.dma_start(out[rows, :].rearrange("(t p) f -> p t f", p=P), do[s][:, :, :]).then_inc(d_stored[s], 16)

        @block.vector
        def _(dve):
            V = nc.vector

            def low(job, n, dst, hi, op=None):
                dve.wait_ge(hi_done[BANK[job]], val(n, HI_USES[BANK[job]], HI_USE[job]))
                bank = ps[BANK[job]]
                if op is None:
                    ins = V.tensor_tensor(dst, bank[:, :], hi, ALU.subtract)
                else:
                    ins = V.scalar_tensor_tensor(out=dst, in0=bank[:, :], scalar=0.0, in1=hi, op0=op, op1=ALU.subtract)
                ins.then_inc(bank_free[BANK[job]], 1)

            def low_scaled(job, n, dst, hi, gph, d):
                dve.wait_ge(hi_done[BANK[job]], val(n, HI_USES[BANK[job]], HI_USE[job]))
                for i in range(2):
                    t = 2 * gph + i
                    ins = V.scalar_tensor_tensor(out=dst[:, t, :], in0=ps[BANK[job]][:, i * D:(i + 1) * D], scalar=d[:, t:t + 1],
                                                 in1=hi[:, t, :].bitcast(fp32), op0=ALU.mult, op1=ALU.subtract)
                ins.then_inc(bank_free[BANK[job]], 1)

            def stats(n, q, src):
                for t in range(T):
                    ins = V.bn_stats(st[q][:, t, :], src[:, t, :])
                ins.then_inc(st_ready[q], 1)
                dve.wait_ge(st_ready[q], val(n, 1, 1))
                hold(dve)
                for t in range(T):
                    ins = V.bn_aggr(mv[q][:, t, :], st[q][:, t, :])
                ins.then_inc(mv_ready[q], 1)
                dve.wait_ge(mv_ready[q], val(n, 1, 1))
                V.tensor_scalar(vp[q][:, 12:16], mv[q][:, :, 0], -1.0, None, ALU.mult)
                V.tensor_scalar(vp[q][:, 0:T], mv[q][:, :, 1], LN_EPS, None, ALU.add).then_inc(var_ready[q], 1)

            def degree_factors(n):
                dve.wait_ge(deg_ready, val(n, 1, 1))
                V.tensor_scalar(dz[:, :], deg[:, :], 0.0, None, ALU.is_equal).then_inc(dz_ready, 1)
                dve.wait_ge(dz_ready, val(n, 1, 1))
                V.tensor_tensor(vp["0"][:, 4:8], deg[:, :], dz[:, :], ALU.add)
                V.tensor_scalar(nz[:, :], dz[:, :], -1.0, 1.0, ALU.mult, ALU.add)
                V.tensor_scalar(vp["0"][:, 8:12], deg[:, :], 1.0, DEG_EPS, ALU.add, ALU.add).then_inc(var_ready["0"], 1)

            def scales(n):
                dve.wait_ge(rstd_ready["0"], val(n, 1, 1))
                s = slot(n)
                V.tensor_tensor(dsc[s][:, 0, :], rs["0"][:, 4:8], nz[:, :], ALU.mult)
                V.tensor_copy(dsc[s][:, 1, :], rs["0"][:, 8:12])
                V.tensor_tensor(dsc[s][:, 2, :], rs["0"][:, 8:12], mask_cols[:, rows_of(n, T, T)], ALU.mult).then_inc(scale_ready, 1)

            CHOICE_STEPS = 30

            def choices(b, d, B, D_):
                k = [0]

                def after(ins):
                    k[0] += 1
                    ins.then_inc(choice_steps, 1)

                def settle():
                    dve.wait_ge(choice_steps, val(b, CHOICE_STEPS, k[0]))

                r8 = cst[:, C_REV8:C_REV8 + E1].unsqueeze(1).to_broadcast([P, 2 * T, E1])
                b8 = lambda ap: ap.unsqueeze(2).to_broadcast([P, 2 * T, E1])
                F = slice(None)
                if B:
                    job = "GL"
                    dve.wait_ge(bank_full[BANK[job]], val(b, USES[BANK[job]], USE[job]))
                    V.tensor_tensor(ch["lg"][:, 0:T, 0:E0], ps[BANK[job]][:, 0:T * E0].rearrange("p (t e) -> p t e", t=T),
                                    gb[:, :].unsqueeze(1).to_broadcast([P, T, E0]), ALU.add).then_inc(bank_free[BANK[job]], 1)
                    dve.wait_ge(bank_free[BANK[job]], val(b, USES[BANK[job]], USE[job] + 1))
                if D_:
                    job = "RL"
                    dve.wait_ge(bank_full[BANK[job]], val(d, USES[BANK[job]], USE[job]))
                    V.tensor_copy(ch["lg"][:, T:2 * T, :], ps[BANK[job]][:, 0:T * E1].rearrange("p (t e) -> p t e", t=T))\
                        .then_inc(bank_free[BANK[job]], 1)
                    dve.wait_ge(bank_free[BANK[job]], val(d, USES[BANK[job]], USE[job] + 1))
                yield
                after(V.tensor_reduce(cs["m"][:, :], ch["lg"][:, :, :], axis=AX.X, op=ALU.max))
                settle()
                after(V.tensor_tensor(ch["r1"][:, :, :], ch["lg"][:, :, :], b8(cs["m"][:, :]), ALU.subtract))
                settle()
                V.tensor_scalar(ch["key"][:, :, :], ch["r1"][:, :, :], KEY_FLOOR, None, ALU.max).then_inc(shift_ready, 1)
                dve.wait_ge(shift_ready, val(b, 1, 1))
                after(V.scalar_tensor_tensor(out=ch["r1"][:, :, :], in0=ch["key"][:, :, :], scalar=0.0, in1=r8, op0=ALU.is_equal, op1=ALU.mult))
                yield
                settle()
                after(V.tensor_reduce(cs["a"][:, :], ch["r1"][:, :, :], axis=AX.X, op=ALU.max))
                settle()
                after(V.tensor_tensor(ch["oh1"][:, :, :], ch["r1"][:, :, :], b8(cs["a"][:, :]), ALU.is_equal))
                yield
                settle()
                after(V.scalar_tensor_tensor(out=ch["r1"][:, :, :], in0=ch["oh1"][:, :, :], scalar=-1000.0, in1=ch["key"][:, :, :], op0=ALU.mult, op1=ALU.add))
                settle()
                after(V.tensor_reduce(cs["m2"][:, :], ch["r1"][:, :, :], axis=AX.X, op=ALU.max))
                yield
                settle()
                after(V.tensor_tensor(ch["r2"][:, :, :], ch["r1"][:, :, :], b8(cs["m2"][:, :]), ALU.is_equal))
                settle()
                after(V.tensor_tensor(ch["r1"][:, :, :], ch["r2"][:, :, :], r8, ALU.mult))
                yield
                settle()
                after(V.tensor_reduce(cs["b"][:, :], ch["r1"][:, :, :], axis=AX.X, op=ALU.max))
                dve.wait_ge(exp_ready, val(b, 1, 1))
                after(V.reduce_sum(cs["s"][:, :], ch["ex"][:, :, :], axis=AX.X))
                yield
                settle()
                after(V.tensor_tensor(ch["oh2"][:, :, :], ch["r1"][:, :, :], b8(cs["b"][:, :]), ALU.is_equal))
                after(V.reciprocal(cs["rs"][:, :], cs["s"][:, :]))
                yield
                settle()
                if D_:
                    V.tensor_tensor(mb[:, :, :], ch["oh1"][:, T:2 * T, :], ch["oh2"][:, T:2 * T, :], ALU.add).then_inc(mask_ready, 1)
                after(V.tensor_tensor(ch["msk"][:, :, :], ch["oh1"][:, :, :], ch["oh2"][:, :, :], ALU.add))
                after(V.tensor_tensor(ch["pr"][:, :, :], ch["ex"][:, :, :], b8(cs["rs"][:, :]), ALU.mult))
                settle()
                V.tensor_tensor(ch["w"][:, 0:T, :], ch["pr"][:, 0:T, :], cs["rs"][:, 0:T].unsqueeze(2).to_broadcast([P, T, E1]), ALU.subtract)\
                    .then_inc(diff_ready, 1)
                yield
                dve.wait_ge(exp2_ready, val(b, 1, 1))
                after(V.tensor_tensor(ch["w"][:, :, :], ch["pr"][:, :, :], ch["msk"][:, :, :], ALU.mult))
                settle()
                after(V.reduce_sum(cs["s2"][:, :], ch["w"][:, :, :], axis=AX.X))
                yield
                settle()
                after(V.tensor_scalar(cs["a"][:, :], cs["s2"][:, :], 1e-12, None, ALU.max))
                settle()
                after(V.reciprocal(cs["rs2"][:, :], cs["a"][:, :]))
                yield
                settle()
                after(V.tensor_tensor(ch["c"][:, :, :], ch["w"][:, :, :], b8(cs["rs2"][:, :]), ALU.mult))
                settle()
                if B:
                    after(V.tensor_copy(cb[:, :, 0:4], ch["c"][:, 0:T, 0:E0]))
                    yield
                    settle()
                    after(V.tensor_copy(cb[:, :, 4:8], cb[:, :, 0:4].bitcast(fp32)))
                    V.tensor_tensor(cb[:, :, 8:12], ch["c"][:, 0:T, 0:E0], cb[:, :, 0:4].bitcast(fp32), ALU.subtract).then_inc(cb_ready, 1)
                else:
                    V.sem_inc(choice_steps, 2)
                    k[0] += 2
                yield
                if D_:
                    s = slot(d, 2)
                    after(V.tensor_copy(pay[s][:, :, D:D + E1], ch["c"][:, T:2 * T, :]))
                    after(V.tensor_tensor(pay[s][:, :, D + E1:ROW], ch["oh2"][:, T:2 * T, :], tok2[:, :].unsqueeze(2).to_broadcast([P, T, E1]), ALU.add))
                    job = "POS"
                    dve.wait_ge(bank_full[BANK[job]], val(d, USES[BANK[job]], USE[job]))
                    after(V.tensor_tensor(rt["pos"][:, :, :], ps[BANK[job]][:, 0:T * E1].rearrange("p (t e) -> p t e", t=T),
                                          base[:, :].unsqueeze(1).to_broadcast([P, T, E1]), ALU.add))
                    settle()
                    after(V.tensor_tensor(rt["q1"][:, :, :], rt["pos"][:, :, :], ch["oh1"][:, T:2 * T, :], ALU.mult))
                    after(V.tensor_tensor(rt["q2"][:, :, :], rt["pos"][:, :, :], ch["oh2"][:, T:2 * T, :], ALU.mult))
                    V.tensor_tensor(base[:, :], ps[BANK[job]][:, T * E1:(T + 1) * E1], base[:, :], ALU.add).then_inc(bank_free[BANK[job]], 1)
                    after(V.tensor_scalar(tok2[:, :], tok2[:, :], float(2 * PT), None, ALU.add))
                    yield
                    settle()
                    after(V.reduce_sum(idx_f[:, 0, :], rt["q1"][:, :, :], axis=AX.X))
                    after(V.reduce_sum(idx_f[:, 1, :], rt["q2"][:, :, :], axis=AX.X))
                    settle()
                    V.tensor_copy(idx[s][:, :, :], idx_f[:, :, :]).then_inc(idx_ready, 1)
                else:
                    V.sem_inc(choice_steps, 8)
                    k[0] += 8
                assert k[0] == CHOICE_STEPS, k[0]

            def lead(n):
                for i in range(KD):
                    low(f"xT0k{i}", n, xTlA[:, i, :], xThA[:, i, :].bitcast(fp32))
                flat = lambda t, q: t[slot(n)][:, q, :, :].rearrange("p a b -> p (a b)")
                for q in range(2):
                    low(f"ATg{q}", n, flat(ATl, q), flat(ATh, q).bitcast(fp32))

            def step(k):
                a, b, c, d, nxt = k, ago(k, 1), ago(k, 2), ago(k, 3), ago(k, -1)
                A, B, C_, D_ = active(a), active(b), active(c), active(d)
                chain = choices(b, d, B, D_) if B or D_ else iter(())
                go = lambda: next(chain, None)
                if k[1] == 0 and k[2] == 0:
                    dve.wait_ge(x_loaded[0], 16)
                    stats(a, "0", x[0])
                    degree_factors(a)
                    scales(a)
                    lead(a)
                if B:
                    for i in range(KD):
                        low(f"xT1k{i}", b, xTlB[:, i, :], xThB[:, i, :].bitcast(fp32))
                if C_:
                    stats(c, "2", x[slot(c)])
                if A:
                    for q in range(2):
                        low_scaled(f"T0g{q}", a, TlA, ThA, q, dsc[slot(a)][:, 0, :])
                if B:
                    for m in range(2):
                        low(f"S1m{m}", b, hl[:, m, :], hh[:, m, :].bitcast(fp32), ALU.max)
                go()
                go()
                go()
                for i in range(KD):
                    if C_:
                        low(f"xT2k{i}", c, xTlY[:, i, :], xThY[:, i, :].bitcast(fp32))
                    go()
                for i in range(2):
                    if B:
                        low(f"E1e{i}", b, hl[:, 2 + i, :], hh[:, 2 + i, :].bitcast(fp32), ALU.max)
                    go()
                if B:
                    low("S2", b, s2l[:, :], s2h[:, :].bitcast(fp32), ALU.max)
                go()
                for q in range(2):
                    if C_:
                        low_scaled(f"T1g{q}", c, TlY, ThY, q, dsc[slot(c)][:, 1, :])
                    go()
                for i in range(2):
                    if B:
                        low(f"E1e{2 + i}", b, hl[:, i, :], hh[:, i, :].bitcast(fp32), ALU.max)
                    go()
                if starts(k):
                    dve.wait_ge(x_loaded[slot(nxt)], x_value(nxt))
                    stats(nxt, "0", x[slot(nxt)])
                    degree_factors(nxt)
                go()
                if A:
                    dve.wait_ge(x1_ready, val(a, 2, 2))
                    stats(a, "1", x[slot(a)])
                for _ in chain:
                    pass
                if starts(k):
                    scales(nxt)
                if B:
                    for i in range(2):
                        job = f"G{i}"
                        dve.wait_ge(bank_full[BANK[job]], val(b, USES[BANK[job]], USE[job]))
                        dve.wait_ge(bank_free[BANK[f"EP{i}"]], val(b, USES[BANK[f"EP{i}"]], USE[f"EP{i}"] + 1))
                        V.tensor_tensor(ef[:, i, :], ef[:, i, :], ps[BANK[job]][:, :], ALU.mult).then_inc(bank_free[BANK[job]], 1)
                    for i in range(2):
                        dve.wait_ge(gh_ready, val(b, 2, i + 1))
                        V.tensor_tensor(gl[:, i, :], ef[:, i, :], gh[:, i, :].bitcast(fp32), ALU.subtract).then_inc(gl_ready, 1)
                if starts(k):
                    lead(nxt)
                if C_:
                    dve.wait_ge(x3_ready, val(c, 2, 2))
                    stats(c, "3", x[slot(c)])
                if B:
                    for q in range(2):
                        job = f"O1g{q}"
                        dve.wait_ge(bank_full[BANK[job]], val(b, USES[BANK[job]], USE[job]))
                        half = x[slot(b)][:, 2 * q:2 * q + 2, :].rearrange("p a b -> p (a b)")
                        V.tensor_tensor(half, half, ps[BANK[job]][:, :], ALU.add).then_inc(bank_free[BANK[job]], 1)
                    for q in range(2):
                        dve.wait_ge(bank_free[BANK[f"O1g{q}"]], val(b, USES[BANK[f"O1g{q}"]], USE[f"O1g{q}"] + 1))

            V.memset(stage[:, :], 0.0)
            V.memset(bstage[:, :], 0.0)
            V.memset(ostage[:, :], 0.0).then_inc(w_ready, 1)
            V.memset(minus_half[:, :], -0.5)
            V.memset(ch["lg"][:, :, :], KEY_FLOOR)
            V.memset(ch["pr"][:, :, :], 0.0)
            V.memset(cbT[:, :].bitcast(fp32), 0.0)
            V.memset(ones_b[:, :], 1.0)
            V.memset(cb[:, :, :].bitcast(fp32), 0.0)
            V.memset(btmp[:, :].bitcast(fp32), 0.0)
            V.memset(otmp[:, :], 1.0).then_inc(dve_setup, 1)
            dve.wait_ge(dve_setup, 1)
            V.memset(cb[:, :, 12:14].bitcast(fp32), 1.0)
            V.memset(ones_r[:, :].bitcast(fp32), 1.0).then_inc(dve_setup, 1)
            dve.wait_ge(dve_setup, 2)
            dve.wait_ge(misc, 16)
            V.tensor_copy(id_r[:, :], cst[:, C_ID:C_ID + P])
            V.tensor_copy(sel_r[:, :], cst[:, C_SEL:C_SEL + 2 * P])
            V.tensor_copy(tri_b[:, :], cst[:, C_TRI:C_TRI + P])
            V.tensor_copy(base[:, :], cst[:, C_ECAP:C_ECAP + E1])
            V.tensor_copy(tok2[:, :], cst[:, C_TOK2:C_TOK2 + T])
            dve.wait_ge(mask_turned, 1)
            V.tensor_copy(mask_cols[:, :], ps[0][:, 0:P]).then_inc(dve_setup, 1)
            dve.wait_ge(dve_setup, 3)
            for b in range(8):
                V.sem_inc(bank_free[b], 1)
            dve.wait_ge(bias_loaded, 16 * 18)
            V.tensor_copy(brow[:, :], bstage[:, :]).then_inc(dve_setup, 1)
            V.tensor_copy(ohi[:, :], ostage[:, :]).then_inc(dve_setup, 1)
            dve.wait_ge(dve_setup, 5)
            V.tensor_copy(btmp[LOW_ROW:LOW_ROW + 1, :], brow[LOW_ROW:LOW_ROW + 1, :].bitcast(fp32)).then_inc(dve_setup, 1)
            V.tensor_tensor(olo[:, :], ostage[:, :], ohi[:, :].bitcast(fp32), ALU.subtract).then_inc(dve_setup, 1)
            dve.wait_ge(dve_setup, 7)
            V.tensor_tensor(brow[LOW_ROW:LOW_ROW + 1, :], bstage[LOW_ROW:LOW_ROW + 1, :], btmp[LOW_ROW:LOW_ROW + 1, :].bitcast(fp32), ALU.subtract)
            V.tensor_scalar(otmp[:, :], ohi[:, :].bitcast(fp32), cst[0:16, C_MH:C_MH + 1], None, ALU.mult)
            V.memset(o_bias[:, :].bitcast(fp32), 0.0).then_inc(dve_setup, 1)
            dve.wait_ge(dve_setup, 8)
            V.scalar_tensor_tensor(out=o_bias[0:16, :], in0=olo[:, :].bitcast(fp32), scalar=cst[0:16, C_ML:C_ML + 1], in1=otmp[:, :],
                                   op0=ALU.mult, op1=ALU.add)
            dve.wait_ge(w_loaded, 16 * 16)
            V.tensor_copy(w0h[:, :], stage[:, :]).then_inc(w_ready, 1)
            dve.wait_ge(w_ready, 2)
            V.tensor_tensor(w0l[:, :], stage[:, :], w0h[:, :].bitcast(fp32), ALU.subtract).then_inc(w_ready, 1)
            dve.wait_ge(w_ready, 3)

            over_steps(dve, step)

            dve.wait_ge(idx_ready, PAIRS)
            k = [0]

            def b_step(ins):
                k[0] += 1
                ins.then_inc(b_steps, 1)
                dve.wait_ge(b_steps, k[0])

            V.tensor_copy(cnt_i[:, 0:E1], base[:, :]).then_inc(counts_ready, 1)
            dve.wait_ge(counts_ready, 1)
            b_step(V.tensor_tensor(cnt_f[:, 0:E1], base[:, :], cst[:, C_ECAP:C_ECAP + E1], ALU.subtract))
            b_step(V.tensor_scalar(cnt_f[:, 0:E1], cnt_f[:, 0:E1], float(P - 1), None, ALU.add))
            b_step(V.tensor_copy(cnt_i[:, E1:2 * E1], cnt_f[:, 0:E1]))
            b_step(V.tensor_scalar(cnt_i[:, 2 * E1:3 * E1], cnt_i[:, E1:2 * E1], 7, None, ALU.logical_shift_right))
            b_step(V.tensor_copy(cnt_f[:, E1:2 * E1], cnt_i[:, 2 * E1:3 * E1]))
            b_step(V.tensor_scalar(cnt_f[:, E1:2 * E1], cnt_f[:, E1:2 * E1], float(P), None, ALU.mult))
            b_step(V.tensor_copy(cnt_f[:, 2 * E1:3 * E1], cnt_f[:, E1:2 * E1]))
            for e in range(1, E1):
                b_step(V.tensor_tensor(cnt_f[:, 2 * E1 + e:2 * E1 + e + 1], cnt_f[:, 2 * E1 + e:2 * E1 + e + 1],
                                       cnt_f[:, 2 * E1 + e - 1:2 * E1 + e], ALU.add))
            b_step(V.tensor_scalar(cnt_f[:, 3 * E1:4 * E1], cnt_f[:, E1:2 * E1], -1.0, float(CAP), ALU.mult, ALU.add))
            b_step(V.tensor_copy(tab_f[:, 0:NJ], cst[:, C_J:C_J + NJ]))
            for e in range(E1):
                b_step(V.tensor_scalar(tab_f[:, NJ:2 * NJ], cst[:, C_J:C_J + NJ], cnt_f[:, 2 * E1 + e:2 * E1 + e + 1],
                                       cnt_f[:, 3 * E1 + e:3 * E1 + e + 1], ALU.is_ge, ALU.mult))
                b_step(V.tensor_tensor(tab_f[:, 0:NJ], tab_f[:, 0:NJ], tab_f[:, NJ:2 * NJ], ALU.add))
            b_step(V.memset(tab_f[:, 2 * NJ:3 * NJ], 0.0))
            for e in range(E1 - 1):
                b_step(V.tensor_scalar(tab_f[:, NJ:2 * NJ], cst[:, C_J:C_J + NJ], cnt_f[:, 2 * E1 + e:2 * E1 + e + 1], None, ALU.is_ge))
                b_step(V.tensor_tensor(tab_f[:, 2 * NJ:3 * NJ], tab_f[:, 2 * NJ:3 * NJ], tab_f[:, NJ:2 * NJ], ALU.add))
            V.tensor_copy(tab_i[:, 0:NJ], tab_f[:, 0:NJ])
            V.tensor_copy(tab_i[:, NJ:2 * NJ], tab_f[:, 2 * NJ:3 * NJ]).then_inc(table_ready, 1)

            dve.wait_ge(a_done, 1)
            V.memset(mbst[:, :], 0.0).then_inc(m_clear, 1)
            dve.wait_ge(m_loaded, 16 * 4)
            quarter = E1 * WC // 4
            V.tensor_copy(b1r[:, :], mbst[:, :]).then_inc(mb_steps, 1)
            dve.wait_ge(mb_steps, 1)
            V.tensor_copy(mbtmp[LOW_ROW:LOW_ROW + 1, :], b1r[LOW_ROW:LOW_ROW + 1, :].bitcast(fp32)).then_inc(mb_steps, 1)
            dve.wait_ge(mb_steps, 2)
            V.tensor_tensor(b1r[LOW_ROW:LOW_ROW + 1, :], mbst[LOW_ROW:LOW_ROW + 1, :], mbtmp[LOW_ROW:LOW_ROW + 1, :].bitcast(fp32), ALU.subtract)
            for h in range(4):
                dve.wait_ge(mw_loaded, 16 * (h + 1) * E1 // 2)
                cols = slice(h * quarter, (h + 1) * quarter)
                V.tensor_copy(w1h[:, cols], mstage[:, :]).then_inc(mw_ready, 1)
                dve.wait_ge(mw_ready, 2 * h + 1)
                V.tensor_tensor(w1l[:, cols], mstage[:, :], w1h[:, cols].bitcast(fp32), ALU.subtract).then_inc(mw_ready, 1)

            for s in range(SL):
                V.sem_inc(slot_used[s], 1)
            with dve.Fori(0, TILES // SL) as j:
                for s in range(SL):
                    dve.wait_ge(gT_hi[s], j + 1)
                    V.tensor_tensor(gTl[s][:, :], ps[2 * s][:, 0:D], gTh[s][:, :].bitcast(fp32), ALU.subtract).then_inc(gT_lo[s], 1)
                for s in range(SL):
                    dve.wait_ge(g_loaded[s], j * 16 + 16)
                    e = dve.value_load(tab_i[0:1, bass.ds(j * SL + (NJ + s), 1)], min_val=0, max_val=E1 - 1)
                    dve.wait_ge(returned[s], j * 16 + 16)
                    dve.wait_ge(y_ready[s], j + 1)
                    V.tensor_copy(isel[s][:, 0:1], g[s][:, bass.ds(e + (D + E1), 1)])
                    V.tensor_copy(wsel[s][:, 0:1], g[s][:, bass.ds(e + D, 1)]).then_inc(sel_ready[s], 1)
                    dve.wait_ge(sel_ready[s], j + 1)
                    V.sem_inc(slot_used[s], 1)
                for s in range(SL):
                    dve.wait_ge(hT_hi[s], j + 1)
                    V.tensor_tensor(hTl[s][:, :], ps[2 * s][:, 0:D], hTh[s][:, :].bitcast(fp32), ALU.subtract).then_inc(hT_lo[s], 1)

            for s in range(2):
                V.sem_inc(d_stored[s], 16)
            with dve.Fori(0, PAIRS // 2) as j:
                for s in range(2):
                    dve.wait_ge(dy_loaded[s], j * 16 + 16)
                    dve.wait_ge(dx_loaded[s], j * 16 + 16)
                    V.tensor_tensor(dt_[s][:, :, :], dx[s][:, :, :], dy[s][:, :, 0:D], ALU.add).then_inc(d_added[s], 1)
                    dve.wait_ge(d_added[s], j * 2 + 1)
                    dve.wait_ge(d_stored[s], j * 16 + 16)
                    V.tensor_tensor(do[s][:, :, :], dt_[s][:, :, :], dy[s][:, :, D:2 * D], ALU.add).then_inc(d_added[s], 1)

        @block.gpsimd
        def _(pool):
            G = nc.gpsimd
            for s in range(2):
                pool.dma_start(idx_credit[:, 2 * s:2 * s + 2], a["consts"][:, 0:2]).then_inc(scattered[s], 2 * T * 16)
            for s in range(SL):
                pool.dma_start(idx_credit[:, 4 + 2 * s:6 + 2 * s], a["consts"][:, 0:2]).then_inc(returned[s], 16)
            pool.wait_ge(dve_setup, 3)
            G.sem_inc(x3_stored, 16)

            def power(n, q, cols):
                per = 2 if q == "0" else 1
                pool.wait_ge(var_ready[q], val(n, per, per))
                G.tensor_tensor(rs[q][:, 0:cols], vp[q][:, 0:cols], minus_half[:, 0:cols], ALU.pow).then_inc(pow_ready[q], 1)
                pool.wait_ge(pow_ready[q], val(n, 1, 1))
                G.tensor_tensor(rs[q][:, 12:16], vp[q][:, 12:16], rs[q][:, 0:T], ALU.mult).then_inc(rstd_ready[q], 1)

            def residual(n, name, add, ready):
                for q in range(2):
                    job = f"{name}g{q}"
                    pool.wait_ge(bank_free[BANK[job]], val(n, USES[BANK[job]], USE[job] + 1))
                    half = lambda b: b[:, 2 * q:2 * q + 2, :].rearrange("p a b -> p (a b)")
                    G.tensor_tensor(half(x[slot(n)]), half(x[slot(n)]), half(add), ALU.add).then_inc(ready, 1)

            def send(n):
                pool.wait_ge(idx_ready, val(n, 1, 1))
                hold(pool)
                s = slot(n, 2)
                for t in range(T):
                    for i in range(2):
                        G.indirect_dma_start(out=routed, out_offset=bass.IndirectOffsetOnAxis(ap=idx[s][:, i, t:t + 1], axis=0),
                                             in_=pay[s][:, t, :], in_offset=None).then_inc(scattered[s], 16)

            def step(k):
                a, b, c, d, e, nxt = k, ago(k, 1), ago(k, 2), ago(k, 3), ago(k, 4), ago(k, -1)
                A, B, C_, D_ = active(a), active(b), active(c), active(d)
                if k[1] == 0 and k[2] == 0:
                    power(a, "0", 12)
                if C_:
                    power(c, "2", T)
                if D_:
                    pool.wait_ge(xn_ready["3"], val(d, 1, 1))
                    pool.wait_ge(x3_stored, val(d, 16, 16))
                    G.tensor_tensor(xo[:, :, :], x[slot(d)][:, :, :], pay[slot(d, 2)][:, :, 0:D], ALU.add).then_inc(x3_summed, 1)
                if active(e):
                    send(e)
                if A:
                    residual(a, "M0", xnA, x1_ready)
                if starts(k):
                    power(nxt, "0", 12)
                if A:
                    power(a, "1", T)
                if C_:
                    residual(c, "M1", xnY, x3_ready)
                    power(c, "3", T)

            over_steps(pool, step)
            send((None, 0, PAIRS - 1))

            with pool.Fori(0, TILES // SL) as j:
                for s in range(SL):
                    pool.wait_ge(y_ready[s], j + 2)
                    pool.wait_ge(sel_ready[s], j + 1)
                    hold(pool)
                    G.indirect_dma_start(out=back, out_offset=bass.IndirectOffsetOnAxis(ap=isel[s][:, 0:1], axis=0),
                                         in_=ysb[s][:, :], in_offset=None, bounds_check=2 * TOK - 1, oob_is_err=False)\
                        .then_inc(returned[s], 16)

        @block.tensor
        def _(pe):
            mm, turn = nc.tensor.matmul, nc.tensor.transpose
            ident = cst[:, C_ID:C_ID + P]

            def free(job, n):
                pe.wait_ge(bank_free[BANK[job]], val(n, USES[BANK[job]], USE[job]))

            def read_out(job, n):
                pe.wait_ge(bank_free[BANK[job]], val(n, USES[BANK[job]], USE[job] + 1))

            def filled(job, ins):
                ins.then_inc(bank_full[BANK[job]], 1)

            def mm3(o, left, right, start, stop):
                mm(o, left[0], right[0], start=start, stop=False)
                mm(o, left[0], right[1], start=False, stop=False)
                return mm(o, left[1], right[0], start=False, stop=stop)

            def W(name, lo, cols):
                return w0(0, name, lo, cols), w0(1, name, lo, cols)

            def transposes(n, name, src, blocks=range(KD)):
                for k in blocks:
                    job = f"{name}k{k}"
                    free(job, n)
                    for t in range(T):
                        ins = turn(ps[BANK[job]][:, t * P:(t + 1) * P], src[:, t, k * P:(k + 1) * P], ident)
                    filled(job, ins)

            def linear(n, name, xt, h, l, w, bias):
                read_out(f"{xt}k1", n)
                for q in range(2):
                    job = f"{name}g{q}"
                    free(job, n)
                    for i in range(2):
                        t = 2 * q + i
                        o = ps[BANK[job]][:, i * D:(i + 1) * D]
                        mm(o, ones_r[:, 0:P], brow[:, B0[bias]:B0[bias] + D], start=True, stop=False)
                        for k in range(KD):
                            cols = slice(t * P, (t + 1) * P)
                            ins = mm3(o, (h[:, k, cols], l[:, k, cols]), W(w, k * D, D), False, k == KD - 1)
                    filled(job, ins)

            def conv(n, s, name, h, l, loops):
                for q in range(2):
                    job = f"{name}g{q}"
                    free(job, n)
                    for i in range(2):
                        o = ps[BANK[job]][:, i * D:(i + 1) * D]
                        for jb in range(2):
                            cols = slice(i * P, (i + 1) * P)
                            ins = mm3(o, (ATh[s][:, q, jb, cols], ATl[s][:, q, jb, cols]), (h[:, 2 * q + jb, :], l[:, 2 * q + jb, :]),
                                      jb == 0, jb == 1 and not loops)
                        if loops:
                            mm(o, id_r[:, :], h[:, 2 * q + i, :], start=False, stop=False)
                            ins = mm(o, id_r[:, :], l[:, 2 * q + i, :], start=False, stop=True)
                    filled(job, ins)

            def dense(n, job, weights, rights, bias):
                free(job, n)
                o = ps[BANK[job]][:, :]
                if bias is not None:
                    mm(o, brow[:, bias:bias + P], ones_r[:, :], start=True, stop=False)
                for k, (w, x_) in enumerate(zip(weights, rights)):
                    ins = mm3(o, w, x_, bias is None and k == 0, k == len(weights) - 1)
                filled(job, ins)

            def experts_in(n, i):
                e_blocks = [W("eW1", i * D + k * EH1, EH1) for k in range(KD)]
                dense(n, f"E1e{i}", e_blocks, [(xThB[:, k, :], xTlB[:, k, :]) for k in range(KD)], B0["eb1"] + i * EH1)

            def experts_mid(n, i):
                for e in range(2):
                    read_out(f"E1e{2 * i + e}", n)
                dense(n, f"EP{i}", [W("eW2", (2 * i + e) * P, P) for e in range(2)], [H[(2 * (i + 1) + e) % 4] for e in range(2)], None)

            H = [(hh[:, m, :], hl[:, m, :]) for m in range(4)]

            def lead(n):
                pe.wait_ge(xn_ready["0"], val(n, 1, 1))
                transposes(n, "xT0", xnA)
                pe.wait_ge(adj_loaded[slot(n, 2)], adj_value(n))
                for q in range(2):
                    job = f"ATg{q}"
                    free(job, n)
                    for jb in range(2):
                        for i in range(2):
                            ins = turn(ps[BANK[job]][:, jb * N + i * P:jb * N + (i + 1) * P], adj[slot(n, 2)][:, 2 * q + i, jb * P:(jb + 1) * P], ident)
                    filled(job, ins)

            def step(k):
                a, b, c, d, nxt = k, ago(k, 1), ago(k, 2), ago(k, 3), ago(k, -1)
                A, B, C_, D_ = active(a), active(b), active(c), active(d)
                if k[1] == 0 and k[2] == 0:
                    lead(a)
                if B:
                    pe.wait_ge(xn_ready["1"], val(b, 1, 1))
                    transposes(b, "xT1", xnB)
                if D_:
                    pe.wait_ge(xn_ready["3"], val(d, 1, 1))
                    transposes(d, "xT3", pay[slot(d, 2)], (0,))
                if A:
                    linear(a, "T0", "xT0", xThA, xTlA, "g0", "g0")
                if D_:
                    transposes(d, "xT3", pay[slot(d, 2)], (1,))
                if B:
                    for i in range(KD):
                        read_out(f"xT1k{i}", b)
                    job = "GL"
                    free(job, b)
                    for t in range(T):
                        for i in range(KD):
                            cols = slice(t * P, (t + 1) * P)
                            ins = mm3(ps[BANK[job]][:, t * E0:(t + 1) * E0], (xThB[:, i, cols], xTlB[:, i, cols]), W("gW", i * E0, E0), i == 0, i == KD - 1)
                    filled(job, ins)
                    xT = [(xThB[:, i, :], xTlB[:, i, :]) for i in range(KD)]
                    for m in range(2):
                        dense(b, f"S1m{m}", [W("sW1", i * D + m * P, P) for i in range(KD)], xT, B0["sb1"] + m * P)
                if D_:
                    job = "RL"
                    free(job, d)
                    for t in range(T):
                        for i in range(KD):
                            ins = mm(ps[BANK[job]][:, t * E1:(t + 1) * E1], xT3[:, i, t * P:(t + 1) * P], rW[:, i, :], start=(i == 0), stop=(i == KD - 1))
                    filled(job, ins)
                if A:
                    conv(a, slot(a), "M0", ThA, TlA, False)
                if C_:
                    pe.wait_ge(xn_ready["2"], val(c, 1, 1))
                    transposes(c, "xT2", xnY)
                if B:
                    experts_in(b, 0)
                    experts_in(b, 1)
                    dense(b, "S2", [W("sW2", i * P, P) for i in range(KD)], H[0:2], B0["sb2"])
                if C_:
                    linear(c, "T1", "xT2", xThY, xTlY, "g1", "g1")
                if B:
                    experts_in(b, 2)
                    experts_in(b, 3)
                    experts_mid(b, 0)
                if D_:
                    job = "POS"
                    pe.wait_ge(mask_ready, val(d, 1, 1))
                    free(job, d)
                    for t in range(T):
                        o = ps[BANK[job]][:, t * E1:(t + 1) * E1]
                        for u in range(t):
                            mm(o, ones_b[:, :], mb[:, u, :], start=(u == 0), stop=False)
                        mm(o, tri_b[:, :], mb[:, t, :], start=(t == 0), stop=True)
                    for t in range(T):
                        ins = mm(ps[BANK[job]][:, T * E1:(T + 1) * E1], ones_b[:, :], mb[:, t, :], start=(t == 0), stop=(t == T - 1))
                    filled(job, ins)
                if B:
                    experts_mid(b, 1)
                    job = "CBT"
                    pe.wait_ge(cb_ready, val(b, 1, 1))
                    free(job, b)
                    for t in range(T):
                        ins = turn(ps[BANK[job]][0:16, t * P:(t + 1) * P], cb[:, t, :].bitcast(fp32), ident)
                    filled(job, ins)
                if C_:
                    conv(c, slot(c), "M1", ThY, TlY, True)
                if B:
                    read_out("CBT", b)
                    for i in range(2):
                        job = f"G{i}"
                        free(job, b)
                        filled(job, mm(ps[BANK[job]][:, :], sel_r[:, i * P:(i + 1) * P], cbT[:, :], start=True, stop=True))
                if starts(k):
                    lead(nxt)
                if B:
                    for i in range(2):
                        parts = [(q, ps[BANK[f"O1g{q}"]][:, i * D:(i + 1) * D], slice((2 * q + i) * P, (2 * q + i + 1) * P)) for q in range(2)]
                        for q, o, cols in parts:
                            if i == 0:
                                free(f"O1g{q}", b)
                            mm(o, cbT[:, cols], o_bias[:, :], start=True, stop=False)
                            mm3(o, (s2h[:, cols], s2l[:, cols]), W("sW3", 0, D), False, False)
                        for e in range(2):
                            if i == 0:
                                pe.wait_ge(gl_ready, val(b, 2, e + 1))
                            for q, o, cols in parts:
                                ins = mm3(o, (gh[:, e, cols], gl[:, e, cols]), W("eW3", e * D, D), False, e == 1)
                                if e == 1 and i == 1:
                                    filled(f"O1g{q}", ins)

            pe.wait_ge(misc, 16)
            pe.wait_ge(mask_loaded, 16)
            turn(ps[0][:, 0:P], mask_rows[:, :], ident).then_inc(mask_turned, 1)
            pe.wait_ge(w_ready, 3)

            over_steps(pe, step)

            pe.wait_ge(table_ready, 1)
            pe.wait_ge(mw_ready, 8)
            with pe.Fori(0, TILES // SL) as j:
                experts = []
                for s in range(SL):
                    pe.wait_ge(g_loaded[s], j * 16 + 16)
                    for k in range(KD):
                        ins = turn(ps[2 * s][:, k * P:(k + 1) * P], g[s][:, k * P:(k + 1) * P], ident)
                    ins.then_inc(pe_c[s], 1)
                for s in range(SL):
                    experts.append(pe.value_load(tab_i[0:1, bass.ds(j * SL + (NJ + s), 1)], min_val=0, max_val=E1 - 1))

                def product(s, w, h, l):
                    e = experts[s]
                    o = ps[2 * s + 1][:, 0:D]
                    mm(o, ones_r[:, 0:P], b1r[:, bass.ds(e * D + w * E1 * D, D)], start=True, stop=False)
                    for k in range(KD):
                        cols = slice(k * P, (k + 1) * P)
                        c = bass.ds(e * WC + (w * KD + k) * D, D)
                        ins = mm3(o, (h[s][:, cols], l[s][:, cols]), (w1h[:, c], w1l[:, c]), False, k == KD - 1)
                    ins.then_inc(pe_c[s], 1)

                for s in range(SL):
                    pe.wait_ge(gT_lo[s], j + 1)
                    pe.wait_ge(y_ready[s], j + 1)
                    product(s, 0, gTh, gTl)
                for s in range(SL):
                    pe.wait_ge(hf_ready[s], j + 1)
                    for k in range(KD):
                        ins = turn(ps[2 * s][:, k * P:(k + 1) * P], hf[s][:, k * P:(k + 1) * P], ident)
                    ins.then_inc(pe_c[s], 1)
                for s in range(SL):
                    pe.wait_ge(hT_lo[s], j + 1)
                    product(s, 1, hTh, hTl)


def kernel(x, adj, nodemask, L0_gnn_W, L0_gnn_b, L0_ffn_sW1, L0_ffn_sb1, L0_ffn_sW2, L0_ffn_sb2, L0_ffn_sW3, L0_ffn_sb3,
           L0_ffn_eW1, L0_ffn_eb1, L0_ffn_eW2, L0_ffn_eb2, L0_ffn_eW3, L0_ffn_eb3, L0_ffn_gW, L0_ffn_gb, L1_gnn_W, L1_gnn_b,
           L1_ffn_router_w, L1_ffn_w1, L1_ffn_b1, L1_ffn_w2, L1_ffn_b2):
    import concourse.bacc as bacc
    from concourse.bass_utils import run_bass_kernel_spmd

    lay = lambda v: np.ascontiguousarray(np.asarray(v))
    arrays = {
        "x": lay(x).reshape(TOK, D), "adj": lay(adj).reshape(TOK, N), "nodemask": lay(nodemask).reshape(P, P),
        "g0W": lay(np.asarray(L0_gnn_W).T), "g0b": lay(L0_gnn_b), "g1W": lay(np.asarray(L1_gnn_W).T), "g1b": lay(L1_gnn_b),
        "sW1": lay(L0_ffn_sW1), "sb1": lay(L0_ffn_sb1), "sW2": lay(L0_ffn_sW2), "sb2": lay(L0_ffn_sb2),
        "sW3": lay(L0_ffn_sW3), "sb3": lay(L0_ffn_sb3), "eW1": lay(L0_ffn_eW1), "eb1": lay(L0_ffn_eb1),
        "eW2": lay(L0_ffn_eW2), "eb2": lay(L0_ffn_eb2), "eW3": lay(L0_ffn_eW3), "eb3": lay(L0_ffn_eb3),
        "gW": lay(L0_ffn_gW), "gb": lay(L0_ffn_gb), "rW": lay(np.asarray(L1_ffn_router_w).T),
        "w1": lay(L1_ffn_w1), "b1": lay(L1_ffn_b1), "w2": lay(L1_ffn_w2), "b2": lay(L1_ffn_b2),
        "consts": constants(),
    }
    nc = bacc.Bacc("TRN2", target_bir_lowering=False, num_devices=1)
    a = {n: nc.dram_tensor("in_" + n, v.shape, mybir.dt.from_np(v.dtype), kind="ExternalInput").ap() for n, v in arrays.items()}
    out = nc.dram_tensor("out", (TOK, D), fp32, kind="ExternalOutput").ap()
    build(nc, a, out)
    res = run_bass_kernel_spmd(nc, [{"in_" + n: v for n, v in arrays.items()}], core_ids=[0])
    return res.results[0]["out"].reshape(GRAPHS, N, D)
```

```python
from contextlib import ExitStack

import numpy as np

import concourse.bass as bass
from concourse import mybir

fp32 = mybir.dt.float32
f32r = mybir.dt.float32r
bf16 = mybir.dt.bfloat16
i32 = mybir.dt.int32
ALU = mybir.AluOpType
ACT = mybir.ActivationFunctionType
AX = mybir.AxisListType

P = 128
GRAPHS, N, D = 64, 256, 256
TOK = GRAPHS * N
T = 4
PT = T * P
PAIRS = GRAPHS // 2
RING = 4
KD = D // P
E0, E1 = 4, 8
EH1, EH2 = 128, 64
LN_EPS, DEG_EPS = 1e-5, 1e-8
KEY_FLOOR = -88.0
ROW = D + 2 * E1
CAP = TOK + P
NJ = TOK // P + E1
TILES = 2 * NJ
R = 2 * E1
SKIP = 1 << 16

C_ID, C_TRI, C_SEL, C_MH, C_ML = 0, 128, 256, 512, 513
C_REV8, C_REV4, C_CAP, C_TOK, C_J, C_PAD = 514, 522, 526, 526 + R, 530 + R, 530 + R + NJ
C_ALL = C_PAD + ROW


def constants():
    c = np.zeros((P, C_ALL), np.float32)
    p = np.arange(P)
    c[:, C_ID:C_ID + P] = np.eye(P)
    c[:, C_TRI:C_TRI + P] = p[:, None] < p[None, :]
    for b in range(2):
        for m in range(P):
            e = 2 * b + m // EH2
            c[e, C_SEL + b * P + m] = 1.0
            c[8 + e, C_SEL + b * P + m] = 1.0
    c[[0, 1, 2, 3, 8, 9, 10, 11, 12], C_MH] = 1.0
    c[[4, 5, 6, 7, 13], C_ML] = 1.0
    c[:, C_REV8:C_REV8 + E1] = E1 - np.arange(E1)
    c[:, C_REV4:C_REV4 + E0] = E0 - np.arange(E0)
    c[:, C_CAP:C_CAP + R] = np.tile(CAP * np.arange(E1), 2)
    c[:, C_TOK:C_TOK + T] = P * np.arange(T)[None, :] + p[:, None]
    c[:, C_J:C_J + NJ] = P * np.arange(NJ)
    c[:, C_PAD + D + E1:C_PAD + ROW] = SKIP
    return c


JOBS = [
    ("xT0k0", 0), ("xT0k1", 1), ("ATg0", 0), ("ATg1", 1), ("T0g0", 0), ("T0g1", 1), ("M0g0", 0), ("M0g1", 1),
    ("xT1k0", 2), ("xT1k1", 3), ("GL", 7), ("S1m0", 2), ("S1m1", 3), ("S2", 7), ("E1e0", 2), ("E1e1", 3),
    ("E1e2", 2), ("EP0", 7), ("E1e3", 3), ("CBT", 7), ("EP1", 7), ("G0", 2), ("G1", 3), ("O1g0", 7), ("O1g1", 2),
    ("xT2k0", 4), ("xT2k1", 5), ("T1g0", 4), ("T1g1", 5), ("M1g0", 4), ("M1g1", 5),
    ("xT3k0", 6), ("xT3k1", 6), ("RL", 6), ("POS", 6),
]
SPLIT = {j for j, _ in JOBS if j[:2] in ("xT", "AT", "T0", "T1", "S1", "S2", "E1") and not j.startswith("xT3")}
BANK, USE, HI_USE, USES, HI_USES = {}, {}, {}, [0] * 8, [0] * 8
for _j, _b in JOBS:
    USES[_b] += 1
    BANK[_j], USE[_j] = _b, USES[_b]
    if _j in SPLIT:
        HI_USES[_b] += 1
        HI_USE[_j] = HI_USES[_b]

W0 = {}
_at = 0
for _n, _c in [("g0", KD * D), ("g1", KD * D), ("sW1", KD * D), ("eW1", E0 * KD * EH1), ("sW2", KD * P), ("eW2", E0 * P),
               ("sW3", D), ("eW3", 2 * D), ("gW", KD * E0)]:
    W0[_n] = (_at, _c)
    _at += _c
W0_COLS = _at
B0 = {"g0": 0, "g1": D, "sb1": 2 * D, "eb1": 3 * D, "sb2": 3 * D + E0 * EH1}
B0_COLS = 3 * D + E0 * EH1 + P
LOW_ROW = 32


def build(nc, a, out):
    routed = [nc.dram_tensor(f"routed{r}", (E1 * CAP + E1 * P, ROW), fp32, kind="Internal").ap() for r in range(2)]
    bias_parts = nc.dram_tensor("bias_parts", (2, 2 * E1, D), fp32, kind="Internal").ap()

    ctx = ExitStack()
    with ctx:
        def sem(name):
            return ctx.enter_context(nc.semaphore(name))

        def keep(name, shape, dt=fp32, stack=ctx):
            return stack.enter_context(nc.sbuf_tensor(name, shape, dt))

        cst = keep("cst", [P, C_ALL])
        ones_r = keep("ones_r", [P, PT], f32r)
        id_r = keep("id_r", [P, P], f32r)
        sel_r = keep("sel_r", [P, 2 * P], f32r)
        tri_b = keep("tri_b", [P, P], bf16)
        ones_b = keep("ones_b", [P, P], bf16)
        w0h = keep("w0h", [P, W0_COLS], f32r)
        w0l = keep("w0l", [P, W0_COLS], f32r)
        brow = keep("brow", [P, B0_COLS], f32r)
        o_bias = keep("o_bias", [P, D], f32r)
        eb2 = keep("eb2", [P, 2])
        rW = keep("rW", [P, KD, E1])
        gb = keep("gb", [P, E0])
        base = keep("base", [P, R])
        tok = keep("tok", [P, T])
        minus_half = keep("minus_half", [P, 16])
        mask_rows = keep("mask_rows", [P, P])
        mask_cols = keep("mask_cols", [P, P])
        idx_credit = keep("idx_credit", [P, 4 + 8])
        cnt_i = keep("cnt_i", [P, 3 * R], i32)
        cnt_f = keep("cnt_f", [P, 4 * R])

        stage_stack = ExitStack()
        stage = keep("stage", [P, W0_COLS], fp32, stage_stack)
        bstage = keep("bstage", [P, B0_COLS], fp32, stage_stack)
        btmp = keep("btmp", [P, B0_COLS], f32r, stage_stack)
        ostage = keep("ostage", [16, D], fp32, stage_stack)
        ohi = keep("ohi", [16, D], f32r, stage_stack)
        olo = keep("olo", [16, D], f32r, stage_stack)
        otmp = keep("otmp", [16, D], fp32, stage_stack)
        mb_stage = keep("mb_stage", [2 * E1, D], fp32, stage_stack)
        mb_hi = keep("mb_hi", [2 * E1, D], f32r, stage_stack)
        mb_lo = keep("mb_lo", [2 * E1, D], f32r, stage_stack)
        stage_stack.close()
        A = ExitStack()

        def ka(name, shape, dt=fp32):
            return keep(name, shape, dt, A)

        xnY = ka("xnY", [P, T, D])
        xThY, xTlY = ka("xThY", [P, KD, PT], f32r), ka("xTlY", [P, KD, PT], f32r)
        ThY, TlY = ka("ThY", [P, T, D], f32r), ka("TlY", [P, T, D], f32r)
        xT3 = ka("xT3", [P, KD, PT])
        xo = ka("xo", [P, T, D])
        pay = [ka(f"pay_{s}", [P, T, ROW]) for s in range(2)]
        x = [ka(f"x_{s}", [P, T, D]) for s in range(RING)]
        adj = [ka(f"adj_{s}", [P, T, N]) for s in range(2)]
        ATh = [ka(f"ATh_{s}", [P, 2, 2, N], f32r) for s in range(RING)]
        ATl = [ka(f"ATl_{s}", [P, 2, 2, N], f32r) for s in range(RING)]
        junk = ka("junk", [P, T, N], bf16)
        xnA = ka("xnA", [P, T, D])
        xThA, xTlA = ka("xThA", [P, KD, PT], f32r), ka("xTlA", [P, KD, PT], f32r)
        ThA, TlA = ka("ThA", [P, T, D], f32r), ka("TlA", [P, T, D], f32r)
        xnB = ka("xnB", [P, T, D])
        xThB, xTlB = ka("xThB", [P, KD, PT], f32r), ka("xTlB", [P, KD, PT], f32r)
        hh, hl = ka("hh", [P, 4, PT], f32r), ka("hl", [P, 4, PT], f32r)
        gh, gl = hh[:, 2:4, :], hl[:, 2:4, :]
        s2h, s2l = ka("s2h", [P, PT], f32r), ka("s2l", [P, PT], f32r)
        ef = ka("ef", [P, 2, PT])
        cbT = ka("cbT", [P, PT], f32r)
        cb = ka("cb", [P, T, 16], f32r)
        st = {q: ka("st" + q, [P, T, 6]) for q in "0123"}
        mv = {q: ka("mv" + q, [P, T, 2]) for q in "0123"}
        vp = {q: ka("vp" + q, [P, 16]) for q in "0123"}
        rs = {q: ka("rs" + q, [P, 16]) for q in "0123"}
        deg, dz, nz = ka("deg", [P, T]), ka("dz", [P, T]), ka("nz", [P, T])
        dsc = [ka(f"dsc_{s}", [P, 3, T]) for s in range(RING)]
        ch = {n: ka("ch_" + n, [P, 2 * T, E1]) for n in ("lg", "key", "ex", "pr", "r1", "oh1", "r2", "oh2", "msk", "w", "c")}
        cs = {n: ka("cs_" + n, [P, 2 * T]) for n in ("m", "s", "rs", "a", "b", "m2", "s2", "rs2")}
        rt = {n: ka("rt_" + n, [P, T, c]) for n, c in (("pos", R), ("q1", E1), ("q2", E1))}
        mb = ka("mb", [P, T, R], bf16)
        idx_f = ka("idx_f", [P, 2, T])
        idx = [ka(f"idx_{s}", [P, 2, T], i32) for s in range(2)]
        A.close()

        C = ExitStack()
        tab_i = keep("tab_i", [P, 2 * TILES], i32, C)
        tab_f = keep("tab_f", [P, 2 * TILES], fp32, C)
        def kc(name, shape, dt=fp32):
            return keep(name, shape, dt, C)

        WC = 2 * KD * D
        b1r = kc("b1r", [P, 2 * E1 * D], f32r)
        U, UT = 4, 2
        TURNS_C = TILES // (U * UT)
        g = [kc(f"g_{u}", [P, UT, ROW]) for u in range(U)]
        wsel = [kc(f"wsel_{u}", [P, UT, 2]) for u in range(U)]
        isel = [kc(f"isel_{u}", [P, UT, 2], i32) for u in range(U)]
        S = ExitStack()
        keep("leaving", [P, 8 * E1 * P], fp32, S)
        mstage = keep("mstage", [P, E1 * WC], fp32, S)
        w1h = keep("w1h", [P, E1 * WC], f32r, S)
        B = ExitStack()
        scratch = [[keep(n, [P, NJ, E1], fp32, B) for n in ("ends_before_0", "jumps_0")]]
        B.close()
        w1l = keep("w1l", [P, E1 * WC], f32r, S)
        S.close()
        gTh = [kc(f"gTh_{u}", [P, UT * D], f32r) for u in range(U)]
        gTl = [kc(f"gTl_{u}", [P, UT * D], f32r) for u in range(U)]
        hf = [kc(f"hf_{u}", [P, UT * D]) for u in range(U)]
        hTh = [kc(f"hTh_{u}", [P, UT * D], f32r) for u in range(U)]
        hTl = [kc(f"hTl_{u}", [P, UT * D], f32r) for u in range(U)]
        ysb = [kc(f"ysb_{u}", [P, UT, D]) for u in range(U)]
        scratch.append([kc(n, [P, NJ, E1]) for n in ("ends_before_1", "jumps_1")])
        C.close()

        ps = [ctx.enter_context(nc.psum_tensor(f"bank{b}", [P, 512], fp32)) for b in range(8)]

        bank_full = [sem(f"bank_full{b}") for b in range(8)]
        hi_done = [sem(f"hi_done{b}") for b in range(8)]
        bank_free = [sem(f"bank_free{b}") for b in range(8)]
        w_loaded, w_hi, w_ready = sem("w_loaded"), sem("w_hi"), sem("w_ready")
        mb_kept = sem("mb_kept")
        bias_loaded = sem("bias_loaded")
        misc = sem("setup_steps")
        x_loaded, adj_loaded = [sem(f"x_loaded{s}") for s in range(RING)], [sem(f"adj_loaded{s}") for s in range(2)]
        deg_ready = sem("deg_ready")
        var_ready = {q: sem("var_ready" + q) for q in "0123"}
        rstd_ready = {q: sem("rstd_ready" + q) for q in "0123"}
        xn_ready = {q: sem("xn_ready" + q) for q in "0123"}
        scale_ready = sem("scale_ready")
        x1_ready, x3_ready, x3_summed = sem("x1_ready"), sem("x3_ready"), sem("x3_summed")
        shift_ready, exp_ready, diff_ready, exp2_ready, cb_ready = (sem(s) for s in ("shift_ready", "exp_ready", "diff_ready", "exp2_ready", "cb_ready"))
        gh_ready, gl_ready = sem("gh_ready"), sem("gl_ready")
        mask_ready, idx_ready = sem("mask_ready"), sem("idx_ready")
        choice_steps, dz_ready = sem("choice_steps"), sem("dz_ready")
        pow_ready = {q: sem("pow_ready" + q) for q in "0123"}
        st_ready, mv_ready = {q: sem("st_ready" + q) for q in "0123"}, {q: sem("mv_ready" + q) for q in "0123"}
        scattered = [sem(f"scattered{s}") for s in range(2)]
        x3_stored = sem("x3_stored")

        counts_ready, padded, table_ready = sem("counts_ready"), sem("padded"), sem("table_ready")
        m_loaded, mw_hi, mw_ready = sem("m_loaded"), sem("mw_hi"), sem("mw_ready")
        mw_loaded = [sem(f"mw_loaded{h}") for h in range(4)]
        slot_used = [sem(f"slot_used{s}") for s in range(U)]
        g_loaded = [sem(f"g_loaded{s}") for s in range(U)]
        returned = [sem(f"returned{s}") for s in range(U)]
        gT_hi, gT_lo = [sem(f"gT_hi{s}") for s in range(U)], [sem(f"gT_lo{s}") for s in range(U)]
        hf_ready = [sem(f"hf_ready{s}") for s in range(U)]
        hT_hi, hT_lo = [sem(f"hT_hi{s}") for s in range(U)], [sem(f"hT_lo{s}") for s in range(U)]
        y_ready = [sem(f"y_ready{s}") for s in range(U)]
        pe_c = [sem(f"tile_products{s}") for s in range(U)]
        sel_ready = [sem(f"sel_ready{s}") for s in range(U)]

        dve_setup, a_done, m_clear, b_steps, mb_steps = (sem(n) for n in ("dve_setup", "a_done", "m_clear", "b_steps", "mb_steps"))
        mask_turned, mask_loaded, held = sem("mask_turned"), sem("mask_loaded"), sem("held")

        block = ctx.enter_context(nc.Block())

        def val(n, per, k):
            turn, a_turn, first = n
            return first * per + k if a_turn == 0 else turn * (a_turn * per) + (first * per + k)

        def ago(n, d):
            return n[0], n[1], n[2] - d

        def slot(n, ring=RING):
            return n[2] % ring

        def rows_of(n, per, count):
            return bass.ds(val(n, per, 0), count)

        def w0(half, name, lo, cols):
            c0, _ = W0[name]
            return (w0h, w0l)[half][:, c0 + lo:c0 + lo + cols]

        def b3(ap, n):
            return ap.unsqueeze(2).to_broadcast([P, T, n])

        def hold(eng):
            eng.sem_inc(held, 1)

        def loaded(engine, table, first, count, most):
            return nc.values_load_multi_w_load_instructions(table[0:1, bass.ds(first, count)], engines=(engine,), min_val=0, max_val=most)[1]

        STEPS = PAIRS + RING - 1
        FIRST = RING
        TURNS = (PAIRS - 1 - FIRST) // RING

        def over_steps(eng, step):
            for k in range(FIRST):
                step((None, 0, k))
            with eng.Fori(0, TURNS) as j:
                for u in range(RING):
                    step((j, RING, FIRST + u))
            for k in range(FIRST + TURNS * RING, STEPS):
                step((None, 0, k))

        def adj_value(n):
            return 16 * (n[2] // 2) + 16 if n[1] == 0 else n[0] * (16 * n[1] // 2) + 16 * (n[2] // 2) + 16

        def x_value(n):
            return 16 * (n[2] // RING) + 16 if n[1] == 0 else n[0] * 16 + 16 * (n[2] // RING) + 16

        def scatter_value(n):
            each = 2 * T * 16
            return each * (n[2] // 2) + each if n[1] == 0 else n[0] * (each * n[1] // 2) + each * (n[2] // 2) + each

        def active(n):
            return n[1] != 0 or 0 <= n[2] < PAIRS

        def starts(n):
            return n[2] + 1 < PAIRS if n[1] == 0 else True

        @block.sync
        def _(sp):
            sp.dma_start(cst[:, :], a["consts"]).then_inc(misc, 16)
            sp.dma_start(mask_rows[:, :], a["nodemask"]).then_inc(mask_loaded, 16)
            col = lambda name: stage[:, W0[name][0]:W0[name][0] + W0[name][1]]
            kp = lambda ap: ap.rearrange("(k p) n -> p k n", p=P)
            k2 = lambda ap, k: ap.rearrange("p (k n) -> p k n", k=k)
            sp.dma_start(k2(col("g0"), KD), kp(a["g0W"])).then_inc(w_loaded, 16)
            sp.dma_start(k2(col("g1"), KD), kp(a["g1W"])).then_inc(w_loaded, 16)
            sp.dma_start(k2(col("sW1"), KD), kp(a["sW1"])).then_inc(w_loaded, 16)
            sp.dma_start(k2(col("sW2"), KD), kp(a["sW2"])).then_inc(w_loaded, 16)
            sp.dma_start(col("sW3"), a["sW3"]).then_inc(w_loaded, 16)
            sp.dma_start(k2(col("eW3"), 2), a["eW3"].rearrange("(b e) g o -> (e g) b o", b=2)).then_inc(w_loaded, 16)
            sp.dma_start(k2(col("gW"), KD), kp(a["gW"])).then_inc(w_loaded, 16)
            for e in range(E0):
                sp.dma_start(k2(col("eW1")[:, e * D:(e + 1) * D], KD), kp(a["eW1"][e])).then_inc(w_loaded, 16)
                c0 = e * P + (e % 2) * EH2
                if e == 0:
                    sp.wait_ge(w_ready, 1)
                sp.dma_start(col("eW2")[:, c0:c0 + EH2], a["eW2"][e]).then_inc(w_loaded, 16)
            sp.dma_start(rW[:, :, :], kp(a["rW"])).then_inc(w_loaded, 16)
            def load(n):
                rows = rows_of(n, PT, PT)
                sp.dma_start(x[slot(n)][:, :, :], a["x"][rows, :].rearrange("(t p) f -> p t f", p=P)).then_inc(x_loaded[slot(n)], 16)

            def load_adj(n):
                rows = rows_of(n, PT, PT)
                sp.dma_start(adj[slot(n, 2)][:, :, :], a["adj"][rows, :].rearrange("(t p) f -> p t f", p=P)).then_inc(adj_loaded[slot(n, 2)], 16)

            fillers = cst[:, C_PAD:C_PAD + ROW]
            sp.wait_ge(w_loaded, 16 * 16)
            sp.wait_ge(misc, 16)
            for r in range(2):
                for e in range(E1):
                    sp.dma_start(routed[r][E1 * CAP + e * P:E1 * CAP + (e + 1) * P, :], fillers).then_inc(padded, 16)
            sp.wait_ge(mb_steps, 1)
            for i, part in enumerate((mb_hi, mb_lo)):
                sp.dma_start(bias_parts[i], part[:, :].bitcast(fp32)).then_inc(mb_kept, 16)

            def load_experts():
                last, quarter = (None, 0, PAIRS - 1), E1 // 4
                sp.wait_ge(bank_free[BANK["M1g1"]], val(last, USES[BANK["M1g1"]], USE["M1g1"] + 1))
                for h in range(4):
                    experts = mstage[:, h * quarter * WC:(h + 1) * quarter * WC].rearrange("p (e w k n) -> p e w k n", e=quarter, w=2, k=KD)
                    for w, name in enumerate(("w1", "w2")):
                        for e in range(quarter):
                            sp.dma_start(experts[:, e, w, :, :], kp(a[name][h * quarter + e])).then_inc(mw_loaded[h], 16)

            def step(k):
                d, nxt = ago(k, 3), ago(k, -1)
                if k[1] == 0 and k[2] == STEPS - 1:
                    load_experts()
                if starts(k):
                    if k[1] != 0 or k[2] >= 1:
                        sp.wait_ge(bank_full[BANK["ATg1"]], val(ago(k, 1), USES[BANK["ATg1"]], USE["ATg1"]))
                        hold(sp)
                        sp.wait_ge(deg_ready, val(ago(k, 1), 1, 1))
                        hold(sp)
                    load_adj(nxt)
                if active(d):
                    sp.wait_ge(x3_summed, val(d, 1, 1))
                    hold(sp)
                    sp.dma_start(out[rows_of(d, PT, PT), :].rearrange("(t p) f -> p t f", p=P), xo[:, :, :]).then_inc(x3_stored, 16)
                if starts(k):
                    load(nxt)

            over_steps(sp, step)

            sp.wait_ge(counts_ready, 1)
            for r in range(2):
                for row in loaded(mybir.EngineType.SP, cnt_i, r * E1, E1, E1 * CAP):
                    sp.dma_start(routed[r][bass.ds(row, P), :], fillers).then_inc(padded, 16)
            for s in range(2):
                sp.wait_ge(scattered[s], (PAIRS // 2 + 1) * 2 * T * 16)
            sp.wait_ge(x3_stored, (PAIRS + 1) * 16)
            sp.sem_inc(a_done, 1)
            sp.wait_ge(m_clear, 1)
            sp.wait_ge(mb_kept, 2 * 16)
            for i, row in enumerate((0, LOW_ROW)):
                sp.dma_start(b1r[row:row + 1, :].bitcast(fp32), bias_parts[i].rearrange("(a e) n -> a (e n)", a=1)).then_inc(m_loaded, 16)
            sp.wait_ge(padded, 2 * R * 16)

            sp.wait_ge(table_ready, 1)
            for r in range(2):
                if r == 1:
                    sp.wait_ge(table_ready, 2)
                with sp.Fori(0, TURNS_C // 2) as j:
                    t = j + r * (TURNS_C // 2)
                    for u in range(U):
                        sp.wait_ge(slot_used[u], t + 1)
                        hold(sp)
                        for i, row in enumerate(loaded(mybir.EngineType.SP, tab_i, t * (U * UT) + u * UT, UT, E1 * CAP + (E1 - 1) * P)):
                            sp.dma_start(g[u][:, i, :], routed[r][bass.ds(row, P), :]).then_inc(g_loaded[u], 16)
            for u in range(U):
                sp.wait_ge(returned[u], (TURNS_C + 1) * UT * 16)

        @block.scalar
        def _(act):
            def freed(job, n, ins):
                ins.then_inc(bank_free[BANK[job]], 1)

            def full(job, n):
                act.wait_ge(bank_full[BANK[job]], val(n, USES[BANK[job]], USE[job]))

            def high(job, n, dst, func=ACT.Copy):
                full(job, n)
                nc.scalar.activation(dst, ps[BANK[job]][:, :], func).then_inc(hi_done[BANK[job]], 1)

            def high_scaled(job, n, dst, gph, d):
                full(job, n)
                for i in range(2):
                    t = 2 * gph + i
                    ins = nc.scalar.activation(dst[:, t, :], ps[BANK[job]][:, i * D:(i + 1) * D], ACT.Copy, scale=d[:, t:t + 1])
                ins.then_inc(hi_done[BANK[job]], 1)

            def expert_out(i, n):
                job = f"EP{i}"
                full(job, n)
                nc.scalar.activation(ef[:, i, :], ps[BANK[job]][:, :], ACT.Relu, bias=eb2[:, i:i + 1]).then_inc(bank_free[BANK[job]], 1)

            def conv_out(job, n, dst, gph, d):
                full(job, n)
                for i in range(2):
                    t = 2 * gph + i
                    ins = nc.scalar.activation(dst[:, t, :], ps[BANK[job]][:, i * D:(i + 1) * D], ACT.Relu, scale=d[:, t:t + 1])
                ins.then_inc(bank_free[BANK[job]], 1)

            def norm(n, q, src, dst):
                act.wait_ge(rstd_ready[q], val(n, 1, 1))
                for t in range(T):
                    ins = nc.scalar.activation(dst[:, t, 0:D], src[:, t, :], ACT.Identity, scale=rs[q][:, t:t + 1], bias=rs[q][:, 12 + t:13 + t])
                ins.then_inc(xn_ready[q], 1)

            def degrees(n):
                act.wait_ge(adj_loaded[slot(n, 2)], adj_value(n))
                for t in range(T):
                    ins = nc.scalar.activation(junk[:, t, :], adj[slot(n, 2)][:, t, :], ACT.Copy, accum_out=deg[:, t:t + 1])
                ins.then_inc(deg_ready, 1)

            def lead_rows(n):
                for i in range(KD):
                    high(f"xT0k{i}", n, xThA[:, i, :])

            def lead_adj(n):
                for q in range(2):
                    high(f"ATg{q}", n, ATh[slot(n)][:, q, :, :].rearrange("p a b -> p (a b)"))

            def router_in(n, i):
                job = f"xT3k{i}"
                full(job, n)
                nc.scalar.activation(xT3[:, i, :], ps[BANK[job]][:, :], ACT.Copy).then_inc(bank_free[BANK[job]], 1)

            def step(k):
                a, b, c, d, nxt = k, ago(k, 1), ago(k, 2), ago(k, 3), ago(k, -1)
                A, B, C_, D_ = active(a), active(b), active(c), active(d)
                if k[1] == 0 and k[2] == 0:
                    act.wait_ge(x_loaded[0], 16)
                    norm(a, "0", x[0], xnA)
                    lead_rows(a)
                    lead_adj(a)
                if A:
                    act.wait_ge(scale_ready, val(a, 1, 1))
                    high_scaled("T0g0", a, ThA, 0, dsc[slot(a)][:, 0, :])
                if B:
                    for i in range(KD):
                        high(f"xT1k{i}", b, xThB[:, i, :])
                if D_:
                    router_in(d, 0)
                if A:
                    high_scaled("T0g1", a, ThA, 1, dsc[slot(a)][:, 0, :])
                if D_:
                    router_in(d, 1)
                if starts(k):
                    degrees(nxt)
                if C_:
                    norm(c, "2", x[slot(c)], xnY)
                if B:
                    for m in range(2):
                        high(f"S1m{m}", b, hh[:, m, :], ACT.Relu)
                if B or D_:
                    act.wait_ge(shift_ready, val(b, 1, 1))
                    nc.scalar.activation(ch["ex"][:, :, :], ch["key"][:, :, :], ACT.Exp).then_inc(exp_ready, 1)
                if A:
                    for q in range(2):
                        conv_out(f"M0g{q}", a, xnA, q, dsc[slot(a)][:, 0, :])
                if C_:
                    for i in range(KD):
                        high(f"xT2k{i}", c, xThY[:, i, :])
                if B:
                    for i in range(2):
                        high(f"E1e{i}", b, hh[:, 2 + i, :], ACT.Relu)
                    high("S2", b, s2h[:, :], ACT.Relu)
                if B or D_:
                    act.wait_ge(diff_ready, val(b, 1, 1))
                    nc.scalar.activation(ch["pr"][:, 0:T, :], ch["w"][:, 0:T, :], ACT.Exp).then_inc(exp2_ready, 1)
                if C_:
                    for q in range(2):
                        high_scaled(f"T1g{q}", c, ThY, q, dsc[slot(c)][:, 1, :])
                if B:
                    high("E1e2", b, hh[:, 0, :], ACT.Relu)
                    expert_out(0, b)
                    high("E1e3", b, hh[:, 1, :], ACT.Relu)
                if starts(k):
                    norm(nxt, "0", x[slot(nxt)], xnA)
                if B:
                    full("CBT", b)
                    nc.scalar.activation(cbT[0:16, :], ps[BANK["CBT"]][0:16, :], ACT.Copy).then_inc(bank_free[BANK["CBT"]], 1)
                if C_:
                    for q in range(2):
                        conv_out(f"M1g{q}", c, xnY, q, dsc[slot(c)][:, 2, :])
                if B:
                    expert_out(1, b)
                    for i in range(2):
                        act.wait_ge(bank_free[BANK[f"G{i}"]], val(b, USES[BANK[f"G{i}"]], USE[f"G{i}"] + 1))
                        nc.scalar.activation(gh[:, i, :], ef[:, i, :], ACT.Copy).then_inc(gh_ready, 1)
                if starts(k):
                    lead_rows(nxt)
                if A:
                    norm(a, "1", x[slot(a)], xnB)
                if starts(k):
                    lead_adj(nxt)
                if C_:
                    act.wait_ge(scattered[slot(c, 2)], scatter_value(c))
                    norm(c, "3", x[slot(c)], pay[slot(c, 2)])

            rows = bass.ds(0, PT)
            act.dma_start(adj[0][:, :, :], a["adj"][rows, :].rearrange("(t p) f -> p t f", p=P)).then_inc(adj_loaded[0], 16)
            act.dma_start(x[0][:, :, :], a["x"][rows, :].rearrange("(t p) f -> p t f", p=P)).then_inc(x_loaded[0], 16)
            act.wait_ge(w_ready, 2)
            for row in (0, LOW_ROW):
                for name, src in (("g0", a["g0b"]), ("g1", a["g1b"]), ("sb1", a["sb1"]), ("eb1", a["eb1"]), ("sb2", a["sb2"])):
                    flat = src if len(src.shape) == 1 else src.rearrange("e n -> (e n)")
                    n = flat.shape[0]
                    act.dma_start(bstage[row:row + 1, B0[name]:B0[name] + n], flat.rearrange("(a n) -> a n", a=1)).then_inc(bias_loaded, 16)
            for r0 in (0, 4, 8):
                act.dma_start(ostage[r0:r0 + 4, :], a["eb3"]).then_inc(bias_loaded, 16)
            for r0 in (12, 13):
                act.dma_start(ostage[r0:r0 + 1, :], a["sb3"].rearrange("(a n) -> a n", a=1)).then_inc(bias_loaded, 16)
            for b in range(2):
                act.dma_start(eb2[:, b:b + 1], a["eb2"].rearrange("e (g a) -> (e g) a", a=1)[b * P:(b + 1) * P, :]).then_inc(bias_loaded, 16)
            act.dma_start(gb[:, :], a["gb"].rearrange("(a n) -> a n", a=1).to_broadcast([P, E0])).then_inc(bias_loaded, 16)

            for w, name in enumerate(("b1", "b2")):
                act.dma_start(mb_stage[w * E1:(w + 1) * E1, :], a[name]).then_inc(bias_loaded, 16)
            degrees((None, 0, 0))
            act.wait_ge(w_loaded, 16 * 16)
            for i in range(4):
                cols = slice(i * W0_COLS // 4, (i + 1) * W0_COLS // 4)
                nc.scalar.activation(w0h[:, cols], stage[:, cols], ACT.Copy).then_inc(w_hi, 1)
            act.wait_ge(mb_kept, 2 * 16)
            over_steps(act, step)

            quarter = E1 // 4
            for h in range(4):
                act.wait_ge(mw_loaded[h], 16 * 2 * quarter)
                cols = slice(h * quarter * WC, (h + 1) * quarter * WC)
                nc.scalar.activation(w1h[:, cols], mstage[:, cols], ACT.Copy).then_inc(mw_hi, 1)
            for u in range(U):
                act.sem_inc(y_ready[u], 1)

            def rows_high(t, u):
                act.wait_ge(pe_c[u], t * 4 + 1)
                nc.scalar.activation(gTh[u][:, :], ps[2 * u][:, :], ACT.Copy).then_inc(gT_hi[u], 1)

            def weighted(t, u):
                act.wait_ge(pe_c[u], t * 4 + 4)
                act.wait_ge(sel_ready[u], t + 1)
                act.wait_ge(returned[u], t * (UT * 16) + UT * 16)
                for i in range(UT):
                    ins = nc.scalar.activation(ysb[u][:, i, :], ps[2 * u + 1][:, i * D:(i + 1) * D], ACT.Copy, scale=wsel[u][:, i, 0:1])
                ins.then_inc(y_ready[u], 1)

            def turn_c(t, more):
                def gelu(u):
                    act.wait_ge(pe_c[u], t * 4 + 2)
                    nc.scalar.activation(hf[u][:, :], ps[2 * u + 1][:, :], ACT.Gelu).then_inc(hf_ready[u], 1)

                def hidden_high(u):
                    act.wait_ge(pe_c[u], t * 4 + 3)
                    nc.scalar.activation(hTh[u][:, :], ps[2 * u][:, :], ACT.Copy).then_inc(hT_hi[u], 1)

                for u in range(U - 1):
                    gelu(u)
                hidden_high(0)
                gelu(U - 1)
                for u in range(1, U):
                    hidden_high(u)
                for pair in ((0, 1), (2, 3)):
                    for u in pair:
                        weighted(t, u)
                    for u in pair if more else ():
                        rows_high(t + 1, u)

            for u in range(U):
                rows_high(0, u)
            with act.Fori(0, TURNS_C - 1) as j:
                turn_c(j, True)
            turn_c(TURNS_C - 1, False)

        @block.vector
        def _(dve):
            V = nc.vector

            def low(job, n, dst, hi, op=None):
                dve.wait_ge(hi_done[BANK[job]], val(n, HI_USES[BANK[job]], HI_USE[job]))
                bank = ps[BANK[job]]
                if op is None:
                    ins = V.tensor_tensor(dst, bank[:, :], hi, ALU.subtract)
                else:
                    ins = V.scalar_tensor_tensor(out=dst, in0=bank[:, :], scalar=0.0, in1=hi, op0=op, op1=ALU.subtract)
                ins.then_inc(bank_free[BANK[job]], 1)

            def low_scaled(job, n, dst, hi, gph, d):
                dve.wait_ge(hi_done[BANK[job]], val(n, HI_USES[BANK[job]], HI_USE[job]))
                for i in range(2):
                    t = 2 * gph + i
                    ins = V.scalar_tensor_tensor(out=dst[:, t, :], in0=ps[BANK[job]][:, i * D:(i + 1) * D], scalar=d[:, t:t + 1],
                                                 in1=hi[:, t, :].bitcast(fp32), op0=ALU.mult, op1=ALU.subtract)
                ins.then_inc(bank_free[BANK[job]], 1)

            def stats(n, q, src):
                for t in range(T):
                    ins = V.bn_stats(st[q][:, t, :], src[:, t, :])
                ins.then_inc(st_ready[q], 1)
                dve.wait_ge(st_ready[q], val(n, 1, 1))
                hold(dve)
                for t in range(T):
                    ins = V.bn_aggr(mv[q][:, t, :], st[q][:, t, :])
                ins.then_inc(mv_ready[q], 1)
                dve.wait_ge(mv_ready[q], val(n, 1, 1))
                V.tensor_scalar(vp[q][:, 12:16], mv[q][:, :, 0], -1.0, None, ALU.mult)
                V.tensor_scalar(vp[q][:, 0:T], mv[q][:, :, 1], LN_EPS, None, ALU.add).then_inc(var_ready[q], 1)

            def degree_factors(n):
                dve.wait_ge(deg_ready, val(n, 1, 1))
                V.tensor_scalar(dz[:, :], deg[:, :], 0.0, None, ALU.is_equal).then_inc(dz_ready, 1)
                dve.wait_ge(dz_ready, val(n, 1, 1))
                V.tensor_tensor(vp["0"][:, 4:8], deg[:, :], dz[:, :], ALU.add)
                V.tensor_scalar(nz[:, :], dz[:, :], -1.0, 1.0, ALU.mult, ALU.add)
                V.tensor_scalar(vp["0"][:, 8:12], deg[:, :], 1.0, DEG_EPS, ALU.add, ALU.add).then_inc(var_ready["0"], 1)

            def scales(n):
                dve.wait_ge(rstd_ready["0"], val(n, 1, 1))
                s = slot(n)
                V.tensor_tensor(dsc[s][:, 0, :], rs["0"][:, 4:8], nz[:, :], ALU.mult)
                V.tensor_copy(dsc[s][:, 1, :], rs["0"][:, 8:12])
                V.tensor_tensor(dsc[s][:, 2, :], rs["0"][:, 8:12], mask_cols[:, rows_of(n, T, T)], ALU.mult).then_inc(scale_ready, 1)

            CHOICE_STEPS = 30

            def choices(b, d, B, D_):
                k = [0]

                def after(ins):
                    k[0] += 1
                    ins.then_inc(choice_steps, 1)

                def settle():
                    dve.wait_ge(choice_steps, val(b, CHOICE_STEPS, k[0]))

                r8 = cst[:, C_REV8:C_REV8 + E1].unsqueeze(1).to_broadcast([P, 2 * T, E1])
                b8 = lambda ap: ap.unsqueeze(2).to_broadcast([P, 2 * T, E1])
                if B:
                    job = "GL"
                    dve.wait_ge(bank_full[BANK[job]], val(b, USES[BANK[job]], USE[job]))
                    V.tensor_tensor(ch["lg"][:, 0:T, 0:E0], ps[BANK[job]][:, 0:T * E0].rearrange("p (t e) -> p t e", t=T),
                                    gb[:, :].unsqueeze(1).to_broadcast([P, T, E0]), ALU.add).then_inc(bank_free[BANK[job]], 1)
                    dve.wait_ge(bank_free[BANK[job]], val(b, USES[BANK[job]], USE[job] + 1))
                if D_:
                    job = "RL"
                    dve.wait_ge(bank_full[BANK[job]], val(d, USES[BANK[job]], USE[job]))
                    V.tensor_copy(ch["lg"][:, T:2 * T, :], ps[BANK[job]][:, 0:T * E1].rearrange("p (t e) -> p t e", t=T))\
                        .then_inc(bank_free[BANK[job]], 1)
                    dve.wait_ge(bank_free[BANK[job]], val(d, USES[BANK[job]], USE[job] + 1))
                yield
                after(V.tensor_reduce(cs["m"][:, :], ch["lg"][:, :, :], axis=AX.X, op=ALU.max))
                settle()
                after(V.tensor_tensor(ch["r1"][:, :, :], ch["lg"][:, :, :], b8(cs["m"][:, :]), ALU.subtract))
                settle()
                V.tensor_scalar(ch["key"][:, :, :], ch["r1"][:, :, :], KEY_FLOOR, None, ALU.max).then_inc(shift_ready, 1)
                dve.wait_ge(shift_ready, val(b, 1, 1))
                after(V.scalar_tensor_tensor(out=ch["r1"][:, :, :], in0=ch["key"][:, :, :], scalar=0.0, in1=r8, op0=ALU.is_equal, op1=ALU.mult))
                yield
                settle()
                after(V.tensor_reduce(cs["a"][:, :], ch["r1"][:, :, :], axis=AX.X, op=ALU.max))
                settle()
                after(V.tensor_tensor(ch["oh1"][:, :, :], ch["r1"][:, :, :], b8(cs["a"][:, :]), ALU.is_equal))
                yield
                settle()
                after(V.scalar_tensor_tensor(out=ch["r1"][:, :, :], in0=ch["oh1"][:, :, :], scalar=-1000.0, in1=ch["key"][:, :, :], op0=ALU.mult, op1=ALU.add))
                settle()
                after(V.tensor_reduce(cs["m2"][:, :], ch["r1"][:, :, :], axis=AX.X, op=ALU.max))
                yield
                settle()
                after(V.tensor_tensor(ch["r2"][:, :, :], ch["r1"][:, :, :], b8(cs["m2"][:, :]), ALU.is_equal))
                settle()
                after(V.tensor_tensor(ch["r1"][:, :, :], ch["r2"][:, :, :], r8, ALU.mult))
                yield
                settle()
                after(V.tensor_reduce(cs["b"][:, :], ch["r1"][:, :, :], axis=AX.X, op=ALU.max))
                dve.wait_ge(exp_ready, val(b, 1, 1))
                after(V.reduce_sum(cs["s"][:, :], ch["ex"][:, :, :], axis=AX.X))
                yield
                settle()
                after(V.tensor_tensor(ch["oh2"][:, :, :], ch["r1"][:, :, :], b8(cs["b"][:, :]), ALU.is_equal))
                after(V.reciprocal(cs["rs"][:, :], cs["s"][:, :]))
                yield
                settle()
                if D_:
                    V.tensor_copy(mb[:, :, 0:E1], ch["oh1"][:, T:2 * T, :])
                    V.tensor_copy(mb[:, :, E1:R], ch["oh2"][:, T:2 * T, :]).then_inc(mask_ready, 1)
                after(V.tensor_tensor(ch["msk"][:, :, :], ch["oh1"][:, :, :], ch["oh2"][:, :, :], ALU.add))
                after(V.tensor_tensor(ch["pr"][:, :, :], ch["ex"][:, :, :], b8(cs["rs"][:, :]), ALU.mult))
                settle()
                V.tensor_tensor(ch["w"][:, 0:T, :], ch["pr"][:, 0:T, :], cs["rs"][:, 0:T].unsqueeze(2).to_broadcast([P, T, E1]), ALU.subtract)\
                    .then_inc(diff_ready, 1)
                yield
                dve.wait_ge(exp2_ready, val(b, 1, 1))
                after(V.tensor_tensor(ch["w"][:, :, :], ch["pr"][:, :, :], ch["msk"][:, :, :], ALU.mult))
                settle()
                after(V.reduce_sum(cs["s2"][:, :], ch["w"][:, :, :], axis=AX.X))
                yield
                settle()
                after(V.tensor_scalar(cs["a"][:, :], cs["s2"][:, :], 1e-12, None, ALU.max))
                settle()
                after(V.reciprocal(cs["rs2"][:, :], cs["a"][:, :]))
                yield
                settle()
                after(V.tensor_tensor(ch["c"][:, :, :], ch["w"][:, :, :], b8(cs["rs2"][:, :]), ALU.mult))
                settle()
                if B:
                    after(V.tensor_copy(cb[:, :, 0:4], ch["c"][:, 0:T, 0:E0]))
                    yield
                    settle()
                    after(V.tensor_copy(cb[:, :, 4:8], cb[:, :, 0:4].bitcast(fp32)))
                    V.tensor_tensor(cb[:, :, 8:12], ch["c"][:, 0:T, 0:E0], cb[:, :, 0:4].bitcast(fp32), ALU.subtract).then_inc(cb_ready, 1)
                else:
                    V.sem_inc(choice_steps, 2)
                    k[0] += 2
                yield
                if D_:
                    s = slot(d, 2)
                    after(V.tensor_copy(pay[s][:, :, D:D + E1], ch["c"][:, T:2 * T, :]))
                    after(V.tensor_copy(pay[s][:, :, D + E1:ROW], tok[:, :].unsqueeze(2).to_broadcast([P, T, E1])))
                    job = "POS"
                    dve.wait_ge(bank_full[BANK[job]], val(d, USES[BANK[job]], USE[job]))
                    after(V.tensor_tensor(rt["pos"][:, :, :], ps[BANK[job]][:, 0:T * R].rearrange("p (t e) -> p t e", t=T),
                                          base[:, :].unsqueeze(1).to_broadcast([P, T, R]), ALU.add))
                    settle()
                    after(V.tensor_tensor(rt["q1"][:, :, :], rt["pos"][:, :, 0:E1], ch["oh1"][:, T:2 * T, :], ALU.mult))
                    after(V.tensor_tensor(rt["q2"][:, :, :], rt["pos"][:, :, E1:R], ch["oh2"][:, T:2 * T, :], ALU.mult))
                    V.tensor_tensor(base[:, :], ps[BANK[job]][:, T * R:(T + 1) * R], base[:, :], ALU.add).then_inc(bank_free[BANK[job]], 1)
                    after(V.tensor_scalar(tok[:, :], tok[:, :], float(PT), None, ALU.add))
                    yield
                    settle()
                    after(V.reduce_sum(idx_f[:, 0, :], rt["q1"][:, :, :], axis=AX.X))
                    after(V.reduce_sum(idx_f[:, 1, :], rt["q2"][:, :, :], axis=AX.X))
                    settle()
                    V.tensor_copy(idx[s][:, :, :], idx_f[:, :, :]).then_inc(idx_ready, 1)
                else:
                    V.sem_inc(choice_steps, 8)
                    k[0] += 8
                assert k[0] == CHOICE_STEPS, k[0]

            def lead_rows(n):
                for i in range(KD):
                    low(f"xT0k{i}", n, xTlA[:, i, :], xThA[:, i, :].bitcast(fp32))

            def lead_adj(n):
                flat = lambda t, q: t[slot(n)][:, q, :, :].rearrange("p a b -> p (a b)")
                for q in range(2):
                    low(f"ATg{q}", n, flat(ATl, q), flat(ATh, q).bitcast(fp32))

            def step(k):
                a, b, c, d, nxt = k, ago(k, 1), ago(k, 2), ago(k, 3), ago(k, -1)
                A, B, C_, D_ = active(a), active(b), active(c), active(d)
                chain = choices(b, d, B, D_) if B or D_ else iter(())
                go = lambda: next(chain, None)
                if k[1] == 0 and k[2] == 0:
                    lead_rows(a)
                    lead_adj(a)
                if A:
                    low_scaled("T0g0", a, TlA, ThA, 0, dsc[slot(a)][:, 0, :])
                if B:
                    for i in range(KD):
                        low(f"xT1k{i}", b, xTlB[:, i, :], xThB[:, i, :].bitcast(fp32))
                if C_:
                    stats(c, "2", x[slot(c)])
                if A:
                    low_scaled("T0g1", a, TlA, ThA, 1, dsc[slot(a)][:, 0, :])
                if B:
                    for m in range(2):
                        low(f"S1m{m}", b, hl[:, m, :], hh[:, m, :].bitcast(fp32), ALU.max)
                go()
                go()
                go()
                for i in range(KD):
                    if C_:
                        low(f"xT2k{i}", c, xTlY[:, i, :], xThY[:, i, :].bitcast(fp32))
                    go()
                for i in range(2):
                    if B:
                        low(f"E1e{i}", b, hl[:, 2 + i, :], hh[:, 2 + i, :].bitcast(fp32), ALU.max)
                    go()
                if starts(k):
                    dve.wait_ge(x_loaded[slot(nxt)], x_value(nxt))
                    stats(nxt, "0", x[slot(nxt)])
                    degree_factors(nxt)
                if B:
                    low("S2", b, s2l[:, :], s2h[:, :].bitcast(fp32), ALU.max)
                go()
                for q in range(2):
                    if C_:
                        low_scaled(f"T1g{q}", c, TlY, ThY, q, dsc[slot(c)][:, 1, :])
                    go()
                for i in range(2):
                    if B:
                        low(f"E1e{2 + i}", b, hl[:, i, :], hh[:, i, :].bitcast(fp32), ALU.max)
                    go()
                go()
                for _ in chain:
                    pass
                if A:
                    dve.wait_ge(x1_ready, val(a, 2, 2))
                    stats(a, "1", x[slot(a)])
                if starts(k):
                    scales(nxt)
                if B:
                    for i in range(2):
                        job = f"G{i}"
                        dve.wait_ge(bank_full[BANK[job]], val(b, USES[BANK[job]], USE[job]))
                        dve.wait_ge(bank_free[BANK[f"EP{i}"]], val(b, USES[BANK[f"EP{i}"]], USE[f"EP{i}"] + 1))
                        V.tensor_tensor(ef[:, i, :], ef[:, i, :], ps[BANK[job]][:, :], ALU.mult).then_inc(bank_free[BANK[job]], 1)
                    for i in range(2):
                        dve.wait_ge(gh_ready, val(b, 2, i + 1))
                        V.tensor_tensor(gl[:, i, :], ef[:, i, :], gh[:, i, :].bitcast(fp32), ALU.subtract).then_inc(gl_ready, 1)
                if starts(k):
                    lead_rows(nxt)
                if C_:
                    dve.wait_ge(x3_ready, val(c, 2, 2))
                    stats(c, "3", x[slot(c)])
                if starts(k):
                    lead_adj(nxt)
                if B:
                    for q in range(2):
                        job = f"O1g{q}"
                        dve.wait_ge(bank_full[BANK[job]], val(b, USES[BANK[job]], USE[job]))
                        half = x[slot(b)][:, 2 * q:2 * q + 2, :].rearrange("p a b -> p (a b)")
                        V.tensor_tensor(half, half, ps[BANK[job]][:, :], ALU.add).then_inc(bank_free[BANK[job]], 1)
                    for q in range(2):
                        dve.wait_ge(bank_free[BANK[f"O1g{q}"]], val(b, USES[BANK[f"O1g{q}"]], USE[f"O1g{q}"] + 1))

            c0, n = W0["eW2"]
            V.memset(stage[:, c0:c0 + n], 0.0).then_inc(w_ready, 1)
            V.memset(bstage[:, :], 0.0)
            V.memset(ostage[:, :], 0.0).then_inc(w_ready, 1)
            V.memset(minus_half[:, :], -0.5)
            V.memset(ch["lg"][:, :, :], KEY_FLOOR)
            V.memset(ch["pr"][:, :, :], 0.0)
            V.memset(cbT[:, :].bitcast(fp32), 0.0)
            V.memset(ones_b[:, :], 1.0)
            V.memset(cb[:, :, :].bitcast(fp32), 0.0)
            V.memset(btmp[:, :].bitcast(fp32), 0.0)
            V.memset(otmp[:, :], 1.0).then_inc(dve_setup, 1)
            dve.wait_ge(dve_setup, 1)
            V.memset(cb[:, :, 12:14].bitcast(fp32), 1.0)
            V.memset(ones_r[:, :].bitcast(fp32), 1.0).then_inc(dve_setup, 1)
            dve.wait_ge(dve_setup, 2)
            dve.wait_ge(misc, 16)
            V.tensor_copy(id_r[:, :], cst[:, C_ID:C_ID + P])
            V.tensor_copy(sel_r[:, :], cst[:, C_SEL:C_SEL + 2 * P])
            V.tensor_copy(tri_b[:, :], cst[:, C_TRI:C_TRI + P])
            V.tensor_copy(base[:, :], cst[:, C_CAP:C_CAP + R])
            V.tensor_copy(tok[:, :], cst[:, C_TOK:C_TOK + T])
            dve.wait_ge(mask_turned, 1)
            V.tensor_copy(mask_cols[:, :], ps[0][:, 0:P]).then_inc(dve_setup, 1)
            dve.wait_ge(dve_setup, 3)
            for b in range(8):
                V.sem_inc(bank_free[b], 1)
            first = (None, 0, 0)
            dve.wait_ge(x_loaded[0], 16)
            stats(first, "0", x[0])
            degree_factors(first)
            scales(first)
            dve.wait_ge(bias_loaded, 16 * 20)
            V.tensor_copy(brow[:, :], bstage[:, :]).then_inc(dve_setup, 1)
            V.tensor_copy(ohi[:, :], ostage[:, :])
            V.tensor_copy(mb_hi[:, :], mb_stage[:, :]).then_inc(dve_setup, 1)
            dve.wait_ge(dve_setup, 5)
            V.tensor_tensor(mb_lo[:, :], mb_stage[:, :], mb_hi[:, :].bitcast(fp32), ALU.subtract).then_inc(mb_steps, 1)
            V.tensor_copy(btmp[LOW_ROW:LOW_ROW + 1, :], brow[LOW_ROW:LOW_ROW + 1, :].bitcast(fp32)).then_inc(dve_setup, 1)
            V.tensor_tensor(olo[:, :], ostage[:, :], ohi[:, :].bitcast(fp32), ALU.subtract).then_inc(dve_setup, 1)
            dve.wait_ge(dve_setup, 7)
            V.tensor_tensor(brow[LOW_ROW:LOW_ROW + 1, :], bstage[LOW_ROW:LOW_ROW + 1, :], btmp[LOW_ROW:LOW_ROW + 1, :].bitcast(fp32), ALU.subtract)
            V.tensor_scalar(otmp[:, :], ohi[:, :].bitcast(fp32), cst[0:16, C_MH:C_MH + 1], None, ALU.mult)
            V.memset(o_bias[:, :].bitcast(fp32), 0.0).then_inc(dve_setup, 1)
            dve.wait_ge(dve_setup, 8)
            V.scalar_tensor_tensor(out=o_bias[0:16, :], in0=olo[:, :].bitcast(fp32), scalar=cst[0:16, C_ML:C_ML + 1], in1=otmp[:, :],
                                   op0=ALU.mult, op1=ALU.add)
            for i in range(4):
                dve.wait_ge(w_hi, i + 1)
                cols = slice(i * W0_COLS // 4, (i + 1) * W0_COLS // 4)
                V.tensor_tensor(w0l[:, cols], stage[:, cols], w0h[:, cols].bitcast(fp32), ALU.subtract).then_inc(w_ready, 1)
            dve.wait_ge(w_ready, 6)

            over_steps(dve, step)

            dve.wait_ge(idx_ready, PAIRS)
            k = [0]

            def b_step(ins):
                k[0] += 1
                ins.then_inc(b_steps, 1)
                dve.wait_ge(b_steps, k[0])

            V.tensor_copy(cnt_i[:, 0:R], base[:, :]).then_inc(counts_ready, 1)
            dve.wait_ge(counts_ready, 1)
            b_step(V.tensor_tensor(cnt_f[:, 0:R], base[:, :], cst[:, C_CAP:C_CAP + R], ALU.subtract))
            b_step(V.tensor_scalar(cnt_f[:, 0:R], cnt_f[:, 0:R], float(P - 1), None, ALU.add))
            b_step(V.tensor_copy(cnt_i[:, R:2 * R], cnt_f[:, 0:R]))
            b_step(V.tensor_scalar(cnt_i[:, 2 * R:3 * R], cnt_i[:, R:2 * R], 7, None, ALU.logical_shift_right))
            b_step(V.tensor_copy(cnt_f[:, R:2 * R], cnt_i[:, 2 * R:3 * R]))
            b_step(V.tensor_scalar(cnt_f[:, R:2 * R], cnt_f[:, R:2 * R], float(P), None, ALU.mult))
            b_step(V.tensor_copy(cnt_f[:, 2 * R:3 * R], cnt_f[:, R:2 * R]))
            rows_to = cnt_f[:, 2 * R:3 * R].rearrange("p (r e) -> p r e", r=2)
            for e in range(1, E1):
                b_step(V.tensor_tensor(rows_to[:, :, e:e + 1], rows_to[:, :, e:e + 1], rows_to[:, :, e - 1:e], ALU.add))
            b_step(V.tensor_scalar(cnt_f[:, 3 * R:4 * R], cnt_f[:, R:2 * R], -1.0, float(CAP), ALU.mult, ALU.add))
            jump = cnt_f[:, 3 * R:4 * R].rearrange("p (r e) -> p r e", r=2)
            def make_table(r):
                ends_before, jumps = scratch[r]
                b_step(V.tensor_tensor(ends_before[:, :, :], cst[:, C_J:C_J + NJ].unsqueeze(2).to_broadcast([P, NJ, E1]),
                                       rows_to[:, r, :].unsqueeze(1).to_broadcast([P, NJ, E1]), ALU.is_ge))
                b_step(V.tensor_tensor(jumps[:, :, :], ends_before[:, :, :], jump[:, r, :].unsqueeze(1).to_broadcast([P, NJ, E1]), ALU.mult))
                firsts, experts = (tab_f[:, h * TILES + r * NJ:h * TILES + (r + 1) * NJ] for h in range(2))
                b_step(V.reduce_sum(firsts, jumps[:, :, :], axis=AX.X))
                b_step(V.reduce_sum(experts, ends_before[:, :, 0:E1 - 1], axis=AX.X))
                b_step(V.tensor_tensor(firsts, firsts, cst[:, C_J:C_J + NJ], ALU.add))
                for h, part in enumerate((firsts, experts)):
                    ins = V.tensor_copy(tab_i[:, h * TILES + r * NJ:h * TILES + (r + 1) * NJ], part)
                ins.then_inc(table_ready, 1)

            make_table(0)

            quarter = E1 * WC // 4
            for h in range(4):
                dve.wait_ge(mw_hi, h + 1)
                cols = slice(h * quarter, (h + 1) * quarter)
                V.tensor_tensor(w1l[:, cols], mstage[:, cols], w1h[:, cols].bitcast(fp32), ALU.subtract).then_inc(mw_ready, 1)

            for u in range(U):
                V.sem_inc(slot_used[u], 1)

            def rows_low(t, u):
                dve.wait_ge(gT_hi[u], t + 1)
                V.tensor_tensor(gTl[u][:, :], ps[2 * u][:, :], gTh[u][:, :].bitcast(fp32), ALU.subtract).then_inc(gT_lo[u], 1)

            def turn_c(t, more):
                experts = loaded(mybir.EngineType.DVE, tab_i, t * (U * UT) + TILES, U * UT, E1 - 1)
                for u in range(U):
                    dve.wait_ge(returned[u], t * (UT * 16) + UT * 16)
                    dve.wait_ge(y_ready[u], t + 1)
                    V.tensor_copy(isel[u][:, :, 0:1], g[u][:, :, D + E1:D + E1 + 1])
                    for i, e in enumerate(experts[u * UT:(u + 1) * UT]):
                        ins = V.tensor_copy(wsel[u][:, i, 0:1], g[u][:, i, bass.ds(e + D, 1)])
                    ins.then_inc(sel_ready[u], 1)
                    dve.wait_ge(sel_ready[u], t + 1)
                    V.sem_inc(slot_used[u], 1)
                for u in range(U):
                    dve.wait_ge(hT_hi[u], t + 1)
                    V.tensor_tensor(hTl[u][:, :], ps[2 * u][:, :], hTh[u][:, :].bitcast(fp32), ALU.subtract).then_inc(hT_lo[u], 1)
                for u in range(U) if more else ():
                    rows_low(t + 1, u)

            for u in range(U):
                rows_low(0, u)
            make_table(1)
            with dve.Fori(0, TURNS_C - 1) as j:
                turn_c(j, True)
            turn_c(TURNS_C - 1, False)

        @block.gpsimd
        def _(pool):
            G = nc.gpsimd
            for s in range(2):
                pool.dma_start(idx_credit[:, 2 * s:2 * s + 2], a["consts"][:, 0:2]).then_inc(scattered[s], 2 * T * 16)
            for u in range(U):
                pool.dma_start(idx_credit[:, 4 + 2 * u:6 + 2 * u], a["consts"][:, 0:2]).then_inc(returned[u], UT * 16)
            pool.wait_ge(dve_setup, 3)
            G.sem_inc(x3_stored, 16)

            def power(n, q, cols):
                per = 2 if q == "0" else 1
                pool.wait_ge(var_ready[q], val(n, per, per))
                G.tensor_tensor(rs[q][:, 0:cols], vp[q][:, 0:cols], minus_half[:, 0:cols], ALU.pow).then_inc(pow_ready[q], 1)
                pool.wait_ge(pow_ready[q], val(n, 1, 1))
                G.tensor_tensor(rs[q][:, 12:16], vp[q][:, 12:16], rs[q][:, 0:T], ALU.mult).then_inc(rstd_ready[q], 1)

            def residual(n, name, add, ready):
                for q in range(2):
                    job = f"{name}g{q}"
                    pool.wait_ge(bank_free[BANK[job]], val(n, USES[BANK[job]], USE[job] + 1))
                    half = lambda b: b[:, 2 * q:2 * q + 2, :].rearrange("p a b -> p (a b)")
                    G.tensor_tensor(half(x[slot(n)]), half(x[slot(n)]), half(add), ALU.add).then_inc(ready, 1)

            def send(n):
                pool.wait_ge(idx_ready, val(n, 1, 1))
                hold(pool)
                s = slot(n, 2)
                for t in range(T):
                    for i in range(2):
                        G.indirect_dma_start(out=routed[i], out_offset=bass.IndirectOffsetOnAxis(ap=idx[s][:, i, t:t + 1], axis=0),
                                             in_=pay[s][:, t, :], in_offset=None).then_inc(scattered[s], 16)

            def step(k):
                a, b, c, d, e, nxt = k, ago(k, 1), ago(k, 2), ago(k, 3), ago(k, 4), ago(k, -1)
                A, B, C_, D_ = active(a), active(b), active(c), active(d)
                if k[1] == 0 and k[2] == 0:
                    power(a, "0", 12)
                if C_:
                    power(c, "2", T)
                if D_:
                    pool.wait_ge(xn_ready["3"], val(d, 1, 1))
                    pool.wait_ge(x3_stored, val(d, 16, 16))
                    G.tensor_tensor(xo[:, :, :], x[slot(d)][:, :, :], pay[slot(d, 2)][:, :, 0:D], ALU.add).then_inc(x3_summed, 1)
                if active(e):
                    send(e)
                if A:
                    residual(a, "M0", xnA, x1_ready)
                if starts(k):
                    power(nxt, "0", 12)
                if A:
                    power(a, "1", T)
                if C_:
                    residual(c, "M1", xnY, x3_ready)
                    power(c, "3", T)

            over_steps(pool, step)
            pool.wait_ge(mask_ready, PAIRS)
            G.memset(b1r[:, :].bitcast(fp32), 0.0).then_inc(m_clear, 1)
            send((None, 0, PAIRS - 1))

            for r in range(2):
                if r == 1:
                    for u in range(U):
                        pool.wait_ge(returned[u], (TURNS_C // 2 + 1) * UT * 16)
                with pool.Fori(0, TURNS_C // 2) as j:
                    t = j + r * (TURNS_C // 2)
                    for u in range(U):
                        pool.wait_ge(y_ready[u], t + 2)
                        pool.wait_ge(sel_ready[u], t + 1)
                        hold(pool)
                        for i in range(UT):
                            G.indirect_dma_start(out=out, out_offset=bass.IndirectOffsetOnAxis(ap=isel[u][:, i, 0:1], axis=0),
                                                 in_=ysb[u][:, i, :], in_offset=None, bounds_check=TOK - 1, oob_is_err=False,
                                                 compute_op=ALU.add).then_inc(returned[u], 16)

        @block.tensor
        def _(pe):
            mm, turn = nc.tensor.matmul, nc.tensor.transpose
            ident = cst[:, C_ID:C_ID + P]

            def free(job, n):
                pe.wait_ge(bank_free[BANK[job]], val(n, USES[BANK[job]], USE[job]))

            def read_out(job, n):
                pe.wait_ge(bank_free[BANK[job]], val(n, USES[BANK[job]], USE[job] + 1))

            def filled(job, ins):
                ins.then_inc(bank_full[BANK[job]], 1)

            def mm3(o, left, right, start, stop):
                mm(o, left[0], right[0], start=start, stop=False)
                mm(o, left[0], right[1], start=False, stop=False)
                return mm(o, left[1], right[0], start=False, stop=stop)

            def W(name, lo, cols):
                return w0(0, name, lo, cols), w0(1, name, lo, cols)

            def transposes(n, name, src, blocks=range(KD)):
                for k in blocks:
                    job = f"{name}k{k}"
                    free(job, n)
                    for t in range(T):
                        ins = turn(ps[BANK[job]][:, t * P:(t + 1) * P], src[:, t, k * P:(k + 1) * P], ident)
                    filled(job, ins)

            def linear(n, name, xt, h, l, w, bias, graphs=range(2)):
                if 0 in graphs:
                    read_out(f"{xt}k1", n)
                for q in graphs:
                    job = f"{name}g{q}"
                    free(job, n)
                    for i in range(2):
                        t = 2 * q + i
                        o = ps[BANK[job]][:, i * D:(i + 1) * D]
                        mm(o, ones_r[:, 0:P], brow[:, B0[bias]:B0[bias] + D], start=True, stop=False)
                        for k in range(KD):
                            cols = slice(t * P, (t + 1) * P)
                            ins = mm3(o, (h[:, k, cols], l[:, k, cols]), W(w, k * D, D), False, k == KD - 1)
                    filled(job, ins)

            def conv(n, s, name, h, l, loops, graphs=range(2)):
                for q in graphs:
                    job = f"{name}g{q}"
                    free(job, n)
                    for i in range(2):
                        o = ps[BANK[job]][:, i * D:(i + 1) * D]
                        for jb in range(2):
                            cols = slice(i * P, (i + 1) * P)
                            ins = mm3(o, (ATh[s][:, q, jb, cols], ATl[s][:, q, jb, cols]), (h[:, 2 * q + jb, :], l[:, 2 * q + jb, :]),
                                      jb == 0, jb == 1 and not loops)
                        if loops:
                            mm(o, id_r[:, :], h[:, 2 * q + i, :], start=False, stop=False)
                            ins = mm(o, id_r[:, :], l[:, 2 * q + i, :], start=False, stop=True)
                    filled(job, ins)

            def dense(n, job, weights, rights, bias):
                free(job, n)
                o = ps[BANK[job]][:, :]
                if bias is not None:
                    mm(o, brow[:, bias:bias + P], ones_r[:, :], start=True, stop=False)
                for k, (w, x_) in enumerate(zip(weights, rights)):
                    ins = mm3(o, w, x_, bias is None and k == 0, k == len(weights) - 1)
                filled(job, ins)

            def experts_in(n, i):
                e_blocks = [W("eW1", i * D + k * EH1, EH1) for k in range(KD)]
                dense(n, f"E1e{i}", e_blocks, [(xThB[:, k, :], xTlB[:, k, :]) for k in range(KD)], B0["eb1"] + i * EH1)

            def experts_mid(n, i):
                for e in range(2):
                    read_out(f"E1e{2 * i + e}", n)
                dense(n, f"EP{i}", [W("eW2", (2 * i + e) * P, P) for e in range(2)], [H[(2 * (i + 1) + e) % 4] for e in range(2)], None)

            H = [(hh[:, m, :], hl[:, m, :]) for m in range(4)]

            def lead_rows(n):
                pe.wait_ge(xn_ready["0"], val(n, 1, 1))
                transposes(n, "xT0", xnA)

            def lead_adj(n):
                pe.wait_ge(adj_loaded[slot(n, 2)], adj_value(n))
                for q in range(2):
                    job = f"ATg{q}"
                    free(job, n)
                    for jb in range(2):
                        for i in range(2):
                            ins = turn(ps[BANK[job]][:, jb * N + i * P:jb * N + (i + 1) * P], adj[slot(n, 2)][:, 2 * q + i, jb * P:(jb + 1) * P], ident)
                    filled(job, ins)

            def step(k):
                a, b, c, d, nxt = k, ago(k, 1), ago(k, 2), ago(k, 3), ago(k, -1)
                A, B, C_, D_ = active(a), active(b), active(c), active(d)
                if k[1] == 0 and k[2] == 0:
                    lead_rows(a)
                    lead_adj(a)
                if A:
                    linear(a, "T0", "xT0", xThA, xTlA, "g0", "g0", (0,))
                if B:
                    pe.wait_ge(xn_ready["1"], val(b, 1, 1))
                    transposes(b, "xT1", xnB)
                if D_:
                    pe.wait_ge(xn_ready["3"], val(d, 1, 1))
                    transposes(d, "xT3", pay[slot(d, 2)], (0,))
                if A:
                    linear(a, "T0", "xT0", xThA, xTlA, "g0", "g0", (1,))
                if D_:
                    transposes(d, "xT3", pay[slot(d, 2)], (1,))
                if B:
                    for i in range(KD):
                        read_out(f"xT1k{i}", b)
                    job = "GL"
                    free(job, b)
                    for t in range(T):
                        for i in range(KD):
                            cols = slice(t * P, (t + 1) * P)
                            ins = mm3(ps[BANK[job]][:, t * E0:(t + 1) * E0], (xThB[:, i, cols], xTlB[:, i, cols]), W("gW", i * E0, E0), i == 0, i == KD - 1)
                    filled(job, ins)
                    xT = [(xThB[:, i, :], xTlB[:, i, :]) for i in range(KD)]
                    for m in range(2):
                        dense(b, f"S1m{m}", [W("sW1", i * D + m * P, P) for i in range(KD)], xT, B0["sb1"] + m * P)
                if D_:
                    job = "RL"
                    free(job, d)
                    for t in range(T):
                        for i in range(KD):
                            ins = mm(ps[BANK[job]][:, t * E1:(t + 1) * E1], xT3[:, i, t * P:(t + 1) * P], rW[:, i, :], start=(i == 0), stop=(i == KD - 1))
                    filled(job, ins)
                if A:
                    conv(a, slot(a), "M0", ThA, TlA, False)
                if C_:
                    pe.wait_ge(xn_ready["2"], val(c, 1, 1))
                    transposes(c, "xT2", xnY)
                if B:
                    experts_in(b, 0)
                    experts_in(b, 1)
                    dense(b, "S2", [W("sW2", i * P, P) for i in range(KD)], H[0:2], B0["sb2"])
                if C_:
                    linear(c, "T1", "xT2", xThY, xTlY, "g1", "g1")
                if B:
                    experts_in(b, 2)
                    experts_mid(b, 0)
                    experts_in(b, 3)
                if D_:
                    job = "POS"
                    pe.wait_ge(mask_ready, val(d, 1, 1))
                    free(job, d)
                    for t in range(T):
                        o = ps[BANK[job]][:, t * R:(t + 1) * R]
                        for u in range(t):
                            mm(o, ones_b[:, :], mb[:, u, :], start=(u == 0), stop=False)
                        mm(o, tri_b[:, :], mb[:, t, :], start=(t == 0), stop=True)
                    for t in range(T):
                        ins = mm(ps[BANK[job]][:, T * R:(T + 1) * R], ones_b[:, :], mb[:, t, :], start=(t == 0), stop=(t == T - 1))
                    filled(job, ins)
                if C_:
                    conv(c, slot(c), "M1", ThY, TlY, True, (0,))
                if B:
                    job = "CBT"
                    pe.wait_ge(cb_ready, val(b, 1, 1))
                    free(job, b)
                    for t in range(T):
                        ins = turn(ps[BANK[job]][0:16, t * P:(t + 1) * P], cb[:, t, :].bitcast(fp32), ident)
                    filled(job, ins)
                if C_:
                    conv(c, slot(c), "M1", ThY, TlY, True, (1,))
                if B:
                    experts_mid(b, 1)
                    read_out("CBT", b)
                    for i in range(2):
                        job = f"G{i}"
                        free(job, b)
                        filled(job, mm(ps[BANK[job]][:, :], sel_r[:, i * P:(i + 1) * P], cbT[:, :], start=True, stop=True))
                if starts(k):
                    lead_rows(nxt)
                    if not B:
                        lead_adj(nxt)
                if B:
                    for i in range(2):
                        if i == 1 and starts(k):
                            lead_adj(nxt)
                        parts = [(q, ps[BANK[f"O1g{q}"]][:, i * D:(i + 1) * D], slice((2 * q + i) * P, (2 * q + i + 1) * P)) for q in range(2)]
                        for q, o, cols in parts:
                            if i == 0:
                                free(f"O1g{q}", b)
                            mm(o, cbT[:, cols], o_bias[:, :], start=True, stop=False)
                            mm3(o, (s2h[:, cols], s2l[:, cols]), W("sW3", 0, D), False, False)
                        for e in range(2):
                            if i == 0:
                                pe.wait_ge(gl_ready, val(b, 2, e + 1))
                            for q, o, cols in parts:
                                ins = mm3(o, (gh[:, e, cols], gl[:, e, cols]), W("eW3", e * D, D), False, e == 1)
                                if e == 1 and i == 1:
                                    filled(f"O1g{q}", ins)

            pe.wait_ge(misc, 16)
            pe.wait_ge(mask_loaded, 16)
            turn(ps[0][:, 0:P], mask_rows[:, :], ident).then_inc(mask_turned, 1)
            pe.wait_ge(w_ready, 6)

            over_steps(pe, step)

            pe.wait_ge(table_ready, 1)
            def turned(u, src):
                for i in range(UT):
                    for k in range(KD):
                        c0 = (i * KD + k) * P
                        ins = turn(ps[2 * u][:, c0:c0 + P], src(i, k), ident)
                ins.then_inc(pe_c[u], 1)

            def rows_turned(t, u):
                pe.wait_ge(g_loaded[u], t * (UT * 16) + UT * 16)
                turned(u, lambda i, k: g[u][:, i, k * P:(k + 1) * P])

            def product(u, w, h, l, experts):
                for i in range(UT):
                    e = experts[u * UT + i]
                    o = ps[2 * u + 1][:, i * D:(i + 1) * D]
                    mm(o, ones_r[:, 0:P], b1r[:, bass.ds(e * D + w * E1 * D, D)], start=True, stop=False)
                    for k in range(KD):
                        cols = slice((i * KD + k) * P, (i * KD + k + 1) * P)
                        c = bass.ds(e * WC + (w * KD + k) * D, D)
                        ins = mm3(o, (h[u][:, cols], l[u][:, cols]), (w1h[:, c], w1l[:, c]), False, k == KD - 1)
                ins.then_inc(pe_c[u], 1)

            def turn_c(t, more):
                experts = loaded(mybir.EngineType.PE, tab_i, t * (U * UT) + TILES, U * UT, E1 - 1)

                def first_product(u):
                    pe.wait_ge(gT_lo[u], t + 1)
                    pe.wait_ge(y_ready[u], t + 1)
                    product(u, 0, gTh, gTl, experts)

                def hidden_turned(u):
                    pe.wait_ge(hf_ready[u], t + 1)
                    turned(u, lambda i, k: hf[u][:, (i * KD + k) * P:(i * KD + k + 1) * P])

                for u in range(U - 1):
                    first_product(u)
                hidden_turned(0)
                first_product(U - 1)
                for u in range(1, U):
                    hidden_turned(u)
                for pair in ((0, 1), (2, 3)):
                    for u in pair:
                        pe.wait_ge(hT_lo[u], t + 1)
                        product(u, 1, hTh, hTl, experts)
                    for u in pair if more else ():
                        rows_turned(t + 1, u)

            pe.wait_ge(mw_ready, 4)
            pe.wait_ge(m_loaded, 2 * 16)
            for u in range(U):
                rows_turned(0, u)
            with pe.Fori(0, TURNS_C // 2 - 1) as j:
                turn_c(j * 2, True)
                turn_c(j * 2 + 1, True)
            turn_c(TURNS_C - 2, True)
            turn_c(TURNS_C - 1, False)


def kernel(x, adj, nodemask, L0_gnn_W, L0_gnn_b, L0_ffn_sW1, L0_ffn_sb1, L0_ffn_sW2, L0_ffn_sb2, L0_ffn_sW3, L0_ffn_sb3,
           L0_ffn_eW1, L0_ffn_eb1, L0_ffn_eW2, L0_ffn_eb2, L0_ffn_eW3, L0_ffn_eb3, L0_ffn_gW, L0_ffn_gb, L1_gnn_W, L1_gnn_b,
           L1_ffn_router_w, L1_ffn_w1, L1_ffn_b1, L1_ffn_w2, L1_ffn_b2):
    import concourse.bacc as bacc
    from concourse.bass_utils import run_bass_kernel_spmd

    lay = lambda v: np.ascontiguousarray(np.asarray(v))
    arrays = {
        "x": lay(x).reshape(TOK, D), "adj": lay(adj).reshape(TOK, N), "nodemask": lay(nodemask).reshape(P, P),
        "g0W": lay(np.asarray(L0_gnn_W).T), "g0b": lay(L0_gnn_b), "g1W": lay(np.asarray(L1_gnn_W).T), "g1b": lay(L1_gnn_b),
        "sW1": lay(L0_ffn_sW1), "sb1": lay(L0_ffn_sb1), "sW2": lay(L0_ffn_sW2), "sb2": lay(L0_ffn_sb2),
        "sW3": lay(L0_ffn_sW3), "sb3": lay(L0_ffn_sb3), "eW1": lay(L0_ffn_eW1), "eb1": lay(L0_ffn_eb1),
        "eW2": lay(L0_ffn_eW2), "eb2": lay(L0_ffn_eb2), "eW3": lay(L0_ffn_eW3), "eb3": lay(L0_ffn_eb3),
        "gW": lay(L0_ffn_gW), "gb": lay(L0_ffn_gb), "rW": lay(np.asarray(L1_ffn_router_w).T),
        "w1": lay(L1_ffn_w1), "b1": lay(L1_ffn_b1), "w2": lay(L1_ffn_w2), "b2": lay(L1_ffn_b2),
        "consts": constants(),
    }
    nc = bacc.Bacc("TRN2", target_bir_lowering=False, num_devices=1)
    a = {n: nc.dram_tensor("in_" + n, v.shape, mybir.dt.from_np(v.dtype), kind="ExternalInput").ap() for n, v in arrays.items()}
    out = nc.dram_tensor("out", (TOK, D), fp32, kind="ExternalOutput").ap()
    build(nc, a, out)
    res = run_bass_kernel_spmd(nc, [{"in_" + n: v for n, v in arrays.items()}], core_ids=[0])
    return res.results[0]["out"].reshape(GRAPHS, N, D)
```
